# Optimizing a Trainium2 kernel written in Bass

```python
import numpy as np
import jax
import jax.numpy as jnp

def _softmax(x, axis=-1):
    return jax.nn.softmax(x, axis=axis)

def _gelu(x):
    return jax.nn.gelu(x, approximate=True)

def _silu(x):
    return jax.nn.silu(x)

def _sigmoid(x):
    return jax.nn.sigmoid(x)

def _layernorm(x, axis=-1, eps=1e-05):
    m = jnp.mean(x, axis=axis, keepdims=True)
    v = jnp.var(x, axis=axis, keepdims=True)
    return (x - m) / jnp.sqrt(v + eps)

def _scatter_add(tgt, idx, src, axis=0):
    return tgt.at[idx].add(src)

def _segment_sum(src, seg, n):
    return jax.ops.segment_sum(src, seg, n)
kernel_name = 'mk_adaln_d2_jaxref_r8_ae8805'

def setup_inputs(seed: int=0):
    np.random.seed(seed)
    _w = jnp.asarray

    def _L0_attn_setup():
        import jax, jax.numpy as jnp
        import numpy as np
        import math
        D_MODEL = 256
        N_HEADS = 16
        N_KV_HEADS = 4
        MAX_SEQ_LEN = 256
        ROPE_THETA = 10000.0
        DK = D_MODEL // N_HEADS
        B, T = (2, 256)

        def rope_tables(T, dk, theta, dtype=jnp.float32):
            pairs = jnp.arange(dk // 2, dtype=dtype)
            freqs = 1.0 / theta ** (2.0 * pairs / dk)
            pos = jnp.arange(T, dtype=dtype)
            angles = pos[:, None] * freqs[None, :]
            return (jnp.cos(angles), jnp.sin(angles))

        def apply_rope(t, cos, sin):
            te = t[..., 0::2]
            to = t[..., 1::2]
            oe = te * cos - to * sin
            oo = te * sin + to * cos
            return jnp.stack([oe, oo], axis=-1).reshape(t.shape)
        key = jax.random.key(seed)
        k1, k2, k3, k4 = jax.random.split(key, 4)
        s = 1.0 / math.sqrt(D_MODEL)
        x = jax.random.normal(k1, (B, T, D_MODEL), dtype=jnp.float32)
        q_w = jax.random.normal(k2, (D_MODEL, D_MODEL), dtype=jnp.float32) * s
        kv_w = jax.random.normal(k3, (2 * N_KV_HEADS * DK, D_MODEL), dtype=jnp.float32) * s
        c_w = jax.random.normal(k4, (D_MODEL, D_MODEL), dtype=jnp.float32) * s
        return {'x': x, 'q_w': q_w, 'kv_w': kv_w, 'c_w': c_w}
    _L0_attn_in = _L0_attn_setup()

    def _L0_ffn_setup():
        import jax, jax.numpy as jnp
        import numpy as np
        E = 8
        TOP_K = 2
        H = 256
        I_MOE = 176
        I_SH = 704
        B, S = (2, 256)

        def _moe_forward(hidden_states, router_weight, gate_up_proj, down_proj, sh_gate_w, sh_up_w, sh_down_w, shared_gate_w):
            b, s, h = hidden_states.shape
            x = hidden_states.reshape(-1, h)
            shared = jnp.einsum('ti,hi->th', jax.nn.silu(x @ sh_gate_w.T) * (x @ sh_up_w.T), sh_down_w)
            logits = x @ router_weight.T
            probs = jax.nn.softmax(logits.astype(jnp.float32), axis=-1)
            top_v, top_i = jax.lax.top_k(probs, TOP_K)
            top_v = top_v / top_v.sum(axis=-1, keepdims=True)
            combine = (jax.nn.one_hot(top_i, E, dtype=top_v.dtype) * top_v[..., None]).sum(axis=1)
            out = jnp.zeros_like(x)
            for e in range(E):
                gu = x @ gate_up_proj[e].T
                gate, up = (gu[:, :I_MOE], gu[:, I_MOE:])
                cur = jax.nn.silu(gate) * up @ down_proj[e].T
                out = out + cur * combine[:, e:e + 1]
            out = out + jax.nn.sigmoid(x @ shared_gate_w.T) * shared
            return out.reshape(b, s, h)
        key = jax.random.key(seed)
        ks = jax.random.split(key, 8)
        scale = 0.02
        return {'hidden_states': jax.random.normal(ks[0], (B, S, H), dtype=jnp.float32), 'router_weight': jax.random.normal(ks[1], (E, H), dtype=jnp.float32) * scale, 'gate_up_proj': jax.random.normal(ks[2], (E, 2 * I_MOE, H), dtype=jnp.float32) * scale, 'down_proj': jax.random.normal(ks[3], (E, H, I_MOE), dtype=jnp.float32) * scale, 'sh_gate_w': jax.random.normal(ks[4], (I_SH, H), dtype=jnp.float32) * scale, 'sh_up_w': jax.random.normal(ks[5], (I_SH, H), dtype=jnp.float32) * scale, 'sh_down_w': jax.random.normal(ks[6], (H, I_SH), dtype=jnp.float32) * scale, 'shared_gate_w': jax.random.normal(ks[7], (1, H), dtype=jnp.float32) * scale}
    _L0_ffn_in = _L0_ffn_setup()
    _L0_c = _w((lambda *s: np.random.randn(*s).astype(np.float32) * 0.05)(4, 256))
    _L0_wmod = _w((lambda *s: np.random.randn(*s).astype(np.float32) * 0.05)(256, 6 * 256) * 256 ** (-0.5))

    def _L1_attn_setup():
        import jax, jax.numpy as jnp
        import numpy as np
        NUM_HEADS = 16
        ROPE_BASE = 10000.0

        def _rope_tables(seq_len, head_dim, scaling_factor=1.0):
            inv_freq = 1.0 / ROPE_BASE ** (jnp.arange(0, head_dim, 2, dtype=jnp.float32) / head_dim)
            t = jnp.arange(seq_len, dtype=jnp.float32) * scaling_factor
            freqs = jnp.einsum('i,j->ij', t, inv_freq)
            c = jnp.sin(freqs)
            s = jnp.cos(freqs)
            return (c, s)

        def _apply_rope(x, c, s):
            x1, x2 = jnp.split(x, 2, axis=-1)
            c = c[None, None]
            s = s[None, None]
            return jnp.concatenate([x1 * c - x2 * s, x1 * s + x2 * c], axis=-1)
        key = jax.random.key(seed)
        ks = jax.random.split(key, 5)
        B, S, H = (4, 256, 256)
        x = jax.random.normal(ks[0], (B, S, H), dtype=jnp.float32)
        scale = 1.0 / np.sqrt(H)
        Wq = jax.random.normal(ks[1], (H, H), dtype=jnp.float32) * scale
        Wk = jax.random.normal(ks[2], (H, H), dtype=jnp.float32) * scale
        Wv = jax.random.normal(ks[3], (H, H), dtype=jnp.float32) * scale
        Wo = jax.random.normal(ks[4], (H, H), dtype=jnp.float32) * scale
        return {'x': x, 'Wq': Wq, 'Wk': Wk, 'Wv': Wv, 'Wo': Wo}
    _L1_attn_in = _L1_attn_setup()

    def _L1_ffn_setup():
        import jax, jax.numpy as jnp
        import numpy as np
        B, S, H, I, E, K, R = (4, 128, 256, 896, 8, 2, 64)
        SCALING = 16.0 / 64.0
        key = jax.random.key(seed)
        ks = jax.random.split(key, 14)
        rn = lambda k, shape, sc: jax.random.normal(k, shape, jnp.float32) * sc
        x = rn(ks[0], (B, S, H), 1.0)
        expert_wealth = jnp.full((E,), 100.0, jnp.float32)
        conf_W = rn(ks[1], (E, H), 0.02)
        conf_b = ((jnp.arange(E) - E / 2.0) * 0.1).astype(jnp.float32)
        base_gate = rn(ks[2], (H, I), H ** (-0.5))
        base_up = rn(ks[3], (H, I), H ** (-0.5))
        base_down = rn(ks[4], (I, H), I ** (-0.5))
        gate_A = rn(ks[5], (E, H, R), H ** (-0.5))
        gate_B = rn(ks[6], (E, R, I), 0.01)
        up_A = rn(ks[7], (E, H, R), H ** (-0.5))
        up_B = rn(ks[8], (E, R, I), 0.01)
        down_A = rn(ks[9], (E, I, R), I ** (-0.5))
        down_B = rn(ks[10], (E, R, H), 0.01)
        return {'hidden_states': x, 'expert_wealth': expert_wealth, 'conf_W': conf_W, 'conf_b': conf_b, 'base_gate': base_gate, 'base_up': base_up, 'base_down': base_down, 'gate_A': gate_A, 'gate_B': gate_B, 'up_A': up_A, 'up_B': up_B, 'down_A': down_A, 'down_B': down_B}
    _L1_ffn_in = _L1_ffn_setup()
    _L1_c = _w((lambda *s: np.random.randn(*s).astype(np.float32) * 0.05)(4, 256))
    _L1_wmod = _w((lambda *s: np.random.randn(*s).astype(np.float32) * 0.05)(256, 6 * 256) * 256 ** (-0.5))
    _d = {'L0_attn_x': _L0_attn_in['x'], 'L0_attn_q_w': _L0_attn_in['q_w'], 'L0_attn_kv_w': _L0_attn_in['kv_w'], 'L0_attn_c_w': _L0_attn_in['c_w'], 'L0_ffn_router_weight': _L0_ffn_in['router_weight'], 'L0_ffn_gate_up_proj': _L0_ffn_in['gate_up_proj'], 'L0_ffn_down_proj': _L0_ffn_in['down_proj'], 'L0_ffn_sh_gate_w': _L0_ffn_in['sh_gate_w'], 'L0_ffn_sh_up_w': _L0_ffn_in['sh_up_w'], 'L0_ffn_sh_down_w': _L0_ffn_in['sh_down_w'], 'L0_ffn_shared_gate_w': _L0_ffn_in['shared_gate_w'], 'L0_c': _L0_c, 'L0_wmod': _L0_wmod, 'L1_attn_Wq': _L1_attn_in['Wq'], 'L1_attn_Wk': _L1_attn_in['Wk'], 'L1_attn_Wv': _L1_attn_in['Wv'], 'L1_attn_Wo': _L1_attn_in['Wo'], 'L1_ffn_expert_wealth': _L1_ffn_in['expert_wealth'], 'L1_ffn_conf_W': _L1_ffn_in['conf_W'], 'L1_ffn_conf_b': _L1_ffn_in['conf_b'], 'L1_ffn_base_gate': _L1_ffn_in['base_gate'], 'L1_ffn_base_up': _L1_ffn_in['base_up'], 'L1_ffn_base_down': _L1_ffn_in['base_down'], 'L1_ffn_gate_A': _L1_ffn_in['gate_A'], 'L1_ffn_gate_B': _L1_ffn_in['gate_B'], 'L1_ffn_up_A': _L1_ffn_in['up_A'], 'L1_ffn_up_B': _L1_ffn_in['up_B'], 'L1_ffn_down_A': _L1_ffn_in['down_A'], 'L1_ffn_down_B': _L1_ffn_in['down_B'], 'L1_c': _L1_c, 'L1_wmod': _L1_wmod}
    _x0 = _d['L0_attn_x']
    _d['L0_attn_x'] = jax.random.normal(jax.random.fold_in(jax.random.key(seed), 1), (4, 256, 256), dtype=_x0.dtype)
    del _x0
    return _d

def reference(L0_attn_x, L0_attn_q_w, L0_attn_kv_w, L0_attn_c_w, L0_ffn_router_weight, L0_ffn_gate_up_proj, L0_ffn_down_proj, L0_ffn_sh_gate_w, L0_ffn_sh_up_w, L0_ffn_sh_down_w, L0_ffn_shared_gate_w, L0_c, L0_wmod, L1_attn_Wq, L1_attn_Wk, L1_attn_Wv, L1_attn_Wo, L1_ffn_expert_wealth, L1_ffn_conf_W, L1_ffn_conf_b, L1_ffn_base_gate, L1_ffn_base_up, L1_ffn_base_down, L1_ffn_gate_A, L1_ffn_gate_B, L1_ffn_up_A, L1_ffn_up_B, L1_ffn_down_A, L1_ffn_down_B, L1_c, L1_wmod):

    def _L0_attn_ref(x, q_w, kv_w, c_w):
        import jax, jax.numpy as jnp
        import numpy as np
        import math
        D_MODEL = 256
        N_HEADS = 16
        N_KV_HEADS = 4
        MAX_SEQ_LEN = 256
        ROPE_THETA = 10000.0
        DK = D_MODEL // N_HEADS
        B, T = (2, 256)

        def rope_tables(T, dk, theta, dtype=jnp.float32):
            pairs = jnp.arange(dk // 2, dtype=dtype)
            freqs = 1.0 / theta ** (2.0 * pairs / dk)
            pos = jnp.arange(T, dtype=dtype)
            angles = pos[:, None] * freqs[None, :]
            return (jnp.cos(angles), jnp.sin(angles))

        def apply_rope(t, cos, sin):
            te = t[..., 0::2]
            to = t[..., 1::2]
            oe = te * cos - to * sin
            oo = te * sin + to * cos
            return jnp.stack([oe, oo], axis=-1).reshape(t.shape)
        Bx, Tx, _ = x.shape
        H, HKV, dk = (N_HEADS, N_KV_HEADS, DK)
        rep = H // HKV
        q = x @ q_w.T
        kv = x @ kv_w.T
        k, v = jnp.split(kv, 2, axis=-1)
        q = q.reshape(Bx, Tx, H, dk).transpose(0, 2, 1, 3)
        k = k.reshape(Bx, Tx, HKV, dk).transpose(0, 2, 1, 3)
        v = v.reshape(Bx, Tx, HKV, dk).transpose(0, 2, 1, 3)
        cos, sin = rope_tables(Tx, dk, ROPE_THETA, x.dtype)
        q = apply_rope(q, cos, sin)
        k = apply_rope(k, cos, sin)
        k_ctx = jnp.repeat(k, rep, axis=1)
        v_ctx = jnp.repeat(v, rep, axis=1)
        logits = jnp.einsum('bhqd,bhkd->bhqk', q, k_ctx) / math.sqrt(dk)
        row = jnp.arange(Tx)
        mask = jnp.where(row[None, :] > row[:, None], -jnp.inf, 0.0).astype(x.dtype)
        logits = logits + mask[None, None]
        probs = jax.nn.softmax(logits, axis=-1)
        out = jnp.einsum('bhqk,bhkd->bhqd', probs, v_ctx)
        out = out.transpose(0, 2, 1, 3).reshape(Bx, Tx, D_MODEL)
        return out @ c_w.T

    def _L0_ffn_ref(hidden_states, router_weight, gate_up_proj, down_proj, sh_gate_w, sh_up_w, sh_down_w, shared_gate_w):
        import jax, jax.numpy as jnp
        import numpy as np
        E = 8
        TOP_K = 2
        H = 256
        I_MOE = 176
        I_SH = 704
        B, S = (2, 256)

        def _moe_forward(hidden_states, router_weight, gate_up_proj, down_proj, sh_gate_w, sh_up_w, sh_down_w, shared_gate_w):
            b, s, h = hidden_states.shape
            x = hidden_states.reshape(-1, h)
            shared = jnp.einsum('ti,hi->th', jax.nn.silu(x @ sh_gate_w.T) * (x @ sh_up_w.T), sh_down_w)
            logits = x @ router_weight.T
            probs = jax.nn.softmax(logits.astype(jnp.float32), axis=-1)
            top_v, top_i = jax.lax.top_k(probs, TOP_K)
            top_v = top_v / top_v.sum(axis=-1, keepdims=True)
            combine = (jax.nn.one_hot(top_i, E, dtype=top_v.dtype) * top_v[..., None]).sum(axis=1)
            out = jnp.zeros_like(x)
            for e in range(E):
                gu = x @ gate_up_proj[e].T
                gate, up = (gu[:, :I_MOE], gu[:, I_MOE:])
                cur = jax.nn.silu(gate) * up @ down_proj[e].T
                out = out + cur * combine[:, e:e + 1]
            out = out + jax.nn.sigmoid(x @ shared_gate_w.T) * shared
            return out.reshape(b, s, h)
        return _moe_forward(hidden_states, router_weight, gate_up_proj, down_proj, sh_gate_w, sh_up_w, sh_down_w, shared_gate_w)

    def _L1_attn_ref(x, Wq, Wk, Wv, Wo):
        import jax, jax.numpy as jnp
        import numpy as np
        NUM_HEADS = 16
        ROPE_BASE = 10000.0

        def _rope_tables(seq_len, head_dim, scaling_factor=1.0):
            inv_freq = 1.0 / ROPE_BASE ** (jnp.arange(0, head_dim, 2, dtype=jnp.float32) / head_dim)
            t = jnp.arange(seq_len, dtype=jnp.float32) * scaling_factor
            freqs = jnp.einsum('i,j->ij', t, inv_freq)
            c = jnp.sin(freqs)
            s = jnp.cos(freqs)
            return (c, s)

        def _apply_rope(x, c, s):
            x1, x2 = jnp.split(x, 2, axis=-1)
            c = c[None, None]
            s = s[None, None]
            return jnp.concatenate([x1 * c - x2 * s, x1 * s + x2 * c], axis=-1)
        B, S, H = x.shape
        nh = NUM_HEADS
        hd = H // nh
        scale = hd ** (-0.5)

        def proj(W):
            y = jnp.einsum('bsi,oi->bso', x, W)
            return y.reshape(B, S, nh, hd).transpose(0, 2, 1, 3)
        Q = proj(Wq)
        K = proj(Wk)
        V = proj(Wv)
        c, s = _rope_tables(S, hd)
        Q = _apply_rope(Q, c, s)
        K = _apply_rope(K, c, s)
        scores = jnp.einsum('bhqd,bhkd->bhqk', Q, K) * scale
        mask = jnp.tril(jnp.ones((S, S), dtype=bool))
        scores = jnp.where(mask[None, None], scores, -jnp.inf)
        attn = jax.nn.softmax(scores, axis=-1)
        out = jnp.einsum('bhqk,bhkd->bhqd', attn, V)
        out = out.transpose(0, 2, 1, 3).reshape(B, S, H)
        return jnp.einsum('bsi,oi->bso', out, Wo)

    def _L1_ffn_ref(hidden_states, expert_wealth, conf_W, conf_b, base_gate, base_up, base_down, gate_A, gate_B, up_A, up_B, down_A, down_B):
        import jax, jax.numpy as jnp
        import numpy as np
        B, S, H, I, E, K, R = (4, 128, 256, 896, 8, 2, 64)
        SCALING = 16.0 / 64.0
        x = hidden_states
        conf = jax.nn.sigmoid(jnp.einsum('bsh,eh->bse', x, conf_W) + conf_b)
        bids = conf * expert_wealth
        top_bids, sel = jax.lax.top_k(bids, K)
        routing = jax.nn.softmax(top_bids, axis=-1)
        base_g = jnp.einsum('bsh,hi->bsi', x, base_gate)
        base_u = jnp.einsum('bsh,hi->bsi', x, base_up)
        out = jnp.zeros_like(x)
        for e in range(E):
            g = base_g + x @ gate_A[e] @ gate_B[e] * SCALING
            u = base_u + x @ up_A[e] @ up_B[e] * SCALING
            h = jax.nn.silu(g) * u
            oe = h @ base_down + h @ down_A[e] @ down_B[e] * SCALING
            we = jnp.sum(routing * (sel == e), axis=-1)
            out = out + we[..., None] * oe
        return out
    x = L0_attn_x
    mod = (_silu(L0_c) @ L0_wmod).reshape(L0_c.shape[0], 6, 1, -1)
    sa, ca, ga, sb, cb, gb = (mod[:, 0], mod[:, 1], mod[:, 2], mod[:, 3], mod[:, 4], mod[:, 5])
    ga = (2 * (ga >= 0) - 1) * jnp.maximum(jnp.abs(ga), 0.25)
    gb = (2 * (gb >= 0) - 1) * jnp.maximum(jnp.abs(gb), 0.25)
    h = _layernorm(x, axis=-1) * (1 + ca) + sa
    x = x + ga * _L0_attn_ref(h, L0_attn_q_w, L0_attn_kv_w, L0_attn_c_w)
    h = _layernorm(x, axis=-1) * (1 + cb) + sb
    x = x + gb * _L0_ffn_ref(h, L0_ffn_router_weight, L0_ffn_gate_up_proj, L0_ffn_down_proj, L0_ffn_sh_gate_w, L0_ffn_sh_up_w, L0_ffn_sh_down_w, L0_ffn_shared_gate_w)
    mod = (_silu(L1_c) @ L1_wmod).reshape(L1_c.shape[0], 6, 1, -1)
    sa, ca, ga, sb, cb, gb = (mod[:, 0], mod[:, 1], mod[:, 2], mod[:, 3], mod[:, 4], mod[:, 5])
    ga = (2 * (ga >= 0) - 1) * jnp.maximum(jnp.abs(ga), 0.25)
    gb = (2 * (gb >= 0) - 1) * jnp.maximum(jnp.abs(gb), 0.25)
    h = _layernorm(x, axis=-1) * (1 + ca) + sa
    x = x + ga * _L1_attn_ref(h, L1_attn_Wq, L1_attn_Wk, L1_attn_Wv, L1_attn_Wo)
    h = _layernorm(x, axis=-1) * (1 + cb) + sb
    x = x + gb * _L1_ffn_ref(h, L1_ffn_expert_wealth, L1_ffn_conf_W, L1_ffn_conf_b, L1_ffn_base_gate, L1_ffn_base_up, L1_ffn_base_down, L1_ffn_gate_A, L1_ffn_gate_B, L1_ffn_up_A, L1_ffn_up_B, L1_ffn_down_A, L1_ffn_down_B)
    return x

_drawn_inputs = setup_inputs


def setup_inputs(seed=0):
    import zlib

    import numpy as np

    out = dict(_drawn_inputs(seed))
    spreads = {'L1_ffn_expert_wealth': (100.0, 0.6)}
    factors = {'L0_ffn_router_weight': 8.0,
     'L0_ffn_gate_up_proj': 8.0,
     'L0_ffn_down_proj': 8.0,
     'L0_ffn_sh_gate_w': 8.0,
     'L0_ffn_sh_up_w': 8.0,
     'L0_ffn_sh_down_w': 8.0,
     'L0_ffn_shared_gate_w': 8.0,
     'L1_ffn_conf_W': 8.0,
     'L1_ffn_conf_b': 8.0,
     'L1_ffn_gate_A': 8.0,
     'L1_ffn_gate_B': 8.0,
     'L1_ffn_up_A': 8.0,
     'L1_ffn_up_B': 8.0,
     'L1_ffn_down_A': 8.0,
     'L1_ffn_down_B': 8.0,
     'L1_attn_Wq': 4.103,
     'L1_attn_Wk': 4.203,
     'L1_attn_Wv': 2.71,
     'L1_attn_Wo': 2.868}
    for name, (base, spread) in spreads.items():
        noise = np.random.default_rng([zlib.crc32(name.encode()), seed]).standard_normal(out[name].shape)
        drawn = base * np.exp(spread * noise) if base else spread * noise
        out[name] = jnp.asarray(drawn.astype(out[name].dtype))
    for name, factor in factors.items():
        out[name] = (out[name] * factor).astype(out[name].dtype)
    return out
```

```python
from contextlib import ExitStack

import numpy as np

import concourse.bass as bass
from concourse import mybir

F32, BF16, U32 = mybir.dt.float32, mybir.dt.bfloat16, mybir.dt.uint32
ACT = mybir.ActivationFunctionType
ALU = mybir.AluOpType
AX = mybir.AxisListType.X

P = 128
B, S, D = 4, 256, 256
TB = S // P
DC = D // P
NH, HD = 16, 16
NKV = [4, 16]
QK = [(NH + n) * HD for n in NKV]
QKV = [(NH + 2 * n) * HD for n in NKV]
NPART = 6
E = 8
I0, ISH = 176, 704
H0 = E * I0 + ISH
HC0 = -(-H0 // P)
HP0 = (HC0 + 1) // 2
I1, R1 = 896, 64
IC1 = I1 // P
RC1 = E * R1 // P
EPS = 1e-5
SCALE = HD ** -0.5
LORA = 16.0 / 64.0
NEG = -1e30
ATT, FFN = 0, 1


def rows0(i):
    return min(P, H0 - i * P)


def chunks_of(p):
    return [i for i in (2 * p, 2 * p + 1) if i < HC0]


def plan():
    jobs = []
    state = {"ring": list(range(8)), "at": 0}

    def job(kind, *key, n=1, banks=None):
        if banks is None:
            banks = []
            for _ in range(n):
                banks.append(state["ring"][state["at"] % len(state["ring"])])
                state["at"] += 1
        jobs.append((kind, key, banks))

    def ring(banks):
        state["ring"], state["at"] = banks, 0

    def norm(L, half, b):
        job("ln", L, half, b, banks=[])

    def qkv(L, b):
        for j in range(TB):
            for i in range(-(-QKV[L] // 512)):
                job("qkv", L, b, j, i)

    def stack(L, b, j):
        for i in range(2):
            job("stq", L, b, j, i)
        for i in range(-(-NKV[L] // 8)):
            job("stk", L, b, j, i)

    def maxima(L, b, part):
        for i in range(part * 4, part * 4 + 4):
            if i < NH // 4:
                job("mx0", L, b, i)
            else:
                job("mx1", L, b, i - NH // 4)
        if part == 2:
            job("mp", L, b, banks=[])

    def attend(L, b):
        nb = b + 1
        units = NH // 2
        for u in range(units + 1):
            if u < units:
                job("T", L, b, u, banks=[2 * (u % 2), 2 * (u % 2) + 1])
            if nb < B:
                if u in (0, 1):
                    job("rope", L, nb, u, banks=[])
                if u in (3, 4):
                    stack(L, nb, u - 3)
                if u in (5, 6, 7):
                    maxima(L, nb, u - 5)
                if b + 2 < B:
                    if u == 2:
                        norm(L, ATT, b + 2)
                    if u == 5:
                        job("xT", L, ATT, b + 2)
            else:
                if u == 1:
                    norm(L, FFN, 0)
                if u == 3:
                    job("xT", L, FFN, 0)
                if u == 5:
                    job("rt", L, 0)
            if u > 0:
                job("pv", L, b, u - 1, banks=[4 + (u - 1) // 2 % 2])
        if b + 2 < B:
            qkv(L, b + 2)
        elif b == B - 1 and L == 0:
            job("wT", L, 0)
        job("op", L, b)
        if nb < B:
            job("mT", L, nb)

    for i in range(3):
        job("mod", 0, i)
    job("mt", 0)
    for L in range(2):
        ring(list(range(8)))
        if L == 0:
            norm(L, ATT, 0)
            job("xT", L, ATT, 0)
            qkv(L, 0)
            for j in range(TB):
                job("rope", L, 0, j, banks=[])
            for b in range(B):
                job("gb", L, b)
            norm(L, ATT, 1)
            job("xT", L, ATT, 1)
            for i in range(3):
                job("mod", 1, i)
            job("mt", 1)
        for j in range(TB):
            stack(L, 0, j)
        qkv(L, 1)
        for part in range(3):
            maxima(L, 0, part)
        job("mT", L, 0)
        ring([6, 7])
        for b in range(B):
            attend(L, b)
        ring(list(range(8)))
        if L == 0:
            ahead = 3
            for b in range(B):
                if b == 0:
                    for p in range(ahead):
                        job("g", b, p)
                        job("u", b, p)
                for p in range(HP0):
                    job("wb", b, p)
                    if p + ahead < HP0:
                        job("g", b, p + ahead)
                        job("u", b, p + ahead)
                    if p == 1 and b < B - 1:
                        norm(L, FFN, b + 1)
                    if p == 2 and b < B - 1:
                        job("xT", L, FFN, b + 1)
                    if p == 3 and b < B - 1:
                        job("rt", L, b + 1)
                    if b == B - 1:
                        if p == 0:
                            norm(1, ATT, 0)
                        if p == 1:
                            job("xT", 1, ATT, 0)
                        if p == 2:
                            qkv(1, 0)
                        if p in (3, 4):
                            job("rope", 1, 0, p - 3, banks=[])
                        if p == 4:
                            norm(1, ATT, 1)
                        if p == 5:
                            job("xT", 1, ATT, 1)
                if b < B - 1:
                    job("wT", L, b + 1)
                    for p in range(ahead):
                        job("g", b + 1, p)
                        job("u", b + 1, p)
                job("dn", L, b)
            for b in range(B):
                job("gb", 1, b)
        else:
            def inputs(b):
                for i in range(3):
                    job("base", b, i)
                job("wT", L, b)
                for k in range(2):
                    for q in range(RC1 // 2):
                        job("sel", b, k, q)
                job("base", b, 3)
                for c in range(RC1):
                    job("xa", b, c)
                for i in range(4, IC1):
                    job("base", b, i)
                job("wk", b)
            inputs(0)
            for b in range(B):
                for k in range(2):
                    for i in range(IC1):
                        job("lora", b, k, i)
                        if k == 0 and b < B - 1:
                            if i == 1:
                                norm(L, FFN, b + 1)
                            if i == 3:
                                job("xT", L, FFN, b + 1)
                            if i == 5:
                                job("rt", L, b + 1)
                for k in range(2):
                    for q in range(RC1 // 2):
                        job("da", b, k, q)
                if b < B - 1:
                    inputs(b + 1)
                job("dn", L, b)
    return jobs


INPUTS = [
    ("x", (P, B * TB, D), F32), ("cT", (P, 2, DC, B), F32), ("wmod0", (P, DC, 6 * D), F32), ("wmod1", (P, DC, 6 * D), F32),
    ("wqkv0", (P, DC, QKV[0]), F32), ("wo0", (P, DC, D), F32),
    ("wqkv1", (P, DC, QKV[1]), F32), ("wo1", (P, DC, D), F32),
    ("wr0", (P, DC, E + 1), F32), ("wr1", (P, DC, E), F32), ("bw", (P, 2, E), F32),
    ("wgu0", (P, DC, 2, H0), F32), ("wd0", (P, HC0, D), F32),
    ("wa1", (P, DC, 2, E * R1), F32), ("wbase1", (P, DC, 2, I1), F32),
    ("wb1", (P, RC1, 2, I1), F32), ("wda1", (P, IC1, E * R1), F32),
    ("wd1", (P, IC1, D), F32), ("wdb1", (P, RC1, D), F32),
    ("identf", (P, P), F32), ("rope", (P, 2, TB, 2, HD), F32),
    ("iota", (P, E), F32),
    ("identb", (P, P), BF16), ("maskT", (P, S), BF16), ("maskQ0", (P, P), BF16), ("maskQ1", (P, S), BF16),
    ("msel", (3 * NH, NH, P), BF16), ("wsel0", (3 * (E + 1), HC0, P), BF16),
    ("wsel1", (2 * E + 6, 2 * RC1 + 2, P), BF16),
]


def build(nc, dram, out):
    jobs = plan()
    order = {}
    nth = {}
    owner, before = {}, {}
    seen = {}
    finished = 0
    for n, (kind, key, banks) in enumerate(jobs):
        if not banks:
            continue
        group = key[:2] + (key[2] // 2,) if kind == "pv" else None
        finished += 1
        order[kind, key] = finished
        count_as = ("pv", group) if kind == "pv" else (kind, key)
        if count_as not in nth:
            nth[count_as] = seen.get(kind, 0)
            seen[kind] = seen.get(kind, 0) + 1
        before[n] = {owner[k] for k in banks if k in owner and owner[k] != count_as}
        for k in banks:
            owner[k] = count_as

    with ExitStack() as ctx:
        def sb(name, shape, dt):
            return ctx.enter_context(nc.sbuf_tensor(name, shape, dt))

        def sem(name):
            return ctx.enter_context(nc.semaphore(name))

        x = sb("x_resid", [P, B * TB, D], F32)
        hT = sb("hT", [P, 2, DC, S], F32)
        xn = sb("xn", [P, 2, TB, D], F32)
        gate = sb("gate_bcast", [P, B, 2, D], F32)
        gate4 = sb("gate_rows", [B, 2, 2, D], F32)
        modT = sb("modT", [P, 2, 8, B], F32)
        scT = sb("silu_cT", [P, 2, DC, B], F32)
        stats = sb("stats", [P, TB, 6], F32)
        mv = sb("mean_var", [P, 8, TB, 2], F32)
        ve = sb("var_eps", [P, 8, TB], F32)
        rstd = sb("rstd", [P, 8, TB], F32)
        mhalf = sb("minus_half", [P, TB], F32)
        tmp = sb("resid_tmp", [P, TB, D], F32)
        small = {}
        for name in ("cT", "wqkv1", "wo1", "wr0", "wr1", "bw", "identf",
                     "rope", "iota", "identb", "maskT", "maskQ0", "maskQ1", "msel", "wsel0", "wsel1"):
            shape, dt = next((s, d) for n, s, d in INPUTS if n == name)
            small[name] = sb("c_" + name, list(shape), dt)
        lg = sb("logits", [P, TB, E + 1], F32)
        bids = sb("bids", [P, TB, E], F32)
        top = sb("top", [P, TB, 8], F32)
        topi = sb("top_index", [P, TB, 8], U32)
        topf = sb("top_index_f", [P, TB, 8], F32)
        diff = sb("diff", [P, TB, 3], F32)
        sig = sb("sig", [P, TB, 3], F32)
        comb = sb("comb", [P, TB, E + 1], F32)
        comb2 = sb("comb2", [P, TB, E + 1], F32)
        wres = sb("w_rest", [P, TB, E + 1], F32)
        cp0 = sb("w_parts0", [P, 2, TB, 3, E + 1], BF16)
        cp1 = sb("w_parts1", [P, 2, TB, 2 * E + 6], BF16)
        wT = sb("w_partsT", [3 * (E + 1), 2, S], BF16)

        WB = DC * 2 * H0 + HC0 * D
        wreg = sb("expert_weights", [P, WB], F32)

        def carve(region, at, shape, dt=F32):
            n = int(np.prod(shape))
            words = n * (2 if dt == BF16 else 4) // 4
            v = region[:, at:at + words]
            if dt != F32:
                v = v.bitcast(dt)
            names = "abcde"[:len(shape)]
            if len(shape) > 1:
                v = v.rearrange(f"p ({' '.join(names)}) -> p {' '.join(names)}",
                                **dict(zip(names, shape)))
            return v, at + words

        wgu0, at = carve(wreg, 0, (DC, 2, H0))
        wd0, _ = carve(wreg, at, (HC0, D))
        wbase1, at = carve(wreg, 0, (DC, 2, I1))
        wa1, at = carve(wreg, at, (DC, 2, E * R1))
        wb1, at = carve(wreg, at, (RC1, 2, I1))
        assert at <= WB

        areg = sb("attention0_weights", [P, DC * (QKV[0] + D)], F32)
        small["wqkv0"], at = carve(areg, 0, (DC, QKV[0]))
        small["wo0"], _ = carve(areg, at, (DC, D))
        wdb1, _ = carve(areg, 0, (RC1, D))

        AR = 24576
        arena = sb("arena", [P, AR], F32)
        vpad, at = carve(arena, 0, (2, TB, NH, P))
        qk_at = at
        qT, at = carve(arena, at, (2, NH, S), BF16)
        kT, at = carve(arena, at, (2, NH, S), BF16)
        pr_at = at
        pr, at = carve(arena, at, (2, 3 * S))
        qs, at = carve(arena, at, (2, 2 * NH, NPART, HD), BF16)
        qkr, at = carve(arena, at, (2, 2 * NH, HD))
        rot, at = carve(arena, at, (2 * NH, HD))
        rot2, at = carve(arena, at, (2 * NH, HD))
        aT, at = carve(arena, at, (2, DC, S))
        rs, at = carve(arena, at, (S,))
        assert at <= AR
        mx = sb("row_max", [P, 2, TB, NH], F32)
        mrest = sb("max_rest", [P, TB, NH], F32)
        mparts = sb("max_parts", [P, 2, TB, 3, NH], BF16)
        mT = sb("max_T", [3 * NH, 2, S], BF16)
        wmod, at = carve(arena, qk_at, (2, DC, 6 * D))
        modr = [carve(arena, w, (6 * D,))[0] for w in (at, pr_at)]
        hid0, at = carve(arena, qk_at, (2, HC0, S))
        s0, at = carve(arena, at, (2, 2, S))
        xam, at = carve(arena, 0, (2, RC1, 2, S))
        base, at = carve(arena, at, (IC1, 2, S))
        hk, at = carve(arena, at, (2, IC1, S))
        hw, at = carve(arena, at, (IC1, S))
        selb, at = carve(arena, at, (2, RC1, S), BF16)
        wkb, at = carve(arena, at, (2, S))
        gu1, at = carve(arena, at, (2, 2, S))
        sl1, at = carve(arena, at, (2, S))
        hm, at = carve(arena, at, (2, S))
        tk, at = carve(arena, at, (RC1, S))
        tk1, at = carve(arena, at, (2, 2, S))
        wda1, at = carve(arena, at, (IC1, E * R1))
        wd1, at = carve(arena, at, (IC1, D))
        assert at <= AR, at

        pt = ctx.enter_context(nc.psum_tensor("psum", [P, 8, 512], F32))
        ptb = pt[:, :, :].bitcast(BF16)

        pe_jobs = sem("pe_jobs")
        done = {k: sem("done_" + k) for k in seen}
        loaded = {n: sem("ld_" + n) for n, _, _ in INPUTS}
        silu_ready = sem("silu_ready")
        gates_ready = sem("gates_ready")
        stats_ready, rstd_ready, xn_ready = sem("stats_ready"), sem("rstd_ready"), sem("xn_ready")
        vpad_ready, mhalf_ready = sem("vpad_ready"), sem("mhalf_ready")
        roped = sem("roped")
        parts_ready = sem("parts_ready")
        stack_ready = sem("stack_ready")
        max_ready = sem("max_parts_ready")
        diff_ready, sig_ready = sem("diff_ready"), sem("sig_ready")
        z_ready, conf_ready = sem("z_ready"), sem("conf_ready")
        wparts_ready = sem("wparts_ready")
        hid_ready = sem("hid_ready")
        silu0 = sem("silu0_ready")
        silu1 = sem("silu1_ready")
        h_ready = sem("h_ready")
        hw_ready = sem("hw_ready")
        tsum_ready, tprod_ready = sem("tsum_ready"), sem("tprod_ready")
        out_ready, stored = sem("out_ready"), sem("stored")
        dve_step, act_step, pool_step = sem("dve_step"), sem("act_step"), sem("pool_step")

        def after_pe(eng, kind, key):
            eng.wait_ge(pe_jobs, order[kind, key])

        def after(eng, kind, key):
            eng.wait_ge(done[kind], nth[kind, key] + 1)

        def need(eng, *names):
            for n in names:
                eng.wait_ge(loaded[n], 16)

        def chain(eng, s):
            count = [0]

            def link(ins):
                count[0] += 1
                ins.then_inc(s, 1)
                eng.wait_ge(s, count[0])
            return link

        def step_of(L, half, b):
            return (2 * L + half) * B + b

        def tok(L, b, j):
            return (L * B + b) * TB + j

        def unit(L, b, u):
            return (L * B + b) * (NH // 2) + u

        def p_slot(b, p):
            return (b * HP0 + p) % 2

        block = ctx.enter_context(nc.Block())

        @block.sync
        def _(sp):
            def load(name, dst):
                sp.dma_start(dst, dram[name]).then_inc(loaded[name], 16)

            def load_small(name):
                t = small[name]
                load(name, t[tuple(slice(None) for _ in t.shape)])

            load_small("cT")
            load("wmod0", wmod[:, 0, :, :])
            sp.dma_start(x[:, :, :], dram["x"]).then_inc(loaded["x"], 16)
            for name in ("identf", "wqkv0", "rope", "identb"):
                load_small(name)
            load("wmod1", wmod[:, 1, :, :])
            for name in ("maskQ0", "maskQ1", "msel", "maskT", "wo0", "wr0", "iota", "wsel0"):
                load_small(name)
            load("wgu0", wgu0)
            load("wd0", wd0)
            for name in ("wqkv1", "wo1", "wr1", "bw", "wsel1"):
                load_small(name)
            after_pe(sp, "dn", (0, B - 1))
            load("wdb1", wdb1)
            load("wbase1", wbase1)
            load("wa1", wa1)
            load("wb1", wb1)
            after(sp, "op", (1, B - 1))
            load("wda1", wda1)
            load("wd1", wd1)
            for b in range(B):
                sp.wait_ge(out_ready, b + 1)
                sp.dma_start(out.rearrange("b (j p) d -> p (b j) d", p=P)[:, b * TB:(b + 1) * TB, :],
                             x[:, b * TB:(b + 1) * TB, :]).then_inc(stored, 16)
            sp.wait_ge(stored, 16 * B)

        @block.tensor
        def _(pe):
            mm = nc.tensor.matmul
            for n, (kind, key, banks) in enumerate(jobs):
                if not banks:
                    continue
                for k, kk in sorted(before[n]):
                    pe.wait_ge(done[k], nth[k, kk] + 1)
                pb = pt[:, banks[0], :]
                if kind == "mod":
                    L, i = key
                    if i == 0:
                        pe.wait_ge(silu_ready, L + 1)
                        need(pe, f"wmod{L}")
                    for c in range(DC):
                        last = mm(pb[0:B, :], scT[:, L, c, :], wmod[:, L, c, i * 512:(i + 1) * 512],
                                  start=c == 0, stop=c == DC - 1)
                elif kind == "mt":
                    L, = key
                    need(pe, "identf")
                    after(pe, "mod", (L, 2))
                    for q, col in enumerate((0, 128, 256, 384, 768, 896, 1024, 1152)):
                        last = nc.tensor.transpose(pb[:, q * B:(q + 1) * B], modr[L][0:B, col:col + P],
                                                   small["identf"][0:B, 0:B])
                elif kind == "gb":
                    L, b = key
                    need(pe, "identf")
                    pe.wait_ge(gates_ready, L + 1)
                    last = mm(pb, small["identf"][0:B, b:b + 1].broadcast_to((B, P)),
                              gate4[:, L, :, :].rearrange("p g d -> p (g d)"), start=True, stop=True)
                elif kind == "xT":
                    L, half, b = key
                    st = step_of(*key)
                    need(pe, "identf")
                    pe.wait_ge(xn_ready, st + 1)
                    for c in range(DC):
                        for j in range(TB):
                            last = nc.tensor.transpose(pb[:, c * S + j * P:c * S + (j + 1) * P],
                                                       xn[:, st % 2, j, c * P:(c + 1) * P],
                                                       small["identf"][:, :])
                elif kind == "qkv":
                    L, b, j, i = key
                    st = step_of(L, ATT, b)
                    after(pe, "xT", (L, ATT, b))
                    need(pe, f"wqkv{L}")
                    w = small[f"wqkv{L}"]
                    lo, hi = i * 512, min(i * 512 + 512, QKV[L])
                    for c in range(DC):
                        last = mm(pb[:, 0:hi - lo], hT[:, st % 2, c, j * P:(j + 1) * P], w[:, c, lo:hi],
                                  start=c == 0, stop=c == DC - 1)
                elif kind in ("stq", "stk"):
                    L, b, j, i = key
                    need(pe, "identb")
                    pe.wait_ge(stack_ready, tok(L, b, j) + 1)
                    h0 = (NH if kind == "stk" else 0) + 8 * i
                    nh = min(8, NKV[L]) if kind == "stk" else 8
                    for h in range(nh):
                        last = nc.tensor.transpose(
                            ptb[0:NPART * HD, banks[0], h * P:(h + 1) * P],
                            qs[:, tok(L, b, j) % 2, h0 + h, :, :].rearrange("p s d -> p (s d)"),
                            small["identb"][:, :])
                elif kind in ("mx0", "mx1"):
                    L, b, i = key
                    if kind == "mx0" and i == 0:
                        need(pe, "maskQ0", "maskQ1")
                        after(pe, "stq", (L, b, TB - 1, 1))
                        after(pe, "stk", (L, b, TB - 1, -(-NKV[L] // 8) - 1))
                    j = 0 if kind == "mx0" else 1
                    nk = P * (j + 1)
                    nh = 512 // nk
                    mask = small["maskQ0"][:, :] if j == 0 else small["maskQ1"][:, :]
                    mm(pb.rearrange("p (h k) -> p h k", h=nh), small["identb"][:, :],
                       mask.unsqueeze(1).broadcast_to((P, nh, nk)), start=True, stop=False)
                    for q in range(nh):
                        h = i * nh + q
                        last = mm(pb[:, q * nk:(q + 1) * nk],
                                  qT[0:NPART * HD, b % 2, h, j * P:(j + 1) * P],
                                  kT[0:NPART * HD, b % 2, h * NKV[L] // NH, 0:nk],
                                  start=False, stop=q == nh - 1)
                elif kind == "mT":
                    L, b = key
                    pe.wait_ge(max_ready, L * B + b + 1)
                    for j in range(TB):
                        last = nc.tensor.transpose(
                            ptb[0:3 * NH, banks[0], j * P:(j + 1) * P],
                            mparts[:, b % 2, j, :, :].rearrange("p s h -> p (s h)"), small["identb"][:, :])
                elif kind == "T":
                    L, b, u = key
                    if u == 0:
                        need(pe, "maskT", "msel")
                        after(pe, "mT", (L, b))
                    pb2 = pt[:, banks[1], :]
                    for kc, (bank, nq) in enumerate(((pb, S), (pb2, P))):
                        mm(bank[:, 0:2 * nq].rearrange("p (h k) -> p h k", h=2), small["identb"][:, :],
                           small["maskT"][:, 0:nq].unsqueeze(1).broadcast_to((P, 2, nq)),
                           start=True, stop=False)
                        for i in range(2):
                            h = 2 * u + i
                            o = bank[:, i * nq:(i + 1) * nq]
                            mm(o, kT[0:NPART * HD, b % 2, h * NKV[L] // NH, kc * P:(kc + 1) * P],
                               qT[0:NPART * HD, b % 2, h, S - nq:S], start=False, stop=False)
                            last = mm(o, small["msel"][:, h, :], mT[:, b % 2, S - nq:S],
                                      start=False, stop=i == 1)
                elif kind == "pv":
                    L, b, u = key
                    after(pe, "T", (L, b, u))
                    need_v = -(-QKV[L] // 512) - 1
                    if u == 0:
                        after(pe, "qkv", (L, b, TB - 1, need_v))
                        pe.wait_ge(vpad_ready, 2)
                    pu = unit(L, b, u) % 2
                    for i in range(2):
                        h = 2 * u + i
                        mm(pb[:, 0:S], vpad[:, b % 2, 0, h, :], pr[:, pu, i * S:(i + 1) * S],
                           start=u % 2 == 0 and i == 0, stop=False)
                        last = mm(pb[:, P:S], vpad[:, b % 2, 1, h, :],
                                  pr[:, pu, 2 * S + i * P:2 * S + (i + 1) * P],
                                  start=False, stop=u % 2 == 1 and i == 1)
                elif kind == "op":
                    L, b = key
                    need(pe, f"wo{L}")
                    after(pe, "pv", (L, b, NH // 4 - 1))
                    for j in range(TB):
                        for c in range(DC):
                            last = mm(pb[:, j * D:(j + 1) * D], aT[:, b % 2, c, j * P:(j + 1) * P],
                                      small[f"wo{L}"][:, c, :], start=c == 0, stop=c == DC - 1)
                elif kind == "rt":
                    L, b = key
                    ne = E + 1 - L
                    need(pe, f"wr{L}")
                    after(pe, "xT", (L, FFN, b))
                    st = step_of(L, FFN, b)
                    for j in range(TB):
                        for c in range(DC):
                            last = mm(pb[:, j * ne:(j + 1) * ne], hT[:, st % 2, c, j * P:(j + 1) * P],
                                      small[f"wr{L}"][:, c, :], start=c == 0, stop=c == DC - 1)
                elif kind == "wT":
                    L, b = key
                    pe.wait_ge(wparts_ready, L * B + b + 1)
                    for j in range(TB):
                        if L == 0:
                            nr, src = 3 * (E + 1), cp0[:, b % 2, j, :, :].rearrange("p s e -> p (s e)")
                        else:
                            nr, src = 2 * E + 6, cp1[:, b % 2, j, :]
                        last = nc.tensor.transpose(ptb[0:nr, banks[0], j * P:(j + 1) * P], src,
                                                   small["identb"][:, :])
                elif kind in ("g", "u"):
                    b, p = key
                    st = step_of(0, FFN, b)
                    if kind == "g" and p == 0:
                        need(pe, "wgu0")
                    for q, i in enumerate(chunks_of(p)):
                        for c in range(DC):
                            last = mm(pb[0:rows0(i), q * S:(q + 1) * S],
                                      wgu0[:, c, int(kind == "u"), i * P:i * P + rows0(i)],
                                      hT[:, st % 2, c, :], start=c == 0, stop=c == DC - 1)
                elif kind == "wb":
                    b, p = key
                    if p == 0:
                        need(pe, "wsel0")
                        after(pe, "wT", (0, b))
                    for q, i in enumerate(chunks_of(p)):
                        last = mm(pb[0:rows0(i), q * S:(q + 1) * S], small["wsel0"][:, i, 0:rows0(i)],
                                  wT[0:3 * (E + 1), b % 2, :], start=True, stop=True)
                elif kind == "dn":
                    L, b = key
                    if L == 0:
                        need(pe, "wd0")
                        after(pe, "wb", (b, HP0 - 1))
                        terms = [(hid0[0:rows0(i), b % 2, i, :], wd0[0:rows0(i), i, :]) for i in range(HC0)]
                    else:
                        need(pe, "wd1", "wdb1")
                        pe.wait_ge(hw_ready, (b + 1) * IC1)
                        pe.wait_ge(tsum_ready, (b + 1) * (RC1 // 2))
                        terms = [(hw[:, i, :], wd1[:, i, :]) for i in range(IC1)]
                        terms += [(tk[:, c, :], wdb1[:, c, :]) for c in range(RC1)]
                    for j in range(TB):
                        for i, (h, w) in enumerate(terms):
                            last = mm(pb[:, j * D:(j + 1) * D], h[:, j * P:(j + 1) * P], w,
                                      start=i == 0, stop=i == len(terms) - 1)
                elif kind == "base":
                    b, i = key
                    st = step_of(1, FFN, b)
                    need(pe, "wbase1")
                    for g in range(2):
                        for c in range(DC):
                            last = mm(pb[:, g * S:(g + 1) * S], wbase1[:, c, g, i * P:(i + 1) * P],
                                      hT[:, st % 2, c, :], start=c == 0, stop=c == DC - 1)
                elif kind == "sel":
                    b, k, q = key
                    if k == 0 and q == 0:
                        need(pe, "wsel1")
                        after(pe, "wT", (1, b))
                    for i in range(2):
                        last = mm(pb[:, i * S:(i + 1) * S], small["wsel1"][:, k * RC1 + 2 * q + i, :],
                                  wT[0:2 * E + 6, b % 2, :], start=True, stop=True)
                elif kind == "wk":
                    b, = key
                    for k in range(2):
                        last = mm(pb[:, k * S:(k + 1) * S], small["wsel1"][:, 2 * RC1 + k, :],
                                  wT[0:2 * E + 6, b % 2, :], start=True, stop=True)
                elif kind == "xa":
                    b, c2 = key
                    st = step_of(1, FFN, b)
                    need(pe, "wa1")
                    for g in range(2):
                        for c in range(DC):
                            last = mm(pb[:, g * S:(g + 1) * S], wa1[:, c, g, c2 * P:(c2 + 1) * P],
                                      hT[:, st % 2, c, :], start=c == 0, stop=c == DC - 1)
                elif kind == "lora":
                    b, k, i = key
                    need(pe, "wb1")
                    after(pe, "xa", (b, RC1 - 1))
                    for g in range(2):
                        for c in range(RC1):
                            last = mm(pb[:, g * S:(g + 1) * S], wb1[:, c, g, i * P:(i + 1) * P],
                                      xam[:, k, c, g, :], start=c == 0, stop=c == RC1 - 1)
                elif kind == "da":
                    b, k, q = key
                    need(pe, "wda1")
                    pe.wait_ge(h_ready, (2 * b + k + 1) * IC1)
                    for i2 in range(2):
                        c2 = 2 * q + i2
                        for i in range(IC1):
                            last = mm(pb[:, i2 * S:(i2 + 1) * S], wda1[:, i, c2 * P:(c2 + 1) * P],
                                      hk[:, k, i, :], start=i == 0, stop=i == IC1 - 1)
                last.then_inc(pe_jobs, 1)

        @block.scalar
        def _(act):
            need(act, "cT")
            for L in range(2):
                nc.scalar.activation(scT[:, L, :, :], small["cT"][:, L, :, :], ACT.Silu).then_inc(silu_ready, 1)
            for kind, key, banks in jobs:
                pb = pt[:, banks[0], :] if banks else None

                def copy_out(dst, src, kind=kind, key=key):
                    nc.scalar.activation(dst, src, ACT.Copy).then_inc(done[kind], 1)

                if kind == "gb":
                    L, b = key
                    after_pe(act, kind, key)
                    if L == 1:
                        after(act, "dn", (0, b))
                    copy_out(gate[:, b, :, :], pb.rearrange("p (g d) -> p g d", g=2))
                elif kind == "xT":
                    L, half, b = key
                    st = step_of(*key)
                    after(act, "mt", (L,))
                    after_pe(act, kind, key)
                    if st >= 2:
                        L2, half2, b2 = (st - 2) // (2 * B), (st - 2) // B % 2, (st - 2) % B
                        if half2 == ATT:
                            after_pe(act, "qkv", (L2, b2, TB - 1, -(-QKV[L2] // 512) - 1))
                        elif L2 == 0:
                            after_pe(act, "u", (b2, HP0 - 1))
                        else:
                            after_pe(act, "xa", (b2, RC1 - 1))
                    for c in range(DC):
                        ins = nc.scalar.activation(hT[:, st % 2, c, :], pb[:, c * S:(c + 1) * S], ACT.Identity,
                                                   bias=modT[:, L, 4 * half + c, b:b + 1],
                                                   scale=modT[:, L, 4 * half + 2 + c, b:b + 1])
                    ins.then_inc(done[kind], 1)
                elif kind == "qkv":
                    L, b, j, i = key
                    t = tok(L, b, j)
                    after_pe(act, kind, key)
                    split = QK[L]
                    parts = [(lo, hi) for lo, hi in ((0, split), (split, QKV[L]))]
                    b_lo, b_hi = i * 512, min(i * 512 + 512, QKV[L])
                    todo = []
                    for which, (lo, hi) in enumerate(parts):
                        lo2, hi2 = max(lo, b_lo), min(hi, b_hi)
                        if lo2 < hi2:
                            todo.append((which, lo2, hi2))
                    for n, (which, lo, hi) in enumerate(todo):
                        if which == 0:
                            if t >= 2:
                                act.wait_ge(roped, t - 1)
                            ins = nc.scalar.activation(
                                qkr[:, t % 2, :, :].rearrange("p h d -> p (h d)")[:, lo:hi],
                                pb[:, lo - b_lo:hi - b_lo], ACT.Copy)
                        else:
                            if j == 0 and b >= 2:
                                after_pe(act, "pv", (L, b - 2, NH // 2 - 1))
                            if t == 0:
                                act.wait_ge(vpad_ready, 2)
                            v = vpad[:, b % 2, j, :, :]
                            dst = bass.AP(v.tensor, v.offset,
                                          [v.ap[0], [4 * P, NH // 4], [P + HD, 4], [1, HD]])
                            src = pb[:, lo - b_lo:hi - b_lo]
                            if NKV[L] == NH:
                                src = src.rearrange("p (g j d) -> p g j d", g=NH // 4, j=4)
                            else:
                                src = src.rearrange("p (g d) -> p g d", g=NH // 4).unsqueeze(2)\
                                    .broadcast_to((P, NH // 4, 4, HD))
                            ins = nc.scalar.activation(dst, src, ACT.Copy)
                    ins.then_inc(done[kind], 1)
                elif kind == "stq":
                    L, b, j, i = key
                    after_pe(act, kind, key)
                    if b >= 2 and j == 0 and i == 0:
                        after_pe(act, "T", (L, b - 2, NH // 2 - 1))
                    copy_out(qT[0:NPART * HD, b % 2, 8 * i:8 * i + 8, j * P:(j + 1) * P],
                             ptb[0:NPART * HD, banks[0], :].rearrange("p (h q) -> p h q", h=8))
                elif kind == "mT":
                    L, b = key
                    after_pe(act, kind, key)
                    if b >= 2:
                        after_pe(act, "T", (L, b - 2, NH // 2 - 1))
                    copy_out(mT[:, b % 2, :], ptb[0:3 * NH, banks[0], 0:S])
                elif kind == "T":
                    L, b, u = key
                    n = unit(L, b, u)
                    after_pe(act, kind, key)
                    if n >= 2:
                        q = n - 2
                        after_pe(act, "pv", (q // (NH // 2) // B, q // (NH // 2) % B, q % (NH // 2)))
                    src = pt[:, banks[0]:banks[0] + 2, :].rearrange("p b n -> p (b n)")[:, 0:3 * S]
                    nc.scalar.activation(pr[:, n % 2, :], src, ACT.Exp, scale=SCALE).then_inc(done[kind], 1)
                elif kind == "rt":
                    L, b = key
                    if L == 1:
                        act.wait_ge(z_ready, b + 1)
                        nc.scalar.activation(bids[:, :, :], lg[:, :, 0:E], ACT.Tanh, scale=0.5).then_inc(conf_ready, 1)
                    act.wait_ge(diff_ready, L * B + b + 1)
                    nc.scalar.activation(sig[:, :, :], diff[:, :, :], ACT.Tanh, scale=0.5).then_inc(sig_ready, 1)
                elif kind == "wT":
                    L, b = key
                    nr = 3 * (E + 1) if L == 0 else 2 * E + 6
                    after_pe(act, kind, key)
                    if b >= 2:
                        if L == 0:
                            after_pe(act, "wb", (b - 2, HP0 - 1))
                        else:
                            after_pe(act, "wk", (b - 2,))
                    copy_out(wT[0:nr, b % 2, :], ptb[0:nr, banks[0], 0:S])
                elif kind == "g":
                    b, p = key
                    after_pe(act, kind, key)
                    n = b * HP0 + p
                    if n >= 2:
                        pp = n - 2
                        after(act, "u", (pp // HP0, pp % HP0))
                    nr, m = rows0(chunks_of(p)[-1]), len(chunks_of(p))
                    nc.scalar.activation(s0[0:nr, p_slot(b, p), 0:m, :],
                                         pb[0:nr, 0:m * S].rearrange("p (q s) -> p q s", q=m),
                                         ACT.Silu).then_inc(done[kind], 1)
                elif kind == "base":
                    b, i = key
                    after_pe(act, kind, key)
                    if b > 0:
                        after(act, "lora", (b - 1, 1, i))
                    copy_out(base[:, i, :, :], pb.rearrange("p (g s) -> p g s", g=2))
                elif kind == "sel":
                    b, k, q = key
                    after_pe(act, kind, key)
                    if b > 0:
                        after(act, "da", (b - 1, k, q))
                    copy_out(selb[:, k, 2 * q:2 * q + 2, :], pb.rearrange("p (g s) -> p g s", g=2))
                elif kind == "wk":
                    b, = key
                    after_pe(act, kind, key)
                    if b > 0:
                        act.wait_ge(tsum_ready, b * (RC1 // 2))
                        act.wait_ge(hw_ready, b * IC1)
                    copy_out(wkb[:, :, :], pb.rearrange("p (g s) -> p g s", g=2))
                elif kind == "lora":
                    b, k, i = key
                    n = (2 * b + k) * IC1 + i
                    after(act, kind, key)
                    if n >= 2:
                        act.wait_ge(h_ready, n - 1)
                    nc.scalar.activation(sl1[:, n % 2, :], gu1[:, n % 2, 0, :], ACT.Silu).then_inc(silu1, 1)

        @block.vector
        def _(dve):
            link = chain(dve, dve_step)
            vec = nc.vector

            def layer_stats(st):
                b = st % B
                if st:
                    dve.wait_ge(stats_ready, st)
                for j in range(TB):
                    ins = vec.bn_stats(stats[:, j, :], x[:, b * TB + j, :])
                link(ins)
                for j in range(TB):
                    ins = vec.bn_aggr(mv[:, st % 8, j, :], stats[:, j, :])
                ins.then_inc(stats_ready, 1)

            def residual(kind, L, half, b, banks):
                after_pe(dve, kind, (L, b))
                after(dve, "gb", (L, b))
                vec.tensor_tensor(tmp[:, :, :], pt[:, banks[0], :].rearrange("p (j d) -> p j d", j=TB),
                                  gate[:, b, half, :].unsqueeze(1).broadcast_to((P, TB, D)),
                                  ALU.mult).then_inc(done[kind], 1)
                after(dve, kind, (L, b))
                xb = x[:, b * TB:(b + 1) * TB, :]
                ins = vec.tensor_tensor(xb, xb, tmp[:, :, :], ALU.add)
                if L == 1 and half == FFN:
                    ins.then_inc(out_ready, 1)
                    return
                link(ins)
                layer_stats(step_of(L, half, b) + B)

            def bf16_parts(src, rest, dst):
                link(vec.tensor_copy(dst(0), src))
                link(vec.tensor_tensor(rest, src, dst(0), ALU.subtract))
                link(vec.tensor_copy(dst(1), rest))
                return vec.tensor_tensor(dst(2), rest, dst(1), ALU.subtract)

            need(dve, "x")
            for b in range(B):
                layer_stats(b)
            for kind, key, banks in jobs:
                pb = pt[:, banks[0], :] if banks else None
                if kind == "mod":
                    L, i = key
                    after_pe(dve, kind, key)
                    vec.tensor_copy(modr[L][0:B, i * 512:(i + 1) * 512], pb[0:B, :]).then_inc(done[kind], 1)
                    if i == 2:
                        after(dve, kind, key)
                        g = modr[L][0:B, :].rearrange("p (g k d) -> p g k d", g=2, k=3)[:, :, 2, :]
                        a, s = tmp[0:B, :, :], gate4[:, L, :, :]
                        link(vec.scalar_tensor_tensor(a, g, -1.0, g, ALU.mult, ALU.max))
                        vec.tensor_scalar(s, g, 0.0, 2.0, ALU.is_ge, ALU.mult)
                        link(vec.tensor_scalar(a, a, 0.25, None, ALU.max))
                        vec.scalar_tensor_tensor(s, s, -1.0, a, ALU.add, ALU.mult).then_inc(gates_ready, 1)
                elif kind == "mt":
                    L, = key
                    after_pe(dve, kind, key)
                    link(vec.tensor_copy(modT[:, L, :, :], pb[:, 0:8 * B].rearrange("p (q b) -> p q b", q=8)))
                    m = modT[:, L, :, :].rearrange("p (g k c) b -> p g k (c b)", g=2, k=2)[:, :, 1, :]
                    vec.tensor_scalar(m, m, 1.0, None, ALU.add).then_inc(done[kind], 1)
                elif kind == "ln":
                    L, half, b = key
                    st = step_of(*key)
                    dve.wait_ge(rstd_ready, st + 1)
                    if st >= 2:
                        q = st - 2
                        after_pe(dve, "xT", (q // (2 * B), q // B % 2, q % B))
                    for j in range(TB):
                        ins = vec.tensor_scalar(xn[:, st % 2, j, :], x[:, b * TB + j, :],
                                                mv[:, st % 8, j, 0:1], rstd[:, st % 8, j:j + 1],
                                                ALU.subtract, ALU.mult)
                    ins.then_inc(xn_ready, 1)
                elif kind == "rope":
                    L, b, j = key
                    t = tok(L, b, j)
                    nh = NH + NKV[L]
                    need(dve, "rope")
                    after(dve, "qkv", (L, b, j, -(-QKV[L] // 512) - 1))
                    r = qkr[:, t % 2, 0:nh, :]
                    o, o2 = rot[:, 0:nh, :], rot2[:, 0:nh, :]
                    cs = small["rope"][:, L, j, 0, :].unsqueeze(1).broadcast_to((P, nh, HD))
                    sn = small["rope"][:, L, j, 1, :].unsqueeze(1).broadcast_to((P, nh, HD))
                    hh = HD // 2
                    if t:
                        dve.wait_ge(parts_ready, t)
                    vec.tensor_tensor(o, r, cs, ALU.mult)
                    vec.tensor_tensor(o2[:, :, 0:hh], r[:, :, hh:HD], sn[:, :, 0:hh], ALU.mult)
                    vec.tensor_tensor(o2[:, :, hh:HD], r[:, :, 0:hh], sn[:, :, hh:HD], ALU.mult).then_inc(roped, 1)
                    dve.wait_ge(roped, t + 1)
                    link(vec.tensor_tensor(o, o, o2, ALU.add))
                    if t >= 2:
                        q = t - 2
                        after_pe(dve, "stk", (q // (B * TB), q // TB % B, q % TB,
                                              -(-NKV[q // (B * TB)] // 8) - 1))
                    st_ = qs[:, t % 2, :, :, :]
                    link(vec.tensor_copy(st_[:, 0:nh, 0, :], o))
                    link(vec.tensor_tensor(o2, o, st_[:, 0:nh, 0, :], ALU.subtract))
                    link(vec.tensor_copy(st_[:, 0:nh, 1, :], o2))
                    vec.tensor_tensor(st_[:, 0:NH, 5, :], o2[:, 0:NH, :], st_[:, 0:NH, 1, :], ALU.subtract)
                    vec.tensor_tensor(st_[:, NH:nh, 4, :], o2[:, NH:nh, :], st_[:, NH:nh, 1, :],
                                      ALU.subtract).then_inc(parts_ready, 1)
                elif kind == "stk":
                    L, b, j, i = key
                    n = min(8, NKV[L])
                    after_pe(dve, kind, key)
                    if b >= 2 and j == 0 and i == 0:
                        after_pe(dve, "T", (L, b - 2, NH // 2 - 1))
                    vec.tensor_copy(kT[0:NPART * HD, b % 2, 8 * i:8 * i + n, j * P:(j + 1) * P],
                                    ptb[0:NPART * HD, banks[0], 0:n * P].rearrange("p (h q) -> p h q", h=n))\
                       .then_inc(done[kind], 1)
                elif kind in ("mx0", "mx1"):
                    L, b, i = key
                    j = 0 if kind == "mx0" else 1
                    nh = 512 // (P * (j + 1))
                    after_pe(dve, kind, key)
                    vec.tensor_reduce(mx[:, b % 2, j, i * nh:(i + 1) * nh], pb.rearrange("p (h k) -> p h k", h=nh),
                                      AX, ALU.max).then_inc(done[kind], 1)
                elif kind == "mp":
                    L, b = key
                    after(dve, "mx1", (L, b, NH // 2 - 1))
                    if L or b:
                        dve.wait_ge(max_ready, L * B + b)
                    bf16_parts(mx[:, b % 2, :, :], mrest[:, :, :],
                               lambda s: mparts[:, b % 2, :, s, :]).then_inc(max_ready, 1)
                elif kind == "pv":
                    L, b, u = key
                    if u % 2 == 0:
                        continue
                    g = u // 2
                    after_pe(dve, kind, key)
                    if L or b or g:
                        dve.wait_ge(done[kind], nth[kind, (L, b, g)])
                    if b >= 2 and g == 0:
                        after_pe(dve, "op", (L, b - 2))
                    link(vec.reciprocal(rs[0:P // 2, :], pb[P // 2:P, 0:S]))
                    lo = P // 2 * (g % 2)
                    vec.tensor_tensor(aT[lo:lo + P // 2, b % 2, g // 2, :], pb[0:P // 2, 0:S],
                                      rs[0:P // 2, :], ALU.mult).then_inc(done[kind], 1)
                elif kind == "op":
                    residual(kind, key[0], ATT, key[1], banks)
                elif kind == "rt":
                    L, b = key
                    after_pe(dve, kind, key)
                    ne = E + 1 - L
                    if L or b:
                        dve.wait_ge(wparts_ready, L * B + b)
                    src = pb[:, 0:TB * ne].rearrange("p (j e) -> p j e", j=TB)
                    if L == 0:
                        vec.tensor_copy(lg[:, :, :], src).then_inc(done[kind], 1)
                        after(dve, kind, key)
                        vals = lg
                    else:
                        need(dve, "bw")
                        vec.tensor_tensor(lg[:, :, 0:E], src,
                                          small["bw"][:, 0:1, :].broadcast_to((P, TB, E)),
                                          ALU.add).then_inc(done[kind], 1)
                        after(dve, kind, key)
                        vec.tensor_copy(comb2[:, :, 0:E], lg[:, :, 0:E]).then_inc(z_ready, 1)
                        dve.wait_ge(conf_ready, b + 1)
                        link(vec.tensor_scalar(bids[:, :, :], bids[:, :, :], 0.5, 0.5, ALU.mult, ALU.add))
                        link(vec.tensor_tensor(bids[:, :, :], bids[:, :, :],
                                               small["bw"][:, 1:2, :].broadcast_to((P, TB, E)), ALU.mult))
                        vals = bids
                    for j in range(TB):
                        ins = vec.max(top[:, j, :], vals[:, j, 0:E])
                    link(ins)
                    for j in range(TB):
                        vec.max_index(topi[:, j, :], top[:, j, :], vals[:, j, 0:E])
                    if L == 0:
                        vec.tensor_copy(diff[:, :, 2:3], lg[:, :, E:E + 1])
                    else:
                        vec.tensor_copy(diff[:, :, 2:3], top[:, :, 0:1])
                    vec.tensor_tensor(diff[:, :, 1:2], top[:, :, 1:2], top[:, :, 0:1], ALU.subtract)
                    vec.tensor_tensor(diff[:, :, 0:1], top[:, :, 0:1], top[:, :, 1:2],
                                      ALU.subtract).then_inc(diff_ready, 1)
                    dve.wait_ge(diff_ready, L * B + b + 1)
                    link(vec.tensor_copy(topf[:, :, :], topi[:, :, :]))
                    need(dve, "iota")
                    dve.wait_ge(sig_ready, L * B + b + 1)
                    link(vec.tensor_scalar(sig[:, :, :], sig[:, :, :], 0.5, 0.5, ALU.mult, ALU.add))
                    if b >= 2:
                        after_pe(dve, "wT", (L, b - 2))
                    if L == 0:
                        for j in range(TB):
                            vec.tensor_scalar(comb[:, j, 0:E], small["iota"][:, :], topf[:, j, 0:1],
                                              sig[:, j, 0:1], ALU.is_equal, ALU.mult)
                            ins = vec.tensor_scalar(comb2[:, j, 0:E], small["iota"][:, :], topf[:, j, 1:2],
                                                    sig[:, j, 1:2], ALU.is_equal, ALU.mult)
                        link(ins)
                        vec.tensor_tensor(comb[:, :, 0:E], comb[:, :, 0:E], comb2[:, :, 0:E], ALU.add)
                        link(vec.tensor_copy(comb[:, :, E:E + 1], sig[:, :, 2:3]))
                        bf16_parts(comb[:, :, :], wres[:, :, :],
                                   lambda s: cp0[:, b % 2, :, s, :]).then_inc(wparts_ready, 1)
                    else:
                        for j in range(TB):
                            for k in range(2):
                                vec.tensor_scalar(cp1[:, b % 2, j, k * E:(k + 1) * E], small["iota"][:, :],
                                                  topf[:, j, k:k + 1], None, ALU.is_equal)
                        bf16_parts(sig[:, :, 0:2], wres[:, :, 0:2],
                                   lambda s: cp1[:, b % 2, :, 2 * E + 2 * s:2 * E + 2 * s + 2])\
                            .then_inc(wparts_ready, 1)
                elif kind == "u":
                    b, p = key
                    after(dve, "g", (b, p))
                    after_pe(dve, kind, key)
                    if b > 1 and p == 0:
                        after_pe(dve, "dn", (0, b - 2))
                    i0, m = 2 * p, len(chunks_of(p))
                    nr = rows0(i0 + m - 1)
                    vec.tensor_tensor(hid0[0:nr, b % 2, i0:i0 + m, :], s0[0:nr, p_slot(b, p), 0:m, :],
                                      pb[0:nr, 0:m * S].rearrange("p (q s) -> p q s", q=m),
                                      ALU.mult).then_inc(done[kind], 1)
                elif kind == "wb":
                    b, p = key
                    after_pe(dve, kind, key)
                    after(dve, "u", (b, p))
                    i0, m = 2 * p, len(chunks_of(p))
                    nr = rows0(i0 + m - 1)
                    h = hid0[0:nr, b % 2, i0:i0 + m, :]
                    vec.tensor_tensor(h, h, pb[0:nr, 0:m * S].rearrange("p (q s) -> p q s", q=m),
                                      ALU.mult).then_inc(done[kind], 1)
                elif kind == "dn":
                    residual(kind, key[0], FFN, key[1], banks)
                elif kind == "xa":
                    b, c = key
                    after_pe(dve, kind, key)
                    if c == 0:
                        after(dve, "sel", (b, 1, RC1 // 2 - 1))
                        if b > 0:
                            after_pe(dve, "lora", (b - 1, 1, IC1 - 1))
                    for k in range(2):
                        ins = vec.tensor_tensor(xam[:, k, c, :, :], pb.rearrange("p (g s) -> p g s", g=2),
                                                selb[:, k, c:c + 1, :].broadcast_to((P, 2, S)), ALU.mult)
                    ins.then_inc(done[kind], 1)
                elif kind == "lora":
                    b, k, i = key
                    n = (2 * b + k) * IC1 + i
                    after_pe(dve, kind, key)
                    after(dve, "base", (b, i))
                    if n >= 2:
                        dve.wait_ge(h_ready, n - 1)
                    g = gu1[:, n % 2, :, :]
                    vec.tensor_tensor(g, pb.rearrange("p (g s) -> p g s", g=2), base[:, i, :, :],
                                      ALU.add).then_inc(done[kind], 1)
                    after(dve, kind, key)
                    dve.wait_ge(silu1, n + 1)
                    vec.tensor_tensor(hk[:, k, i, :], sl1[:, n % 2, :], g[:, 1, :], ALU.mult).then_inc(h_ready, 1)
                elif kind == "da":
                    b, k, q = key
                    n = (b * 2 + k) * (RC1 // 2) + q
                    after_pe(dve, kind, key)
                    if n >= 2:
                        dve.wait_ge(tprod_ready, n - 1)
                    vec.tensor_tensor(tk1[:, n % 2, :, :], pb.rearrange("p (g s) -> p g s", g=2),
                                      selb[:, k, 2 * q:2 * q + 2, :], ALU.mult).then_inc(done[kind], 1)

        @block.gpsimd
        def _(pool):
            link = chain(pool, pool_step)
            gp = nc.gpsimd
            gp.memset(mhalf[:, :], -0.5).then_inc(mhalf_ready, 1)
            pool.wait_ge(mhalf_ready, 1)

            def inverse_std(st):
                pool.wait_ge(stats_ready, st + 1)
                link(gp.tensor_scalar(ve[:, st % 8, :], mv[:, st % 8, :, 1], EPS, None, ALU.add))
                gp.tensor_tensor(rstd[:, st % 8, :], ve[:, st % 8, :], mhalf[:, :], ALU.pow).then_inc(rstd_ready, 1)

            for b in range(B):
                inverse_std(b)
            gp.memset(vpad[:, :, :, :, :], 0.0).then_inc(vpad_ready, 1)
            pool.wait_ge(vpad_ready, 1)
            for r in range(2 * TB):
                v = vpad[:, r // TB, r % TB, :, :]
                ones = bass.AP(v.tensor, v.offset + P // 2, [v.ap[0], [4 * P, NH // 4], [P + HD, 4], [1, HD]])
                ins = gp.memset(ones, 1.0)
            ins.then_inc(vpad_ready, 1)
            for kind, key, banks in jobs:
                if kind == "rope":
                    L, b, j = key
                    t = tok(L, b, j)
                    nh = NH + NKV[L]
                    pool.wait_ge(parts_ready, t + 1)
                    s = qs[:, t % 2, :, :, :]
                    q4 = s[:, 0:NH, :, :].rearrange("p h (a c) d -> p h a c d", c=2)
                    gp.tensor_copy(q4[:, :, 1:3, 0, :], q4[:, :, 0:1, 0, :].broadcast_to((P, NH, 2, HD)))
                    gp.tensor_copy(s[:, 0:NH, 3, :], s[:, 0:NH, 1, :])
                    k4 = s[:, NH:nh, :, :].rearrange("p h (a c) d -> p h a c d", c=2)
                    gp.tensor_copy(k4[:, :, 1:3, 1, :], k4[:, :, 0:1, 0, :].broadcast_to((P, nh - NH, 2, HD)))
                    gp.tensor_copy(s[:, NH:nh, 2, :], s[:, NH:nh, 1, :]).then_inc(stack_ready, 1)
                elif kind in ("op", "dn"):
                    L, b = key
                    st = step_of(L, int(kind == "dn"), b) + B
                    if st < 4 * B:
                        inverse_std(st)
                elif kind == "lora":
                    b, k, i = key
                    n = (2 * b + k) * IC1 + i
                    pool.wait_ge(h_ready, n + 1)
                    after(pool, "wk", (b,))
                    if k == 0:
                        if i == 0 and b > 0:
                            after_pe(pool, "dn", (1, b - 1))
                        gp.tensor_tensor(hw[:, i, :], hk[:, k, i, :], wkb[:, k, :], ALU.mult)
                    else:
                        link(gp.tensor_tensor(hm[:, i % 2, :], hk[:, k, i, :], wkb[:, k, :], ALU.mult))
                        gp.tensor_tensor(hw[:, i, :], hw[:, i, :], hm[:, i % 2, :], ALU.add).then_inc(hw_ready, 1)
                elif kind == "da":
                    b, k, q = key
                    n = (b * 2 + k) * (RC1 // 2) + q
                    after(pool, kind, key)
                    w = wkb[:, k:k + 1, :].broadcast_to((P, 2, S))
                    t2 = tk[:, 2 * q:2 * q + 2, :]
                    if k == 0:
                        gp.tensor_tensor(t2, tk1[:, n % 2, :, :], w, ALU.mult).then_inc(tprod_ready, 1)
                    else:
                        gp.tensor_tensor(tk1[:, n % 2, :, :], tk1[:, n % 2, :, :], w, ALU.mult).then_inc(tprod_ready, 1)
                        pool.wait_ge(tprod_ready, n + 1)
                        gp.tensor_tensor(t2, t2, tk1[:, n % 2, :, :], ALU.add).then_inc(tsum_ready, 1)


def constants():
    bf = np.dtype("bfloat16")
    c = {"identf": np.eye(P, dtype=np.float32), "identb": np.eye(P).astype(bf)}
    c["iota"] = np.broadcast_to(np.arange(E, dtype=np.float32), (P, E)).copy()
    pos = np.arange(S, dtype=np.float32)
    one, theta = np.float32(1.0), np.float32(10000.0)
    pairs = np.arange(HD // 2, dtype=np.float32)
    f0 = one / theta ** (np.float32(2.0) * pairs / np.float32(HD))
    f1 = one / theta ** (np.arange(0, HD, 2, dtype=np.float32) / np.float32(HD))
    rope = np.zeros((2, S, 2, HD), np.float32)
    for L, f in enumerate((f0, f1)):
        a = pos[:, None] * f[None, :]
        co, si = (np.cos(a), np.sin(a)) if L == 0 else (np.sin(a), np.cos(a))
        rope[L, :, 0] = np.concatenate([co, co], 1)
        rope[L, :, 1] = np.concatenate([-si, si], 1)
    c["rope"] = rope.reshape(2, TB, P, 2, HD).transpose(2, 0, 1, 3, 4)
    i = np.arange(P)
    tri = np.where(i[None, :] > i[:, None], NEG, 0.0)
    c["maskQ0"] = tri.astype(bf)
    c["maskQ1"] = np.concatenate([np.zeros((P, P)), tri], 1).astype(bf)
    c["maskT"] = np.concatenate([tri.T, np.zeros((P, P))], 1).astype(bf)
    m = np.zeros((3, NH, NH, P), np.float32)
    for h in range(NH):
        m[:, h, h] = -1.0
    c["msel"] = m.reshape(3 * NH, NH, P).astype(bf)
    row = np.arange(HC0 * P)
    e = np.minimum(row // I0, E)
    w = (e[None, :] == np.arange(E + 1)[:, None]).astype(np.float32)
    c["wsel0"] = np.tile(w, (3, 1)).reshape(3 * (E + 1), HC0, P).astype(bf)
    w = np.zeros((2 * E + 6, 2 * RC1 + 2, P), np.float32)
    for k in range(2):
        for q in range(RC1):
            for r in range(P):
                w[k * E + (q * P + r) // R1, k * RC1 + q, r] = LORA
        w[2 * E + k::2, 2 * RC1 + k] = 1.0
    c["wsel1"] = w.astype(bf)
    return c


def layouts(a):
    def kmajor(w):
        return w.reshape(w.shape[0] // P, P, *w.shape[1:]).transpose(1, 0, *range(2, w.ndim + 1))

    def halves(w):
        return w.reshape(-1, HD // 2, 2, D).transpose(0, 2, 1, 3).reshape(-1, D)

    o = {}
    o["x"] = a["L0_attn_x"].reshape(B * TB, P, D).transpose(1, 0, 2)
    o["cT"] = np.stack([kmajor(a[f"L{L}_c"].T) for L in range(2)], 1)
    for L in range(2):
        o[f"wmod{L}"] = kmajor(a[f"L{L}_wmod"])
    kv = a["L0_attn_kv_w"]
    half = kv.shape[0] // 2
    o["wqkv0"] = kmajor(np.concatenate([halves(a["L0_attn_q_w"]), halves(kv[:half]), kv[half:]], 0).T)
    o["wo0"] = kmajor(a["L0_attn_c_w"].T)
    o["wqkv1"] = kmajor(np.concatenate([a["L1_attn_Wq"], a["L1_attn_Wk"], a["L1_attn_Wv"]], 0).T)
    o["wo1"] = kmajor(a["L1_attn_Wo"].T)
    o["wr0"] = kmajor(np.concatenate([a["L0_ffn_router_weight"], a["L0_ffn_shared_gate_w"]], 0).T)
    o["wr1"] = kmajor(a["L1_ffn_conf_W"].T)
    o["bw"] = np.broadcast_to(np.stack([a["L1_ffn_conf_b"], a["L1_ffn_expert_wealth"]]), (P, 2, E))
    gu = a["L0_ffn_gate_up_proj"]
    g = np.concatenate([gu[:, :I0].reshape(-1, D), a["L0_ffn_sh_gate_w"]], 0)
    u = np.concatenate([gu[:, I0:].reshape(-1, D), a["L0_ffn_sh_up_w"]], 0)
    o["wgu0"] = kmajor(np.stack([g.T, u.T], 1))
    d = np.concatenate([a["L0_ffn_down_proj"].transpose(0, 2, 1).reshape(-1, D), a["L0_ffn_sh_down_w"].T], 0)
    d = np.concatenate([d, np.zeros((HC0 * P - H0, D), d.dtype)], 0)
    o["wd0"] = kmajor(d)
    o["wa1"] = kmajor(np.stack([a[f"L1_ffn_{n}_A"].transpose(1, 0, 2).reshape(D, -1) for n in ("gate", "up")], 1))
    o["wbase1"] = kmajor(np.stack([a["L1_ffn_base_gate"], a["L1_ffn_base_up"]], 1))
    o["wb1"] = kmajor(np.stack([a[f"L1_ffn_{n}_B"].reshape(-1, I1) for n in ("gate", "up")], 1))
    o["wda1"] = kmajor(a["L1_ffn_down_A"].transpose(1, 0, 2).reshape(I1, -1))
    o["wd1"] = kmajor(a["L1_ffn_base_down"])
    o["wdb1"] = kmajor(a["L1_ffn_down_B"].reshape(-1, D))
    return o


def kernel(**inputs):
    import concourse.bacc as bacc
    from concourse.bass_utils import run_bass_kernel_spmd

    nc = bacc.Bacc("TRN2", target_bir_lowering=False, num_devices=1)
    host = layouts({k: np.asarray(v) for k, v in inputs.items()})
    host.update(constants())
    arrays, dram = {}, {}
    for name, shape, dt in INPUTS:
        arr = np.ascontiguousarray(host[name])
        assert tuple(arr.shape) == tuple(shape), (name, arr.shape, shape)
        arrays["in_" + name] = arr
        dram[name] = nc.dram_tensor("in_" + name, list(shape), dt, kind="ExternalInput").ap()
    out = nc.dram_tensor("out_x", [B, S, D], F32, kind="ExternalOutput").ap()
    build(nc, dram, out)
    r = run_bass_kernel_spmd(nc, [arrays], core_ids=[0])
    return r.results[0]["out_x"]
```

```python
from contextlib import ExitStack

import numpy as np

import concourse.bass as bass
from concourse import mybir

F32, F32R, BF16, U32 = mybir.dt.float32, mybir.dt.float32r, mybir.dt.bfloat16, mybir.dt.uint32
ACT = mybir.ActivationFunctionType
ALU = mybir.AluOpType
AX = mybir.AxisListType.X

P = 128
B, S, D = 4, 256, 256
TB = S // P
DC = D // P
NH, HD = 16, 16
NKV = [4, 16]
QK = [(NH + n) * HD for n in NKV]
QKV = [(NH + 2 * n) * HD for n in NKV]
NPART = 6
E = 8
I0, ISH = 176, 704
H0 = E * I0 + ISH
HC0 = -(-H0 // P)
I1, R1 = 896, 64
IC1 = I1 // P
RC1 = E * R1 // P
NMX = NH // 4 + NH // 2
EPS = 1e-5
SCALE = HD ** -0.5
LORA = 16.0 / 64.0
NEG = -1e30
ATT, FFN = 0, 1
PARTS = [(0, 0), (0, 1), (1, 0)]


def rows0(i):
    return min(P, H0 - i * P)


def plan():
    jobs = []
    state = {"ring": list(range(8)), "at": 0}

    def job(kind, *key, n=1, banks=None):
        if banks is None:
            banks = []
            for _ in range(n):
                banks.append(state["ring"][state["at"] % len(state["ring"])])
                state["at"] += 1
        jobs.append((kind, key, banks))

    def ring(banks):
        state["ring"], state["at"] = banks, 0

    def norm(L, half, b):
        job("ln", L, half, b, banks=[])

    def values(L, b):
        for j in range(TB):
            job("v", L, b, j)

    def stack(L, b, j):
        for i in range(2):
            job("stq", L, b, j, i)
        for i in range(-(-NKV[L] // 8)):
            job("stk", L, b, j, i)

    def maxima(L, b, lo, hi):
        for i in range(lo, hi):
            if i < NH // 4:
                job("mx0", L, b, i)
            else:
                job("mx1", L, b, i - NH // 4)
        if hi == NMX:
            job("mp", L, b, banks=[])

    def beside(L, b, u, first):
        nk = -(-NKV[L] // 8)
        if b + 1 < B:
            steps = [[("stq", 0, 0)], [("stq", 0, 1)],
                     [("stk", 0, i) for i in range(nk)], [("stq", 1, 0)],
                     [("stq", 1, 1), 0], [("stk", 1, i) for i in range(nk)],
                     [1, 2], [3], [4, 5], [6], [7, 8], [9], [10, 11], [], ["mT"], []]
            for step in steps[2 * u + 1 - first]:
                if step == "mT":
                    job("mT", L, b + 1)
                elif isinstance(step, int):
                    maxima(L, b + 1, step, step + 1)
                else:
                    kind, j, i = step
                    job(kind, L, b + 1, j, i)
            if b > 0 and (u, first) == (0, False):
                values(L, b + 1)
        if b + 2 < B:
            if L == 0 and (u, first) == (0, True):
                job("st", b + 2, banks=[])
            if (u, first) == (2, True):
                norm(L, ATT, b + 2)
            if (u, first) == (4, False):
                job("xT", L, ATT, b + 2)
            if (u, first) in ((5, False), (7, True)):
                queries(L, b + 2, int(first))
        if L == 1 and b == 0 and first:
            if u in (1, 3):
                job("gb", L, u - 1)
                job("gb", L, u)
            if u == 7:
                values(L, 1)
        if b == B - 1 and first:
            for b2 in range(2 - L):
                if u == 1 + b2:
                    norm(L, FFN, b2)
                if u == 3 + b2:
                    job("xT", L, FFN, b2)
                if u == 5 + b2:
                    job("rt", L, b2)
            if L == 0 and u == 5:
                job("hs0", 0, banks=[])
            if L == 0 and u == 6:
                job("w0hi", 0, banks=[])
                job("w0lo", 0, banks=[])

    def attention(L):
        units = NH // 2
        for g in range(B * units + 1):
            b, u = g // units, g % units
            if b < B:
                job("T", L, b, u, banks=[u % 2, u % 2 + 1])
                beside(L, b, u, True)
            if g:
                b2, u2 = (g - 1) // units, (g - 1) % units
                job("pv", L, b2, u2, banks=[3 + u2 // 2 % 2])
            if b < B:
                if u == 1 and b > 0:
                    job("op", L, b - 1)
                beside(L, b, u, False)

    def queries(L, b, j, copies=True):
        job("qk", L, b, j)
        job("rope", L, b, j, banks=[])
        if copies:
            job("copies", L, b, j, banks=[])

    def before_attention(i):
        tiles = {4: (0, 0), 5: (0, 1), 13: (1, 0), 15: (1, 1)}
        if i - 1 in tiles:
            job("copies", 1, *tiles[i - 1], banks=[])
        if i in tiles:
            queries(1, *tiles[i], copies=False)
        if i in (2, 5):
            norm(1, ATT, i // 3)
        if i in (3, 8):
            job("xT", 1, ATT, i // 8)
        if i == 6:
            values(1, 0)
        if i in (7, 8):
            stack(1, 0, i - 7)
        if 8 <= i <= 13:
            maxima(1, 0, 2 * (i - 8), 2 * (i - 7))
        if i == 15:
            job("mT", 1, 0)

    job("st", 0, banks=[])
    norm(0, ATT, 0)
    job("mod", 0, 0)
    job("mt", 0, 0)
    job("st", 1, banks=[])
    norm(0, ATT, 1)
    job("xT", 0, ATT, 0)
    for j in range(TB):
        queries(0, 0, j)
    values(0, 0)
    job("mod", 0, 1)
    job("mod", 0, 2)
    job("xT", 0, ATT, 1)
    for j in range(TB):
        stack(0, 0, j)
        job("qk", 0, 1, j)
    job("mt", 0, 1)
    for i in range(3):
        maxima(0, 0, 4 * i, 4 * i + 4)
        job("mod", 1, i)
    values(0, 1)
    for half in range(2):
        job("mt", 1, half)
    for b in range(B):
        job("gb", 0, b)
    job("mT", 0, 0)
    for j in range(TB):
        for kind in ("rope", "copies"):
            job(kind, 0, 1, j, banks=[])
    for L in range(2):
        ring([5, 6, 7])
        attention(L)
        if L == 0:
            ring([0, 1, 2, 3, 4, 5])
            job("wT", L, 0)
            job("wT", L, 1)
            for h in range(B // 2):
                for i in range(HC0):
                    n = h * HC0 + i
                    if n + 1 < 2 * HC0:
                        job("w0hi", n + 1, banks=[])
                    job("g", h, i)
                    if n + 1 < 2 * HC0:
                        job("w0lo", n + 1, banks=[])
                    job("u", h, i)
                    job("wb", h, i)
                    if n in (HC0, HC0 + 1):
                        job("res", n - HC0, banks=[])
                    if n == 0:
                        job("op", L, B - 1)
                    if h == 0:
                        for b in (2, 3):
                            if i == 4 * b - 6:
                                norm(L, FFN, b)
                            if i == 4 * b - 4:
                                job("xT", L, FFN, b)
                            if i == 4 * b - 2:
                                job("rt", L, b)
                    if i > 1:
                        job("dn0", h, i - 2, banks=[6, 7])
                    if h == 0 and i == HC0 - 1:
                        job("hs0", 1, banks=[])
                    job("s0", n, banks=[])
                    if h == 1:
                        if i in (1, 2):
                            job("rs", i - 1, banks=[])
                        before_attention(i)
                job("dn0", h, HC0 - 2, banks=[6, 7])
                if h == 0:
                    job("wT", L, 2)
                    job("wT", L, 3)
                job("dn0", h, HC0 - 1, banks=[6, 7])
            for b in (2, 3):
                job("res", b, banks=[])
                job("rs", b, banks=[])
            job("rezero", banks=[])
        else:
            def inputs(b):
                for k in range(2):
                    for q in range(RC1 // 2):
                        job("sel", b, k, q)
                for c in range(RC1):
                    job("xa", b, c)
                job("wk", b)
                if b == 0:
                    job("op", L, B - 1)

            def item(n):
                return n // 2 // IC1, n // 2 % IC1, n % 2

            ring([5, 6, 7, 4])
            job("base", 0, 0)
            job("wT", L, 0)
            job("base", 0, 1)
            job("wbhi", 0, banks=[])
            job("wblo", 0, banks=[])
            inputs(0)
            for b in range(B):
                for i in range(IC1):
                    n = b * IC1 + i
                    for k in range(2):
                        split = "wb" if k == 0 else "wd"
                        at = n + 1 - k
                        if at < B * IC1:
                            job(split + "hi", at, banks=[])
                        job("lora", b, i, k)
                        if at < B * IC1:
                            job(split + "lo", at, banks=[])
                        if (i, k) != (0, 0):
                            job("hs", *item(2 * n + k - 1), banks=[])
                        job("hp", b, i, k, banks=[])
                    if i + 2 < IC1:
                        job("base", b, i + 2)
                    if i > 0:
                        job("da", b, i - 1, banks=[0, 1, 2, 3])
                    if b < B - 1:
                        if i == 0:
                            norm(L, FFN, b + 1)
                        if i == 2:
                            job("xT", L, FFN, b + 1)
                        if i == 3:
                            job("rt", L, b + 1)
                job("hs", b, IC1 - 1, 1, banks=[])
                if b < B - 1:
                    job("base", b + 1, 0)
                    job("wT", L, b + 1)
                job("da", b, IC1 - 1, banks=[0, 1, 2, 3])
                if b < B - 1:
                    job("base", b + 1, 1)
                    inputs(b + 1)
                job("dn", L, b)
    return jobs


INPUTS = [
    ("x", (P, B * TB, D), F32), ("cT", (P, 2, DC, B), F32), ("wmod0", (P, DC, 6 * D), F32), ("wmod1", (P, DC, 6 * D), F32),
    ("wqkv0", (P, DC, QKV[0]), F32), ("wo0", (P, DC, D), F32),
    ("wqkv1", (P, DC, QKV[1]), F32), ("wo1", (P, DC, D), F32),
    ("wr0", (P, DC, E + 1), F32), ("wr1", (P, DC, E), F32), ("bw", (P, 2, E), F32),
    ("wgu0", (P, DC, 2, H0), F32), ("wd0", (P, HC0, D), F32),
    ("wa1", (P, DC, 2, E * R1), F32), ("wbase1", (P, DC, 2, I1), F32),
    ("wb1", (P, RC1, 2, I1), F32), ("wda1", (P, IC1, E * R1), F32),
    ("wd1", (P, IC1, D), F32), ("wdb1", (P, RC1, D), F32),
    ("identf", (P, P), F32), ("rope", (P, 2, TB, 2, HD), F32),
    ("iota", (P, E), F32),
    ("identb", (P, P), BF16), ("maskT", (P, P), BF16), ("maskQ", (P, P), BF16),
    ("msel", (3 * NH, NH, P), BF16), ("wsel0", (3 * (E + 1), HC0, P), BF16),
    ("wsel1", (2 * E + 6, 2 * RC1 + 2, P), BF16),
]


def build(nc, dram, out):
    jobs = plan()
    order = {}
    nth = {}
    owner, before = {}, {}
    seen = {}
    finished = 0
    for n, (kind, key, banks) in enumerate(jobs):
        if not banks:
            continue
        finished += 1
        order[kind, key] = finished
        count_as = (kind, key)
        if kind == "pv":
            count_as = (kind, key[:2] + (key[2] // 2,))
        if kind in ("da", "dn0"):
            count_as = (kind, key[:1])
        if count_as not in nth:
            nth[count_as] = seen.get(kind, 0)
            seen[kind] = seen.get(kind, 0) + 1
        before[n] = {owner[k] for k in banks if k in owner and owner[k] != count_as}
        for k in banks:
            owner[k] = count_as

    with ExitStack() as ctx:
        def sb(name, shape, dt):
            return ctx.enter_context(nc.sbuf_tensor(name, shape, dt))

        def sem(name):
            return ctx.enter_context(nc.semaphore(name))

        x = sb("x_resid", [P, B * TB, D], F32)
        hT = sb("hT", [P, 2, DC, S], F32)
        xn = sb("xn", [P, 2, TB, D], F32)
        gate = sb("gate_bcast", [P, B, 2, D], F32)
        gate4 = sb("gate_rows", [B, 2, 2, D], F32)
        modT = sb("modT", [P, 2, 8, B], F32)
        scT = sb("silu_cT", [P, 2, DC, B], F32)
        stats = sb("stats", [P, TB, 6], F32)
        mv = sb("mean_var", [P, 8, TB, 2], F32)
        ve = sb("var_eps", [P, 8, TB], F32)
        rstd = sb("rstd", [P, 8, TB], F32)
        mhalf = sb("minus_half", [P, TB], F32)
        tmp = sb("resid_tmp", [P, TB, D], F32)
        small = {}
        for name in ("cT", "wr0", "wr1", "bw", "identf", "rope", "iota", "identb", "maskT", "maskQ", "wsel1"):
            shape, dt = next((s, d) for n, s, d in INPUTS if n == name)
            small[name] = sb("c_" + name, list(shape), dt)
        lg = sb("logits", [P, TB, E + 1], F32)
        bids = sb("bids", [P, TB, E], F32)
        top = sb("top", [P, TB, 8], F32)
        topi = sb("top_index", [P, TB, 8], U32)
        topf = sb("top_index_f", [P, TB, 8], F32)
        diff = sb("diff", [P, TB, 3], F32)
        sig = sb("sig", [P, TB, 3], F32)
        comb = sb("comb", [P, TB, E + 1], F32)
        comb2 = sb("comb2", [P, TB, E + 1], F32)
        wres = sb("w_rest", [P, TB, E + 1], F32)
        cp0 = sb("w_parts0", [P, 2, TB, 3, E + 1], BF16)
        cp1 = sb("w_parts1", [P, 2, TB, 2 * E + 6], BF16)
        wT = sb("w_partsT", [3 * (E + 1), 2, S], BF16)

        WB = DC * 2 * H0 + HC0 * D
        wreg = sb("expert_weights", [P, WB], F32)

        def carve(region, at, shape, dt=F32):
            n = int(np.prod(shape))
            words = n * (2 if dt == BF16 else 4) // 4
            v = region[:, at:at + words]
            if dt != F32:
                v = v.bitcast(dt)
            names = "abcde"[:len(shape)]
            if len(shape) > 1:
                v = v.rearrange(f"p ({' '.join(names)}) -> p {' '.join(names)}",
                                **dict(zip(names, shape)))
            return v, at + words

        wgu0, at = carve(wreg, 0, (DC, 2, H0))
        wd0, _ = carve(wreg, at, (HC0, D))
        wbase1, at = carve(wreg, 0, (DC, 2, I1))
        wa1, at = carve(wreg, at, (DC, 2, E * R1))
        wb1, at = carve(wreg, at, (RC1, 2, I1))
        assert at <= WB

        areg = sb("attention0_weights", [P, DC * (QKV[0] + D)], F32)
        small["wqkv0"], at = carve(areg, 0, (DC, QKV[0]))
        small["wo0"], _ = carve(areg, at, (DC, D))
        wdb1, _ = carve(areg, 0, (RC1, D))

        mx = sb("row_max", [P, 2, TB, NH], F32)
        mrest = sb("max_rest", [P, TB, NH], F32)
        mparts = sb("max_parts", [P, 2, TB, 3, NH], BF16)
        mT = sb("max_T", [3 * NH, 2, S], BF16)

        AR = 28736
        with nc.sbuf_tensor("arena", [P, AR], F32) as arena:
            pass
        with ExitStack() as first:
            def sb1(name, shape, dt):
                return first.enter_context(nc.sbuf_tensor(name, shape, dt))

            hTs = sb1("hT_split", [P, 2, DC, 2 * S], F32R)
            wgs = sb1("wgu_split", [P, 2, 2, DC, 2, P], F32R)
            sb1("odd_values", [P, TB * NH * P], F32)
            h0s = sb1("hidden0_split", [P, 2, 2, 2 * S], F32R)
            sb1("odd_queries", [P, NH * S // 2], F32)
            wd0s = sb1("wd0_split", [P, 2, 2, D], F32R)
        with ExitStack() as second:
            def sb2(name, shape, dt):
                return second.enter_context(nc.sbuf_tensor(name, shape, dt))

            xam = sb2("lora_in_split", [P, 2, 2, RC1, 2, S], F32R)
            wbs = sb2("wb_split", [P, 2, 2, RC1, 2, P], F32R)
            wds = sb2("wda_split", [P, 2, 2, E * R1], F32R)
            hks = sb2("hidden_split", [P, 2, 2, 2, S], F32R)
            AR1 = AR - 2 * (2 * RC1 * 2 * S + 2 * RC1 * 2 * P + 2 * E * R1 + 2 * 2 * S)
            arena1 = sb2("arena1", [P, AR1], F32)
        vpad, at = carve(arena, 0, (2, TB, NH, P))
        qk_at = at
        qT, at = carve(arena, at, (2, NH, S), BF16)
        kT, at = carve(arena, at, (2, NH, S), BF16)
        pr_at = at
        pr, at = carve(arena, at, (2, 3 * S))
        qs, at = carve(arena, at, (2, 2 * NH, NPART, HD), BF16)
        qkr, at = carve(arena, at, (2, 2 * NH, HD))
        rot, at = carve(arena, at, (2 * NH, HD))
        rot2, at = carve(arena, at, (2 * NH, HD))
        aT, at = carve(arena, at, (2, DC, S))
        rs, at = carve(arena, at, (S,))
        small["wqkv1"], at = carve(arena, at, (DC, QKV[1]))
        small["wo1"], at = carve(arena, at, (DC, D))
        for name in ("msel", "wsel0"):
            rows, *shape = next(s for n, s, _ in INPUTS if n == name)
            v, at = carve(arena, at, shape, BF16)
            small[name] = v[0:rows]
        assert at <= AR, at
        wmod, at = carve(wreg, 0, (2, DC, 6 * D))
        modr = [carve(wreg, at + w, (6 * D,))[0] for w in (0, 6 * D)]
        kt_at = qk_at + NH * S
        hid0, _ = carve(arena, kt_at + 2 * 2 * D, (2, 2 * S))
        s0, _ = carve(arena, pr_at, (2, 2 * S))
        base, at = carve(arena1, 0, (2, 2, S))
        hw, at = carve(arena1, at, (IC1, S))
        selb, at = carve(arena1, at, (2, RC1, S), BF16)
        wkb, at = carve(arena1, at, (2, S))
        sl1, at = carve(arena1, at, (2, S))
        wda1, at = carve(arena1, at, (IC1, E * R1))
        wd1, at = carve(arena1, at, (IC1, D))
        gu1, _ = carve(arena1, at, (2, 2, S))
        tk, at = carve(arena1, at, (RC1, S))
        xt, _ = carve(arena1, at, (2, 2, S))
        tk1, _ = carve(arena1, at, (RC1, S))
        uw, at = carve(arena1, at, (2, S))
        hk, at = carve(arena1, at, (2, S))
        assert at <= AR1, (at, AR1)

        pt = ctx.enter_context(nc.psum_tensor("psum", [P, 8, 512], F32))
        ptb = pt[:, :, :].bitcast(BF16)

        pe_jobs = sem("pe_jobs")
        done = {k: sem("done_" + k) for k in seen}
        pieces = [f"wmod{L}_{i}" for L in range(2) for i in range(3)] + [f"x_{b}" for b in range(B)]
        loaded = {n: sem("ld_" + n) for n in [n for n, _, _ in INPUTS] + pieces
                  if n not in ("x", "wmod0", "wmod1")}
        silu_ready = sem("silu_ready")
        gates_ready = sem("gates_ready")
        stats_ready, rstd_ready, xn_ready = sem("stats_ready"), sem("rstd_ready"), sem("xn_ready")
        vpad_ready, mhalf_ready = sem("vpad_ready"), sem("mhalf_ready")
        roped = sem("roped")
        parts_ready = sem("parts_ready")
        stack_ready = sem("stack_ready")
        max_ready = sem("max_parts_ready")
        diff_ready, sig_ready = sem("diff_ready"), sem("sig_ready")
        z_ready, conf_ready = sem("z_ready"), sem("conf_ready")
        wparts_ready = sem("wparts_ready")
        hthi_ready, htlo_ready = sem("hthi_ready"), sem("htlo_ready")
        w0hi_ready, w0lo_ready = sem("w0hi_ready"), sem("w0lo_ready")
        d0hi_ready, d0lo_ready = sem("d0hi_ready"), sem("d0lo_ready")
        h0hi_ready, h0lo_ready = sem("h0hi_ready"), sem("h0lo_ready")
        silu1 = sem("silu1_ready")
        uw_ready = sem("uw_ready")
        h_ready = sem("h_ready")
        hw_ready = sem("hw_ready")
        tsum_ready = sem("tsum_ready")
        xt_ready, xhi_ready, xlo1_ready = sem("xt_ready"), sem("xhi_ready"), sem("xlo1_ready")
        wbhi_ready, wblo_ready = sem("wbhi_ready"), sem("wblo_ready")
        wdhi_ready, wdlo_ready = sem("wdhi_ready"), sem("wdlo_ready")
        hhi_ready, hlo_ready = sem("hhi_ready"), sem("hlo_ready")
        out_ready, stored = sem("out_ready"), sem("stored")
        dve_step, act_step, pool_step = sem("dve_step"), sem("act_step"), sem("pool_step")

        def after_pe(eng, kind, key):
            eng.wait_ge(pe_jobs, order[kind, key])

        def after(eng, kind, key):
            eng.wait_ge(done[kind], nth[kind, key] + 1)

        def need(eng, *names):
            for n in names:
                eng.wait_ge(loaded[n], 16)

        def chain(eng, s):
            count = [0]

            def link(ins):
                count[0] += 1
                ins.then_inc(s, 1)
                eng.wait_ge(s, count[0])
            return link

        def step_of(L, half, b):
            return (2 * L + half) * B + b

        def tok(L, b, j):
            return (L * B + b) * TB + j

        def chunk(b, i):
            return b * IC1 + i

        def chunk_key(n):
            return n // IC1, n % IC1

        def slot(L, b):
            return (b + L) % 2

        def unit(L, b, u):
            return (L * B + b) * (NH // 2) + u

        def key0(n):
            return n // HC0, n % HC0

        block = ctx.enter_context(nc.Block())

        @block.sync
        def _(sp):
            def load(name, dst):
                sp.dma_start(dst, dram[name]).then_inc(loaded[name], 16)

            def load_small(name):
                t = small[name]
                load(name, t[tuple(slice(None) for _ in t.shape)])

            def load_wmod(L, i):
                columns = slice(i * 512, (i + 1) * 512)
                sp.dma_start(wmod[:, L, :, columns], dram[f"wmod{L}"][:, :, columns])\
                    .then_inc(loaded[f"wmod{L}_{i}"], 16)

            load_small("cT")
            for b in range(B):
                sp.dma_start(x[:, b * TB:(b + 1) * TB, :], dram["x"][:, b * TB:(b + 1) * TB, :])\
                    .then_inc(loaded[f"x_{b}"], 16)
                if b == 0:
                    load_wmod(0, 0)
                    load_small("identf")
                    load_small("wqkv0")
                if b == 1:
                    load_small("rope")
            for i in (1, 2):
                load_wmod(0, i)
            load_small("identb")
            for i in range(3):
                load_wmod(1, i)
            for name in ("maskQ", "msel", "maskT", "wo0", "wr0", "iota", "wsel0"):
                load_small(name)
            for name in ("wqkv1", "wo1", "wr1", "bw", "wsel1"):
                load_small(name)
            after_pe(sp, "mt", (1, 1))
            sp.wait_ge(gates_ready, 2)
            load("wgu0", wgu0)
            load("wd0", wd0)
            after_pe(sp, "dn0", (1, HC0 - 1))
            load("wdb1", wdb1)
            load("wbase1", wbase1)
            load("wa1", wa1)
            load("wb1", wb1)
            after(sp, "op", (1, B - 1))
            load("wda1", wda1)
            load("wd1", wd1)
            for b in range(B):
                sp.wait_ge(out_ready, b + 1)
                sp.dma_start(out.rearrange("b (j p) d -> p (b j) d", p=P)[:, b * TB:(b + 1) * TB, :],
                             x[:, b * TB:(b + 1) * TB, :]).then_inc(stored, 16)
            sp.wait_ge(stored, 16 * B)

        @block.tensor
        def _(pe):
            mm = nc.tensor.matmul
            for n, (kind, key, banks) in enumerate(jobs):
                if not banks:
                    continue
                for k, kk in sorted(before[n]):
                    pe.wait_ge(done[k], nth[k, kk] + 1)
                pb = pt[:, banks[0], :]
                if kind == "mod":
                    L, i = key
                    pe.wait_ge(silu_ready, L + 1)
                    need(pe, f"wmod{L}_{i}")
                    for c in range(DC):
                        last = mm(pb[0:B, :], scT[:, L, c, :], wmod[:, L, c, i * 512:(i + 1) * 512],
                                  start=c == 0, stop=c == DC - 1)
                elif kind == "mt":
                    L, half = key
                    need(pe, "identf")
                    after(pe, "mod", (L, 2 * half))
                    for q, col in enumerate(range(3 * D * half, 3 * D * half + 4 * P, P)):
                        last = nc.tensor.transpose(pb[:, q * B:(q + 1) * B], modr[L][0:B, col:col + P],
                                                   small["identf"][0:B, 0:B])
                elif kind == "gb":
                    L, b = key
                    need(pe, "identf")
                    pe.wait_ge(gates_ready, L + 1)
                    last = mm(pb, small["identf"][0:B, b:b + 1].broadcast_to((B, P)),
                              gate4[:, L, :, :].rearrange("p g d -> p (g d)"), start=True, stop=True)
                elif kind == "xT":
                    L, half, b = key
                    st = step_of(*key)
                    need(pe, "identf")
                    pe.wait_ge(xn_ready, st + 1)
                    for c in range(DC):
                        for j in range(TB):
                            last = nc.tensor.transpose(pb[:, c * S + j * P:c * S + (j + 1) * P],
                                                       xn[:, st % 2, j, c * P:(c + 1) * P],
                                                       small["identf"][:, :])
                elif kind in ("qk", "v"):
                    L, b, j = key
                    st = step_of(L, ATT, b)
                    after(pe, "xT", (L, ATT, b))
                    need(pe, f"wqkv{L}")
                    lo, hi = (0, QK[L]) if kind == "qk" else (QK[L], QKV[L])
                    for c in range(DC):
                        last = mm(pb[:, 0:hi - lo], hT[:, st % 2, c, j * P:(j + 1) * P],
                                  small[f"wqkv{L}"][:, c, lo:hi], start=c == 0, stop=c == DC - 1)
                elif kind in ("stq", "stk"):
                    L, b, j, i = key
                    need(pe, "identb")
                    pe.wait_ge(stack_ready, tok(L, b, j) + 1)
                    h0 = (NH if kind == "stk" else 0) + 8 * i
                    nh = min(8, NKV[L]) if kind == "stk" else 8
                    for h in range(nh):
                        last = nc.tensor.transpose(
                            ptb[0:NPART * HD, banks[0], h * P:(h + 1) * P],
                            qs[:, tok(L, b, j) % 2, h0 + h, :, :].rearrange("p s d -> p (s d)"),
                            small["identb"][:, :])
                elif kind in ("mx0", "mx1"):
                    L, b, i = key
                    j = 0 if kind == "mx0" else 1
                    if i == 0:
                        need(pe, "maskQ")
                        after(pe, "stq", (L, b, j, 1))
                        after(pe, "stk", (L, b, j, -(-NKV[L] // 8) - 1))
                    nk = P * (j + 1)
                    nh = 512 // nk
                    mm(pb.rearrange("p (h k) -> p h k", h=nh)[:, :, j * P:nk], small["identb"][:, :],
                       small["maskQ"][:, :].unsqueeze(1).broadcast_to((P, nh, P)),
                       start=True, stop=False, skip_group_check=True)
                    for q in range(nh):
                        h = i * nh + q
                        last = mm(pb[:, q * nk:(q + 1) * nk],
                                  qT[0:NPART * HD, slot(L, b), h, j * P:(j + 1) * P],
                                  kT[0:NPART * HD, slot(L, b), h * NKV[L] // NH, 0:nk],
                                  start=False, stop=q == nh - 1, skip_group_check=True)
                elif kind == "mT":
                    L, b = key
                    pe.wait_ge(max_ready, L * B + b + 1)
                    for j in range(TB):
                        last = nc.tensor.transpose(
                            ptb[0:3 * NH, banks[0], j * P:(j + 1) * P],
                            mparts[:, slot(L, b), j, :, :].rearrange("p s h -> p (s h)"), small["identb"][:, :])
                elif kind == "T":
                    L, b, u = key
                    if u == 0:
                        need(pe, "maskT", "msel")
                        after(pe, "mT", (L, b))
                    pb2 = pt[:, banks[1], :]
                    if u % 2 == 0:
                        places = (pb, S), (pb2[:, 0:S], P)
                    else:
                        places = (pb2, S), (pb[:, S:2 * S], P)
                    for kc, (bank, nq) in enumerate(places):
                        mm(bank[:, 0:2 * nq].rearrange("p (h k) -> p h k", h=2)[:, :, 0:P], small["identb"][:, :],
                           small["maskT"][:, :].unsqueeze(1).broadcast_to((P, 2, P)),
                           start=True, stop=False, skip_group_check=True)
                        for i in range(2):
                            h = 2 * u + i
                            o = bank[:, i * nq:(i + 1) * nq]
                            mm(o, kT[0:NPART * HD, slot(L, b), h * NKV[L] // NH, kc * P:(kc + 1) * P],
                               qT[0:NPART * HD, slot(L, b), h, S - nq:S], start=False, stop=False,
                               skip_group_check=True)
                            last = mm(o, small["msel"][:, h, :], mT[:, slot(L, b), S - nq:S],
                                      start=False, stop=i == 1, skip_group_check=True)
                elif kind == "pv":
                    L, b, u = key
                    after(pe, "T", (L, b, u))
                    if u == 0:
                        after(pe, "v", (L, b, TB - 1))
                        pe.wait_ge(vpad_ready, 2)
                    pu = unit(L, b, u) % 2
                    at0, at1 = (0, 2 * S) if u % 2 == 0 else (S, 0)
                    for i in range(2):
                        h = 2 * u + i
                        mm(pb[:, 0:S], vpad[:, slot(L, b), 0, h, :], pr[:, pu, at0 + i * S:at0 + (i + 1) * S],
                           start=u % 2 == 0 and i == 0, stop=False)
                        last = mm(pb[:, P:S], vpad[:, slot(L, b), 1, h, :],
                                  pr[:, pu, at1 + i * P:at1 + (i + 1) * P],
                                  start=False, stop=u % 2 == 1 and i == 1)
                elif kind == "op":
                    L, b = key
                    need(pe, f"wo{L}")
                    after(pe, "pv", (L, b, NH // 4 - 1))
                    for j in range(TB):
                        for c in range(DC):
                            last = mm(pb[:, j * D:(j + 1) * D], aT[:, slot(L, b), c, j * P:(j + 1) * P],
                                      small[f"wo{L}"][:, c, :], start=c == 0, stop=c == DC - 1)
                elif kind == "rt":
                    L, b = key
                    ne = E + 1 - L
                    need(pe, f"wr{L}")
                    after(pe, "xT", (L, FFN, b))
                    st = step_of(L, FFN, b)
                    for j in range(TB):
                        for c in range(DC):
                            last = mm(pb[:, j * ne:(j + 1) * ne], hT[:, st % 2, c, j * P:(j + 1) * P],
                                      small[f"wr{L}"][:, c, :], start=c == 0, stop=c == DC - 1)
                elif kind == "wT":
                    L, b = key
                    pe.wait_ge(wparts_ready, L * B + b + 1)
                    for j in range(TB):
                        if L == 0:
                            nr, src = 3 * (E + 1), cp0[:, b % 2, j, :, :].rearrange("p s e -> p (s e)")
                        else:
                            nr, src = 2 * E + 6, cp1[:, b % 2, j, :]
                        last = nc.tensor.transpose(ptb[0:nr, banks[0], j * P:(j + 1) * P], src,
                                                   small["identb"][:, :])
                elif kind in ("g", "u"):
                    h, i = key
                    n = h * HC0 + i
                    pe.wait_ge(w0lo_ready, n + 1)
                    pe.wait_ge(htlo_ready, h + 1)
                    terms = [(c, w, d) for c in range(DC) for w, d in PARTS]
                    for t, (c, w, d) in enumerate(terms):
                        last = mm(pb, wgs[:, n % 2, w, c, int(kind == "u"), :], hTs[:, d, c, :],
                                  start=t == 0, stop=t == len(terms) - 1)
                elif kind == "wb":
                    h, i = key
                    if i == 0:
                        need(pe, "wsel0")
                        after(pe, "wT", (0, 2 * h + 1))
                    last = mm(pb[0:rows0(i), :], small["wsel0"][:, i, 0:rows0(i)],
                              wT[0:3 * (E + 1), :, :].rearrange("p b s -> p (b s)"), start=True, stop=True)
                elif kind == "dn0":
                    h, i = key
                    n = h * HC0 + i
                    pe.wait_ge(d0lo_ready, n + 1)
                    pe.wait_ge(h0lo_ready, n + 1)
                    for t in range(2 * TB):
                        for a, (w, d) in enumerate(PARTS):
                            last = mm(pt[:, banks[t // TB], t % TB * D:(t % TB + 1) * D],
                                      h0s[0:rows0(i), n % 2, d, t * P:(t + 1) * P], wd0s[0:rows0(i), n % 2, w, :],
                                      start=i == 0 and t % TB == 0 and a == 0,
                                      stop=i == HC0 - 1 and t % TB == TB - 1 and a == len(PARTS) - 1,
                                      skip_group_check=True)
                elif kind == "dn":
                    L, b = key
                    need(pe, "wd1", "wdb1")
                    pe.wait_ge(hw_ready, (b + 1) * IC1)
                    for j in range(TB):
                        for i in range(IC1):
                            mm(pb[:, j * D:(j + 1) * D], hw[:, i, j * P:(j + 1) * P], wd1[:, i, :],
                               start=j == 0 and i == 0, stop=False, skip_group_check=True)
                    pe.wait_ge(tsum_ready, b + 1)
                    for j in range(TB):
                        for c in range(RC1):
                            last = mm(pb[:, j * D:(j + 1) * D], tk[:, c, j * P:(j + 1) * P], wdb1[:, c, :],
                                      start=False, stop=j == TB - 1 and c == RC1 - 1, skip_group_check=True)
                elif kind == "base":
                    b, i = key
                    st = step_of(1, FFN, b)
                    need(pe, "wbase1")
                    for g in range(2):
                        for c in range(DC):
                            last = mm(pb[:, g * S:(g + 1) * S], wbase1[:, c, g, i * P:(i + 1) * P],
                                      hT[:, st % 2, c, :], start=c == 0, stop=c == DC - 1)
                elif kind == "sel":
                    b, k, q = key
                    if k == 0 and q == 0:
                        need(pe, "wsel1")
                        after(pe, "wT", (1, b))
                    for i in range(2):
                        last = mm(pb[:, i * S:(i + 1) * S], small["wsel1"][:, k * RC1 + 2 * q + i, :],
                                  wT[0:2 * E + 6, b % 2, :], start=True, stop=True)
                elif kind == "wk":
                    b, = key
                    for k in range(2):
                        last = mm(pb[:, k * S:(k + 1) * S], small["wsel1"][:, 2 * RC1 + k, :],
                                  wT[0:2 * E + 6, b % 2, :], start=True, stop=True)
                elif kind == "xa":
                    b, c2 = key
                    st = step_of(1, FFN, b)
                    need(pe, "wa1")
                    for g in range(2):
                        for c in range(DC):
                            last = mm(pb[:, g * S:(g + 1) * S], wa1[:, c, g, c2 * P:(c2 + 1) * P],
                                      hT[:, st % 2, c, :], start=c == 0, stop=c == DC - 1)
                elif kind == "lora":
                    b, i, k = key
                    n = chunk(b, i)
                    after(pe, "xa", (b, RC1 - 1))
                    pe.wait_ge(xlo1_ready, (b + 1) * RC1)
                    pe.wait_ge(wblo_ready, n + 1)
                    for g in range(2):
                        terms = [(c, w, h) for c in range(RC1) for w, h in PARTS]
                        for t, (c, w, h) in enumerate(terms):
                            last = mm(pb[:, g * S:(g + 1) * S], wbs[:, n % 2, w, c, g, :],
                                      xam[:, k, h, c, g, :], start=t == 0, stop=t == len(terms) - 1)
                elif kind == "da":
                    b, i = key
                    n = chunk(b, i)
                    pe.wait_ge(hlo_ready, 2 * n + 2)
                    pe.wait_ge(wdlo_ready, n + 1)
                    for k in range(2):
                        for c in range(RC1):
                            bank = pt[:, banks[2 * k + c // 2], :]
                            for t, (w, h) in enumerate(PARTS):
                                last = mm(bank[:, c % 2 * S:(c % 2 + 1) * S], wds[:, n % 2, w, c * P:(c + 1) * P],
                                          hks[:, n % 2, k, h, :], start=i == 0 and c % 2 == 0 and t == 0,
                                          stop=i == IC1 - 1 and c % 2 == 1 and t == len(PARTS) - 1,
                                          skip_group_check=True)
                last.then_inc(pe_jobs, 1)

        @block.scalar
        def _(act):
            need(act, "cT")
            for L in range(2):
                nc.scalar.activation(scT[:, L, :, :], small["cT"][:, L, :, :], ACT.Silu).then_inc(silu_ready, 1)
            for kind, key, banks in jobs:
                pb = pt[:, banks[0], :] if banks else None

                def copy_out(dst, src, kind=kind, key=key):
                    nc.scalar.activation(dst, src, ACT.Copy).then_inc(done[kind], 1)

                if kind == "gb":
                    L, b = key
                    after_pe(act, kind, key)
                    if L == 1:
                        after(act, "dn0", (b // 2,))
                    copy_out(gate[:, b, :, :], pb.rearrange("p (g d) -> p g d", g=2))
                elif kind == "xT":
                    L, half, b = key
                    st = step_of(*key)
                    after(act, "mt", (L, half))
                    after_pe(act, kind, key)
                    if st >= 2:
                        L2, half2, b2 = (st - 2) // (2 * B), (st - 2) // B % 2, (st - 2) % B
                        if half2 == ATT:
                            after_pe(act, "v", (L2, b2, TB - 1))
                        elif L2 == 0:
                            after_pe(act, "rt", (0, b2))
                            act.wait_ge(htlo_ready, b2 // 2 + 1)
                        else:
                            after_pe(act, "base", (b2, IC1 - 1))
                    for c in range(DC):
                        ins = nc.scalar.activation(hT[:, st % 2, c, :], pb[:, c * S:(c + 1) * S], ACT.Identity,
                                                   bias=modT[:, L, 4 * half + c, b:b + 1],
                                                   scale=modT[:, L, 4 * half + 2 + c, b:b + 1])
                    ins.then_inc(done[kind], 1)
                elif kind == "qk":
                    L, b, j = key
                    t = tok(*key)
                    after_pe(act, kind, key)
                    if t >= 2:
                        act.wait_ge(roped, t - 1)
                    copy_out(qkr[:, t % 2, 0:NH + NKV[L], :],
                             pb[:, 0:QK[L]].rearrange("p (h d) -> p h d", d=HD))
                elif kind == "v":
                    L, b, j = key
                    after_pe(act, kind, key)
                    if j == 0 and b >= 2:
                        after_pe(act, "pv", (L, b - 2, NH // 2 - 1))
                    if L == 0 and b == 0:
                        act.wait_ge(vpad_ready, 2)
                    if L == 1 and b == 1:
                        act.wait_ge(vpad_ready, 4)
                    v = vpad[:, slot(L, b), j, :, :]
                    dst = bass.AP(v.tensor, v.offset, [v.ap[0], [4 * P, NH // 4], [P + HD, 4], [1, HD]])
                    src = pb[:, 0:NKV[L] * HD]
                    if NKV[L] == NH:
                        src = src.rearrange("p (g j d) -> p g j d", g=NH // 4, j=4)
                    else:
                        src = src.rearrange("p (g d) -> p g d", g=NH // 4).unsqueeze(2)\
                            .broadcast_to((P, NH // 4, 4, HD))
                    copy_out(dst, src)
                elif kind == "stq":
                    L, b, j, i = key
                    after_pe(act, kind, key)
                    if b >= 2 and j == 0 and i == 0:
                        after_pe(act, "T", (L, b - 2, NH // 2 - 1))
                    copy_out(qT[0:NPART * HD, slot(L, b), 8 * i:8 * i + 8, j * P:(j + 1) * P],
                             ptb[0:NPART * HD, banks[0], :].rearrange("p (h q) -> p h q", h=8))
                elif kind == "stk":
                    L, b, j, i = key
                    n = min(8, NKV[L])
                    after_pe(act, kind, key)
                    copy_out(kT[0:NPART * HD, slot(L, b), 8 * i:8 * i + n, j * P:(j + 1) * P],
                             ptb[0:NPART * HD, banks[0], 0:n * P].rearrange("p (h q) -> p h q", h=n))
                elif kind == "mT":
                    L, b = key
                    after_pe(act, kind, key)
                    if b >= 2:
                        after_pe(act, "T", (L, b - 2, NH // 2 - 1))
                    copy_out(mT[:, slot(L, b), :], ptb[0:3 * NH, banks[0], 0:S])
                elif kind == "T":
                    L, b, u = key
                    n = unit(L, b, u)
                    after_pe(act, kind, key)
                    if n >= 2:
                        q = n - 2
                        after_pe(act, "pv", (q // (NH // 2) // B, q // (NH // 2) % B, q % (NH // 2)))
                    src = pt[:, banks[0]:banks[0] + 2, :].rearrange("p b n -> p (b n)")
                    src = src[:, 0:3 * S] if u % 2 == 0 else src[:, S:4 * S]
                    nc.scalar.activation(pr[:, n % 2, :], src, ACT.Exp, scale=SCALE).then_inc(done[kind], 1)
                elif kind == "rt":
                    L, b = key
                    if L == 1:
                        act.wait_ge(z_ready, b + 1)
                        nc.scalar.activation(bids[:, :, :], lg[:, :, 0:E], ACT.Tanh, scale=0.5).then_inc(conf_ready, 1)
                    act.wait_ge(diff_ready, L * B + b + 1)
                    nc.scalar.activation(sig[:, :, :], diff[:, :, :], ACT.Tanh, scale=0.5).then_inc(sig_ready, 1)
                elif kind == "wT":
                    L, b = key
                    nr = 3 * (E + 1) if L == 0 else 2 * E + 6
                    after_pe(act, kind, key)
                    if b >= 2:
                        if L == 0:
                            after_pe(act, "wb", (0, HC0 - 1))
                        else:
                            after_pe(act, "wk", (b - 2,))
                    copy_out(wT[0:nr, b % 2, :], ptb[0:nr, banks[0], 0:S])
                elif kind == "hs0":
                    h, = key
                    if h == 0:
                        after_pe(act, "pv", (0, B - 2, NH // 2 - 1))
                    else:
                        after_pe(act, "u", (0, HC0 - 1))
                    for b in (2 * h, 2 * h + 1):
                        after(act, "xT", (0, FFN, b))
                        nc.scalar.activation(hTs[:, 0, :, b % 2 * S:(b % 2 + 1) * S], hT[:, b % 2, :, :],
                                             ACT.Copy).then_inc(hthi_ready, 1)
                elif kind == "w0hi":
                    n, = key
                    i = n % HC0
                    need(act, "wgu0")
                    if n >= 2:
                        after_pe(act, "u", key0(n - 2))
                    else:
                        after_pe(act, "pv", (0, B - 2, NH // 2 - 1))
                    nc.scalar.activation(wgs[:, n % 2, 0, :, :, 0:rows0(i)], wgu0[:, :, :, i * P:i * P + rows0(i)],
                                         ACT.Copy).then_inc(w0hi_ready, 1)
                elif kind == "g":
                    h, i = key
                    n = h * HC0 + i
                    after_pe(act, kind, key)
                    if n >= 2:
                        after(act, "u", key0(n - 2))
                    nc.scalar.activation(s0[0:rows0(i), n % 2, :], pb[0:rows0(i), :], ACT.Silu)\
                        .then_inc(done[kind], 1)
                elif kind == "s0":
                    n, = key
                    i = n % HC0
                    nr = rows0(i)
                    need(act, "wd0")
                    if n >= 2:
                        after_pe(act, "dn0", key0(n - 2))
                    else:
                        after_pe(act, "pv", (0, B - 1, NH // 2 - 1))
                    nc.scalar.activation(wd0s[0:nr, n % 2, 0, :], wd0[0:nr, i, :], ACT.Copy).then_inc(d0hi_ready, 1)
                    after(act, "wb", key0(n))
                    nc.scalar.activation(h0s[0:nr, n % 2, 0, :], hid0[0:nr, n % 2, :], ACT.Copy)\
                        .then_inc(h0hi_ready, 1)
                elif kind == "base":
                    b, i = key
                    n = chunk(b, i)
                    after_pe(act, kind, key)
                    if n >= 2:
                        after(act, "lora", (*chunk_key(n - 2), 1))
                    copy_out(base[:, n % 2, :, :], pb.rearrange("p (g s) -> p g s", g=2))
                elif kind == "sel":
                    b, k, q = key
                    after_pe(act, kind, key)
                    if b > 0:
                        after(act, "da", (b - 1,))
                    copy_out(selb[:, k, 2 * q:2 * q + 2, :], pb.rearrange("p (g s) -> p g s", g=2))
                elif kind == "wk":
                    b, = key
                    after_pe(act, kind, key)
                    if b > 0:
                        act.wait_ge(uw_ready, 2 * b * IC1)
                    copy_out(wkb[:, :, :], pb.rearrange("p (g s) -> p g s", g=2))
                elif kind == "xa":
                    b, c = key
                    if c == 0 and b > 0:
                        after_pe(act, "lora", (b - 1, IC1 - 1, 1))
                    for k in range(2):
                        act.wait_ge(xt_ready, 2 * (b * RC1 + c) + k + 1)
                        nc.scalar.activation(xam[:, k, 0, c, :, :], xt[:, k, :, :], ACT.Copy).then_inc(xhi_ready, 1)
                elif kind == "wbhi":
                    n, = key
                    need(act, "wb1")
                    if n >= 2:
                        after_pe(act, "lora", (*chunk_key(n - 2), 1))
                    else:
                        after_pe(act, "pv", (1, B - 1, NH // 2 - 1))
                    i = n % IC1
                    nc.scalar.activation(wbs[:, n % 2, 0, :, :, :], wb1[:, :, :, i * P:(i + 1) * P],
                                         ACT.Copy).then_inc(wbhi_ready, 1)
                elif kind == "wdhi":
                    n, = key
                    need(act, "wda1")
                    if n >= 2:
                        after_pe(act, "da", chunk_key(n - 2))
                    nc.scalar.activation(wds[:, n % 2, 0, :], wda1[:, n % IC1, :], ACT.Copy).then_inc(wdhi_ready, 1)
                elif kind == "lora":
                    b, i, k = key
                    m = 2 * chunk(b, i) + k
                    after(act, kind, key)
                    if m >= 2:
                        act.wait_ge(h_ready, m - 1)
                    nc.scalar.activation(sl1[:, m % 2, :], gu1[:, m % 2, 0, :], ACT.Silu).then_inc(silu1, 1)
                elif kind == "hs":
                    b, i, k = key
                    n = chunk(b, i)
                    act.wait_ge(h_ready, 2 * n + k + 1)
                    if n >= 2:
                        after_pe(act, "da", chunk_key(n - 2))
                    nc.scalar.activation(hks[:, n % 2, k, 0, :], hk[:, k, :], ACT.Copy).then_inc(hhi_ready, 1)

        @block.vector
        def _(dve):
            link = chain(dve, dve_step)
            vec = nc.vector

            def layer_stats(st):
                b = st % B
                if st:
                    dve.wait_ge(stats_ready, st)
                for j in range(TB):
                    ins = vec.bn_stats(stats[:, j, :], x[:, b * TB + j, :])
                link(ins)
                for j in range(TB):
                    ins = vec.bn_aggr(mv[:, st % 8, j, :], stats[:, j, :])
                ins.then_inc(stats_ready, 1)

            def residual(kind, L, half, b, bank, last=True):
                after(dve, "gb", (L, b))
                ins = vec.tensor_tensor(tmp[:, :, :], pt[:, bank, :].rearrange("p (j d) -> p j d", j=TB),
                                        gate[:, b, half, :].unsqueeze(1).broadcast_to((P, TB, D)), ALU.mult)
                if last:
                    ins.then_inc(done[kind], 1)
                    dve.wait_ge(done[kind], nth[kind, (b // 2,) if kind == "dn0" else (L, b)] + 1)
                else:
                    link(ins)
                xb = x[:, b * TB:(b + 1) * TB, :]
                ins = vec.tensor_tensor(xb, xb, tmp[:, :, :], ALU.add)
                if L == 1 and half == FFN:
                    ins.then_inc(out_ready, 1)
                    return
                link(ins)
                layer_stats(step_of(L, half, b) + B)

            def bf16_parts(src, rest, dst):
                link(vec.tensor_copy(dst(0), src))
                link(vec.tensor_tensor(rest, src, dst(0), ALU.subtract))
                link(vec.tensor_copy(dst(1), rest))
                return vec.tensor_tensor(dst(2), rest, dst(1), ALU.subtract)

            for kind, key, banks in jobs:
                pb = pt[:, banks[0], :] if banks else None
                if kind == "st":
                    need(dve, f"x_{key[0]}")
                    layer_stats(key[0])
                elif kind == "mod":
                    L, i = key
                    after_pe(dve, kind, key)
                    vec.tensor_copy(modr[L][0:B, i * 512:(i + 1) * 512], pb[0:B, :]).then_inc(done[kind], 1)
                elif kind == "mt":
                    L, half = key
                    after_pe(dve, kind, key)
                    m = modT[:, L, 4 * half:4 * half + 4, :]
                    link(vec.tensor_copy(m, pb[:, 0:4 * B].rearrange("p (q b) -> p q b", q=4)))
                    vec.tensor_scalar(m[:, 2:4, :], m[:, 2:4, :], 1.0, None, ALU.add).then_inc(done[kind], 1)
                    if half:
                        g = modr[L][0:B, :].rearrange("p (g k d) -> p g k d", g=2, k=3)[:, :, 2, :]
                        a, s = tmp[0:B, :, :], gate4[:, L, :, :]
                        link(vec.scalar_tensor_tensor(a, g, -1.0, g, ALU.mult, ALU.max))
                        vec.tensor_scalar(s, g, 0.0, 2.0, ALU.is_ge, ALU.mult)
                        link(vec.tensor_scalar(a, a, 0.25, None, ALU.max))
                        vec.scalar_tensor_tensor(s, s, -1.0, a, ALU.add, ALU.mult).then_inc(gates_ready, 1)
                elif kind == "ln":
                    L, half, b = key
                    st = step_of(*key)
                    dve.wait_ge(rstd_ready, st + 1)
                    if st >= 2:
                        q = st - 2
                        after_pe(dve, "xT", (q // (2 * B), q // B % 2, q % B))
                    for j in range(TB):
                        ins = vec.tensor_scalar(xn[:, st % 2, j, :], x[:, b * TB + j, :],
                                                mv[:, st % 8, j, 0:1], rstd[:, st % 8, j:j + 1],
                                                ALU.subtract, ALU.mult)
                    ins.then_inc(xn_ready, 1)
                elif kind == "rope":
                    L, b, j = key
                    t = tok(L, b, j)
                    nh = NH + NKV[L]
                    need(dve, "rope")
                    after(dve, "qk", key)
                    r = qkr[:, t % 2, 0:nh, :]
                    o, o2 = rot[:, 0:nh, :], rot2[:, 0:nh, :]
                    cs = small["rope"][:, L, j, 0, :].unsqueeze(1).broadcast_to((P, nh, HD))
                    sn = small["rope"][:, L, j, 1, :].unsqueeze(1).broadcast_to((P, nh, HD))
                    hh = HD // 2
                    if t:
                        dve.wait_ge(parts_ready, t)
                    vec.tensor_tensor(o, r, cs, ALU.mult)
                    vec.tensor_tensor(o2[:, :, 0:hh], r[:, :, hh:HD], sn[:, :, 0:hh], ALU.mult)
                    vec.tensor_tensor(o2[:, :, hh:HD], r[:, :, 0:hh], sn[:, :, hh:HD], ALU.mult).then_inc(roped, 1)
                    dve.wait_ge(roped, t + 1)
                    link(vec.tensor_tensor(o, o, o2, ALU.add))
                    if t >= 2:
                        q = t - 2
                        after_pe(dve, "stk", (q // (B * TB), q // TB % B, q % TB,
                                              -(-NKV[q // (B * TB)] // 8) - 1))
                    st_ = qs[:, t % 2, :, :, :]
                    link(vec.tensor_copy(st_[:, 0:nh, 0, :], o))
                    link(vec.tensor_tensor(o2, o, st_[:, 0:nh, 0, :], ALU.subtract))
                    link(vec.tensor_copy(st_[:, 0:nh, 1, :], o2))
                    vec.tensor_tensor(st_[:, 0:NH, 5, :], o2[:, 0:NH, :], st_[:, 0:NH, 1, :], ALU.subtract)
                    vec.tensor_tensor(st_[:, NH:nh, 4, :], o2[:, NH:nh, :], st_[:, NH:nh, 1, :],
                                      ALU.subtract).then_inc(parts_ready, 1)
                elif kind in ("mx0", "mx1"):
                    L, b, i = key
                    j = 0 if kind == "mx0" else 1
                    nh = 512 // (P * (j + 1))
                    after_pe(dve, kind, key)
                    vec.tensor_reduce(mx[:, slot(L, b), j, i * nh:(i + 1) * nh], pb.rearrange("p (h k) -> p h k", h=nh),
                                      AX, ALU.max).then_inc(done[kind], 1)
                elif kind == "mp":
                    L, b = key
                    after(dve, "mx1", (L, b, NH // 2 - 1))
                    if L or b:
                        dve.wait_ge(max_ready, L * B + b)
                    bf16_parts(mx[:, slot(L, b), :, :], mrest[:, :, :],
                               lambda s: mparts[:, slot(L, b), :, s, :]).then_inc(max_ready, 1)
                elif kind == "pv":
                    L, b, u = key
                    if u % 2 == 0:
                        continue
                    g = u // 2
                    after_pe(dve, kind, key)
                    if L or b or g:
                        dve.wait_ge(done[kind], nth[kind, (L, b, g)])
                    if b >= 2 and g == 0:
                        after_pe(dve, "op", (L, b - 2))
                    link(vec.reciprocal(rs[0:P // 2, :], pb[P // 2:P, 0:S]))
                    lo = P // 2 * (g % 2)
                    vec.tensor_tensor(aT[lo:lo + P // 2, slot(L, b), g // 2, :], pb[0:P // 2, 0:S],
                                      rs[0:P // 2, :], ALU.mult).then_inc(done[kind], 1)
                elif kind == "op":
                    after_pe(dve, kind, key)
                    residual(kind, key[0], ATT, key[1], banks[0])
                elif kind == "rt":
                    L, b = key
                    after_pe(dve, kind, key)
                    ne = E + 1 - L
                    if L or b:
                        dve.wait_ge(wparts_ready, L * B + b)
                    src = pb[:, 0:TB * ne].rearrange("p (j e) -> p j e", j=TB)
                    if L == 0:
                        vec.tensor_copy(lg[:, :, :], src).then_inc(done[kind], 1)
                        after(dve, kind, key)
                        vals = lg
                    else:
                        need(dve, "bw")
                        vec.tensor_tensor(lg[:, :, 0:E], src,
                                          small["bw"][:, 0:1, :].broadcast_to((P, TB, E)),
                                          ALU.add).then_inc(done[kind], 1)
                        after(dve, kind, key)
                        vec.tensor_copy(comb2[:, :, 0:E], lg[:, :, 0:E]).then_inc(z_ready, 1)
                        dve.wait_ge(conf_ready, b + 1)
                        link(vec.tensor_scalar(bids[:, :, :], bids[:, :, :], 0.5, 0.5, ALU.mult, ALU.add))
                        link(vec.tensor_tensor(bids[:, :, :], bids[:, :, :],
                                               small["bw"][:, 1:2, :].broadcast_to((P, TB, E)), ALU.mult))
                        vals = bids
                    for j in range(TB):
                        ins = vec.max(top[:, j, :], vals[:, j, 0:E])
                    link(ins)
                    for j in range(TB):
                        vec.max_index(topi[:, j, :], top[:, j, :], vals[:, j, 0:E])
                    if L == 0:
                        vec.tensor_copy(diff[:, :, 2:3], lg[:, :, E:E + 1])
                    else:
                        vec.tensor_copy(diff[:, :, 2:3], top[:, :, 0:1])
                    vec.tensor_tensor(diff[:, :, 1:2], top[:, :, 1:2], top[:, :, 0:1], ALU.subtract)
                    vec.tensor_tensor(diff[:, :, 0:1], top[:, :, 0:1], top[:, :, 1:2],
                                      ALU.subtract).then_inc(diff_ready, 1)
                    dve.wait_ge(diff_ready, L * B + b + 1)
                    link(vec.tensor_copy(topf[:, :, :], topi[:, :, :]))
                    need(dve, "iota")
                    dve.wait_ge(sig_ready, L * B + b + 1)
                    link(vec.tensor_scalar(sig[:, :, :], sig[:, :, :], 0.5, 0.5, ALU.mult, ALU.add))
                    if b >= 2:
                        after_pe(dve, "wT", (L, b - 2))
                    if L == 0:
                        for j in range(TB):
                            vec.tensor_scalar(comb[:, j, 0:E], small["iota"][:, :], topf[:, j, 0:1],
                                              sig[:, j, 0:1], ALU.is_equal, ALU.mult)
                            ins = vec.tensor_scalar(comb2[:, j, 0:E], small["iota"][:, :], topf[:, j, 1:2],
                                                    sig[:, j, 1:2], ALU.is_equal, ALU.mult)
                        link(ins)
                        vec.tensor_tensor(comb[:, :, 0:E], comb[:, :, 0:E], comb2[:, :, 0:E], ALU.add)
                        link(vec.tensor_copy(comb[:, :, E:E + 1], sig[:, :, 2:3]))
                        bf16_parts(comb[:, :, :], wres[:, :, :],
                                   lambda s: cp0[:, b % 2, :, s, :]).then_inc(wparts_ready, 1)
                    else:
                        for j in range(TB):
                            for k in range(2):
                                vec.tensor_scalar(cp1[:, b % 2, j, k * E:(k + 1) * E], small["iota"][:, :],
                                                  topf[:, j, k:k + 1], None, ALU.is_equal)
                        bf16_parts(sig[:, :, 0:2], wres[:, :, 0:2],
                                   lambda s: cp1[:, b % 2, :, 2 * E + 2 * s:2 * E + 2 * s + 2])\
                            .then_inc(wparts_ready, 1)
                elif kind == "hs0":
                    h, = key
                    for b in (2 * h, 2 * h + 1):
                        dve.wait_ge(hthi_ready, b + 1)
                        half = slice(b % 2 * S, (b % 2 + 1) * S)
                        ins = vec.tensor_tensor(hTs[:, 1, :, half], hT[:, b % 2, :, :],
                                                hTs[:, 0, :, half].bitcast(F32), ALU.subtract)
                    ins.then_inc(htlo_ready, 1)
                elif kind == "u":
                    h, i = key
                    n = h * HC0 + i
                    nr = rows0(i)
                    after(dve, "g", key)
                    after_pe(dve, kind, key)
                    if n >= 2:
                        dve.wait_ge(h0lo_ready, n - 1)
                    vec.tensor_tensor(hid0[0:nr, n % 2, :], s0[0:nr, n % 2, :], pb[0:nr, :],
                                      ALU.mult).then_inc(done[kind], 1)
                elif kind == "wb":
                    h, i = key
                    nr = rows0(i)
                    after_pe(dve, kind, key)
                    after(dve, "u", key)
                    hid = hid0[0:nr, (h * HC0 + i) % 2, :]
                    vec.tensor_tensor(hid, hid, pb[0:nr, :], ALU.mult).then_inc(done[kind], 1)
                elif kind == "s0":
                    n, = key
                    i = n % HC0
                    nr = rows0(i)
                    dve.wait_ge(h0hi_ready, n + 1)
                    after(dve, "wb", key0(n))
                    vec.tensor_tensor(h0s[0:nr, n % 2, 1, :], hid0[0:nr, n % 2, :],
                                      h0s[0:nr, n % 2, 0, :].bitcast(F32), ALU.subtract).then_inc(h0lo_ready, 1)
                elif kind == "dn":
                    after_pe(dve, kind, key)
                    residual(kind, key[0], FFN, key[1], banks[0])
                elif kind == "res":
                    b, = key
                    after_pe(dve, "dn0", (b // 2, HC0 - 1))
                    residual("dn0", 0, FFN, b, 6 + b % 2, last=b % 2 == 1)
                elif kind == "xa":
                    b, c = key
                    n = b * RC1 + c
                    after_pe(dve, kind, key)
                    if c == 0:
                        after(dve, "sel", (b, 1, RC1 // 2 - 1))
                        if b > 0:
                            dve.wait_ge(tsum_ready, b)
                    if n:
                        after(dve, kind, ((n - 1) // RC1, (n - 1) % RC1))
                    for k in range(2):
                        if n and k == 1:
                            dve.wait_ge(xlo1_ready, n)
                        ins = vec.tensor_tensor(xt[:, k, :, :], pb.rearrange("p (g s) -> p g s", g=2),
                                                selb[:, k, c:c + 1, :].broadcast_to((P, 2, S)), ALU.mult)
                        ins.then_inc(xt_ready, 1)
                    dve.wait_ge(xt_ready, 2 * n + 1)
                    dve.wait_ge(xhi_ready, 2 * n + 1)
                    vec.tensor_tensor(xam[:, 0, 1, c, :, :], xt[:, 0, :, :],
                                      xam[:, 0, 0, c, :, :].bitcast(F32), ALU.subtract).then_inc(done[kind], 1)
                elif kind == "wblo":
                    n, = key
                    i = n % IC1
                    dve.wait_ge(wbhi_ready, n + 1)
                    vec.tensor_tensor(wbs[:, n % 2, 1, :, :, :], wb1[:, :, :, i * P:(i + 1) * P],
                                      wbs[:, n % 2, 0, :, :, :].bitcast(F32), ALU.subtract).then_inc(wblo_ready, 1)
                elif kind == "wdlo":
                    n, = key
                    dve.wait_ge(wdhi_ready, n + 1)
                    vec.tensor_tensor(wds[:, n % 2, 1, :], wda1[:, n % IC1, :],
                                      wds[:, n % 2, 0, :].bitcast(F32), ALU.subtract).then_inc(wdlo_ready, 1)
                elif kind == "lora":
                    b, i, k = key
                    n = chunk(b, i)
                    m = 2 * n + k
                    after_pe(dve, kind, key)
                    after(dve, "base", (b, i))
                    if m >= 2:
                        dve.wait_ge(h_ready, m - 1)
                    if b > 0 and i == 0:
                        after_pe(dve, "dn", (1, b - 1))
                    vec.tensor_tensor(gu1[:, m % 2, :, :], pb.rearrange("p (g s) -> p g s", g=2),
                                      base[:, n % 2, :, :], ALU.add).then_inc(done[kind], 1)
                elif kind == "hp":
                    b, i, k = key
                    m = 2 * chunk(b, i) + k
                    dve.wait_ge(silu1, m + 1)
                    dve.wait_ge(uw_ready, m + 1)
                    if m >= 2:
                        dve.wait_ge(hw_ready, m // 2)
                        dve.wait_ge(hlo_ready, m - 1)
                    vec.tensor_tensor(hk[:, k, :], sl1[:, m % 2, :], uw[:, k, :], ALU.mult).then_inc(h_ready, 1)
                elif kind == "hs":
                    b, i, k = key
                    n = chunk(b, i)
                    dve.wait_ge(hhi_ready, 2 * n + k + 1)
                    vec.tensor_tensor(hks[:, n % 2, k, 1, :], hk[:, k, :], hks[:, n % 2, k, 0, :].bitcast(F32),
                                      ALU.subtract).then_inc(hlo_ready, 1)
                elif kind == "da" and key[1] == IC1 - 1:
                    b = key[0]
                    after_pe(dve, kind, key)
                    dve.wait_ge(hlo_ready, 2 * (b + 1) * IC1)
                    dve.wait_ge(hw_ready, (b + 1) * IC1)
                    half = RC1 // 2
                    for k, sums in enumerate((tk, tk1)):
                        for q in range(2):
                            ins = vec.tensor_tensor(sums[:, half * q:half * (q + 1), :],
                                                    pt[:, banks[2 * k + q], :].rearrange("p (g s) -> p g s", g=2),
                                                    selb[:, k, half * q:half * (q + 1), :], ALU.mult)
                    ins.then_inc(done[kind], 1)
                    dve.wait_ge(done[kind], b + 1)
                    vec.tensor_tensor(tk[:, :, :], tk[:, :, :], tk1[:, :, :], ALU.add).then_inc(tsum_ready, 1)

        @block.gpsimd
        def _(pool):
            link = chain(pool, pool_step)
            gp = nc.gpsimd
            gp.memset(mhalf[:, :], -0.5).then_inc(mhalf_ready, 1)
            pool.wait_ge(mhalf_ready, 1)

            def inverse_std(st):
                pool.wait_ge(stats_ready, st + 1)
                link(gp.tensor_scalar(ve[:, st % 8, :], mv[:, st % 8, :, 1], EPS, None, ALU.add))
                gp.tensor_tensor(rstd[:, st % 8, :], ve[:, st % 8, :], mhalf[:, :], ALU.pow).then_inc(rstd_ready, 1)

            inverse_std(0)
            def pad(slots, count):
                gp.memset(vpad[:, slots, :, :, :], 0.0).then_inc(vpad_ready, 1)
                pool.wait_ge(vpad_ready, count)
                for q in range(slots.start, slots.stop):
                    for r in range(TB):
                        v = vpad[:, q, r, :, :]
                        ones = bass.AP(v.tensor, v.offset + P // 2, [v.ap[0], [4 * P, NH // 4], [P + HD, 4], [1, HD]])
                        ins = gp.memset(ones, 1.0)
                ins.then_inc(vpad_ready, 1)

            pad(slice(0, 2), 1)
            for kind, key, banks in jobs:
                if kind == "copies":
                    L, b, j = key
                    t = tok(L, b, j)
                    nh = NH + NKV[L]
                    pool.wait_ge(parts_ready, t + 1)
                    s = qs[:, t % 2, :, :, :]
                    q4 = s[:, 0:NH, :, :].rearrange("p h (a c) d -> p h a c d", c=2)
                    gp.tensor_copy(q4[:, :, 1:3, 0, :], q4[:, :, 0:1, 0, :].broadcast_to((P, NH, 2, HD)))
                    gp.tensor_copy(s[:, 0:NH, 3, :], s[:, 0:NH, 1, :])
                    k4 = s[:, NH:nh, :, :].rearrange("p h (a c) d -> p h a c d", c=2)
                    gp.tensor_copy(k4[:, :, 1:3, 1, :], k4[:, :, 0:1, 0, :].broadcast_to((P, nh - NH, 2, HD)))
                    gp.tensor_copy(s[:, NH:nh, 2, :], s[:, NH:nh, 1, :]).then_inc(stack_ready, 1)
                elif kind == "rezero":
                    after_pe(pool, "dn0", (1, HC0 - 1))
                    pad(slice(0, 1), 3)
                elif kind == "st" and key[0]:
                    inverse_std(key[0])
                elif kind == "op":
                    inverse_std(step_of(*key[:1], ATT, key[1]) + B)
                elif kind == "rs":
                    inverse_std(step_of(0, FFN, key[0]) + B)
                elif kind == "w0lo":
                    n, = key
                    i = n % HC0
                    nr = rows0(i)
                    pool.wait_ge(w0hi_ready, n + 1)
                    gp.tensor_tensor(wgs[:, n % 2, 1, :, :, 0:nr], wgu0[:, :, :, i * P:i * P + nr],
                                     wgs[:, n % 2, 0, :, :, 0:nr].bitcast(F32), ALU.subtract)\
                      .then_inc(w0lo_ready, 1)
                elif kind == "s0":
                    n, = key
                    i = n % HC0
                    nr = rows0(i)
                    pool.wait_ge(d0hi_ready, n + 1)
                    gp.tensor_tensor(wd0s[0:nr, n % 2, 1, :], wd0[0:nr, i, :],
                                     wd0s[0:nr, n % 2, 0, :].bitcast(F32), ALU.subtract).then_inc(d0lo_ready, 1)
                elif kind == "lora":
                    b, i, k = key
                    m = 2 * chunk(b, i) + k
                    after(pool, kind, key)
                    after(pool, "wk", (b,))
                    if m >= 2:
                        pool.wait_ge(h_ready, m - 1)
                    gp.tensor_tensor(uw[:, k, :], gu1[:, m % 2, 1, :], wkb[:, k, :], ALU.mult).then_inc(uw_ready, 1)
                elif kind == "xa":
                    b, c = key
                    n = b * RC1 + c
                    pool.wait_ge(xhi_ready, 2 * n + 2)
                    gp.tensor_tensor(xam[:, 1, 1, c, :, :], xt[:, 1, :, :],
                                     xam[:, 1, 0, c, :, :].bitcast(F32), ALU.subtract).then_inc(xlo1_ready, 1)
                elif kind == "hp" and key[2] == 1:
                    b, i, _ = key
                    pool.wait_ge(h_ready, 2 * chunk(b, i) + 2)
                    if i == 0 and b > 0:
                        after_pe(pool, "dn", (1, b - 1))
                    gp.tensor_tensor(hw[:, i, :], hk[:, 0, :], hk[:, 1, :], ALU.add).then_inc(hw_ready, 1)


def constants():
    bf = np.dtype("bfloat16")
    c = {"identf": np.eye(P, dtype=np.float32), "identb": np.eye(P).astype(bf)}
    c["iota"] = np.broadcast_to(np.arange(E, dtype=np.float32), (P, E)).copy()
    pos = np.arange(S, dtype=np.float32)
    one, theta = np.float32(1.0), np.float32(10000.0)
    pairs = np.arange(HD // 2, dtype=np.float32)
    f0 = one / theta ** (np.float32(2.0) * pairs / np.float32(HD))
    f1 = one / theta ** (np.arange(0, HD, 2, dtype=np.float32) / np.float32(HD))
    rope = np.zeros((2, S, 2, HD), np.float32)
    for L, f in enumerate((f0, f1)):
        a = pos[:, None] * f[None, :]
        co, si = (np.cos(a), np.sin(a)) if L == 0 else (np.sin(a), np.cos(a))
        rope[L, :, 0] = np.concatenate([co, co], 1)
        rope[L, :, 1] = np.concatenate([-si, si], 1)
    c["rope"] = rope.reshape(2, TB, P, 2, HD).transpose(2, 0, 1, 3, 4)
    i = np.arange(P)
    tri = np.where(i[None, :] > i[:, None], NEG, 0.0)
    c["maskQ"] = tri.astype(bf)
    c["maskT"] = tri.T.astype(bf)
    m = np.zeros((3, NH, NH, P), np.float32)
    for h in range(NH):
        m[:, h, h] = -1.0
    c["msel"] = m.reshape(3 * NH, NH, P).astype(bf)
    row = np.arange(HC0 * P)
    e = np.minimum(row // I0, E)
    w = (e[None, :] == np.arange(E + 1)[:, None]).astype(np.float32)
    c["wsel0"] = np.tile(w, (3, 1)).reshape(3 * (E + 1), HC0, P).astype(bf)
    w = np.zeros((2 * E + 6, 2 * RC1 + 2, P), np.float32)
    for k in range(2):
        for q in range(RC1):
            for r in range(P):
                w[k * E + (q * P + r) // R1, k * RC1 + q, r] = LORA
        w[2 * E + k::2, 2 * RC1 + k] = 1.0
    c["wsel1"] = w.astype(bf)
    return c


def layouts(a):
    def kmajor(w):
        return w.reshape(w.shape[0] // P, P, *w.shape[1:]).transpose(1, 0, *range(2, w.ndim + 1))

    def halves(w):
        return w.reshape(-1, HD // 2, 2, D).transpose(0, 2, 1, 3).reshape(-1, D)

    o = {}
    o["x"] = a["L0_attn_x"].reshape(B * TB, P, D).transpose(1, 0, 2)
    o["cT"] = np.stack([kmajor(a[f"L{L}_c"].T) for L in range(2)], 1)
    for L in range(2):
        o[f"wmod{L}"] = kmajor(a[f"L{L}_wmod"])
    kv = a["L0_attn_kv_w"]
    half = kv.shape[0] // 2
    o["wqkv0"] = kmajor(np.concatenate([halves(a["L0_attn_q_w"]), halves(kv[:half]), kv[half:]], 0).T)
    o["wo0"] = kmajor(a["L0_attn_c_w"].T)
    o["wqkv1"] = kmajor(np.concatenate([a["L1_attn_Wq"], a["L1_attn_Wk"], a["L1_attn_Wv"]], 0).T)
    o["wo1"] = kmajor(a["L1_attn_Wo"].T)
    o["wr0"] = kmajor(np.concatenate([a["L0_ffn_router_weight"], a["L0_ffn_shared_gate_w"]], 0).T)
    o["wr1"] = kmajor(a["L1_ffn_conf_W"].T)
    o["bw"] = np.broadcast_to(np.stack([a["L1_ffn_conf_b"], a["L1_ffn_expert_wealth"]]), (P, 2, E))
    gu = a["L0_ffn_gate_up_proj"]
    g = np.concatenate([gu[:, :I0].reshape(-1, D), a["L0_ffn_sh_gate_w"]], 0)
    u = np.concatenate([gu[:, I0:].reshape(-1, D), a["L0_ffn_sh_up_w"]], 0)
    o["wgu0"] = kmajor(np.stack([g.T, u.T], 1))
    d = np.concatenate([a["L0_ffn_down_proj"].transpose(0, 2, 1).reshape(-1, D), a["L0_ffn_sh_down_w"].T], 0)
    d = np.concatenate([d, np.zeros((HC0 * P - H0, D), d.dtype)], 0)
    o["wd0"] = kmajor(d)
    o["wa1"] = kmajor(np.stack([a[f"L1_ffn_{n}_A"].transpose(1, 0, 2).reshape(D, -1) for n in ("gate", "up")], 1))
    o["wbase1"] = kmajor(np.stack([a["L1_ffn_base_gate"], a["L1_ffn_base_up"]], 1))
    o["wb1"] = kmajor(np.stack([a[f"L1_ffn_{n}_B"].reshape(-1, I1) for n in ("gate", "up")], 1))
    o["wda1"] = kmajor(a["L1_ffn_down_A"].transpose(1, 0, 2).reshape(I1, -1))
    o["wd1"] = kmajor(a["L1_ffn_base_down"])
    o["wdb1"] = kmajor(a["L1_ffn_down_B"].reshape(-1, D))
    return o


def kernel(**inputs):
    import concourse.bacc as bacc
    from concourse.bass_utils import run_bass_kernel_spmd

    nc = bacc.Bacc("TRN2", target_bir_lowering=False, num_devices=1)
    host = layouts({k: np.asarray(v) for k, v in inputs.items()})
    host.update(constants())
    arrays, dram = {}, {}
    for name, shape, dt in INPUTS:
        arr = np.ascontiguousarray(host[name])
        assert tuple(arr.shape) == tuple(shape), (name, arr.shape, shape)
        arrays["in_" + name] = arr
        dram[name] = nc.dram_tensor("in_" + name, list(shape), dt, kind="ExternalInput").ap()
    out = nc.dram_tensor("out_x", [B, S, D], F32, kind="ExternalOutput").ap()
    build(nc, dram, out)
    r = run_bass_kernel_spmd(nc, [arrays], core_ids=[0])
    return r.results[0]["out_x"]
```

```python
from contextlib import ExitStack

import numpy as np

import concourse.bass as bass
from concourse import mybir

F32, F32R, BF16, U32 = mybir.dt.float32, mybir.dt.float32r, mybir.dt.bfloat16, mybir.dt.uint32
ACT = mybir.ActivationFunctionType
ALU = mybir.AluOpType
AX = mybir.AxisListType.X

P = 128
B, S, D = 4, 256, 256
TB = S // P
DC = D // P
NH, HD = 16, 16
NKV = [4, 16]
QK = [(NH + n) * HD for n in NKV]
QKV = [(NH + 2 * n) * HD for n in NKV]
NPART = 6
E = 8
I0, ISH = 176, 704
H0 = E * I0 + ISH
HC0 = -(-H0 // P)
I1, R1 = 896, 64
IC1 = I1 // P
RC1 = E * R1 // P
NF1 = IC1 + RC1
NMX = NH // 4 + NH // 2
EPS = 1e-5
SCALE = HD ** -0.5
LORA = 16.0 / 64.0
NEG = -1e30
ATT, FFN = 0, 1
PARTS = [(0, 0), (0, 1), (1, 0)]


def rows0(i):
    return min(P, H0 - i * P)


def feature_step(kind, b, i):
    if kind == "xa":
        return b * NF1 + 2 + i
    return b * NF1 + i + (0 if i < 2 else RC1)


def plan():
    jobs = []
    state = {"ring": list(range(8)), "at": 0}

    def job(kind, *key, banks=None):
        if banks is None:
            banks = [state["ring"][state["at"] % len(state["ring"])]]
            state["at"] += 1
        jobs.append((kind, key, banks))

    def ring(banks):
        state["ring"], state["at"] = banks, 0

    def norm(L, half, b):
        job("ln", L, half, b, banks=[])

    def values(L, b):
        for j in range(TB):
            job("v", L, b, j)

    def stack(L, b, j):
        for i in range(2):
            job("stq", L, b, j, i)
        for i in range(-(-NKV[L] // 8)):
            job("stk", L, b, j, i)

    def maxima(L, b, lo, hi):
        for i in range(lo, hi):
            if i < NH // 4:
                job("mx0", L, b, i)
            else:
                job("mx1", L, b, i - NH // 4)
        if hi == NMX:
            job("mp", L, b, banks=[])

    def beside(L, b, u, first):
        nk = -(-NKV[L] // 8)
        if b + 1 < B:
            steps = [[("stq", 0, 0)], [("stq", 0, 1)],
                     [("stk", 0, i) for i in range(nk)], [("stq", 1, 0)],
                     [("stq", 1, 1), 0], [("stk", 1, i) for i in range(nk)],
                     [1, 2], [3], [4, 5], [6], [7, 8], [9], [10, 11], [], ["mT"], []]
            for step in steps[2 * u + 1 - first]:
                if step == "mT":
                    job("mT", L, b + 1)
                elif isinstance(step, int):
                    maxima(L, b + 1, step, step + 1)
                else:
                    kind, j, i = step
                    job(kind, L, b + 1, j, i)
            if b > 0 and (u, first) == (0, False):
                values(L, b + 1)
        if b + 2 < B:
            if L == 0 and (u, first) == (0, True):
                job("st", b + 2, banks=[])
            if (u, first) == (1, True):
                norm(L, ATT, b + 2)
            if (u, first) == (2, False):
                job("xT", L, ATT, b + 2)
            if (u, first) in ((3, True), (6, False)):
                queries(L, b + 2, u // 6)
        if L == 1 and b == 0 and first:
            if u in (1, 3):
                job("gb", L, u - 1)
                job("gb", L, u)
            if u == 7:
                values(L, 1)
        if b == B - 1 and first:
            for b2 in range(2 - L):
                if u == 1 + b2:
                    norm(L, FFN, b2)
                if u == 3 + b2:
                    job("xT", L, FFN, b2)
                if u == 5 + b2:
                    job("rt", L, b2)
            if L == 0 and u == 5:
                job("hs0", 0, banks=[])
            if L == 0 and u > 5:
                job("w0", u - 6, banks=[])
            if L == 1 and u == 5:
                job("hs1", 0, banks=[])
            if L == 1 and u > 5:
                job("bx", u - 6, banks=[])

    def attention(L):
        units = NH // 2
        for g in range(B * units + 1):
            b, u = g // units, g % units
            if b < B:
                job("T", L, b, u, banks=[u % 2, u % 2 + 1])
                beside(L, b, u, True)
            if g:
                b2, u2 = (g - 1) // units, (g - 1) % units
                job("pv", L, b2, u2, banks=[3 + u2 // 2 % 2])
            if b < B:
                if u == 1 and b > 0:
                    job("op", L, b - 1)
                beside(L, b, u, False)

    def queries(L, b, j, copies=True):
        job("qk", L, b, j)
        job("rope", L, b, j, banks=[])
        if copies:
            job("copies", L, b, j, banks=[])

    def before_attention(i):
        tiles = {4: (0, 0), 5: (0, 1), 13: (1, 0), 16: (1, 1)}
        if i - 1 in tiles:
            job("copies", 1, *tiles[i - 1], banks=[])
        if i in tiles:
            queries(1, *tiles[i], copies=False)
        if i in (2, 5):
            norm(1, ATT, i // 3)
        if i in (3, 8):
            job("xT", 1, ATT, i // 8)
        if i == 6:
            values(1, 0)
        if i in (7, 8):
            stack(1, 0, i - 7)
        if 8 <= i <= 13:
            maxima(1, 0, 2 * (i - 8), 2 * (i - 7))
        if i == 15:
            job("mT", 1, 0)

    job("st", 0, banks=[])
    norm(0, ATT, 0)
    job("mod", 0, 0)
    job("mt", 0, 0)
    job("st", 1, banks=[])
    norm(0, ATT, 1)
    job("xT", 0, ATT, 0)
    for j in range(TB):
        queries(0, 0, j)
    values(0, 0)
    job("mod", 0, 1)
    job("mod", 0, 2)
    job("xT", 0, ATT, 1)
    for j in range(TB):
        stack(0, 0, j)
        job("qk", 0, 1, j)
    job("mt", 0, 1)
    for i in range(3):
        maxima(0, 0, 4 * i, 4 * i + 4)
        job("mod", 1, i)
    values(0, 1)
    for half in range(2):
        job("mt", 1, half)
    for b in range(B):
        job("gb", 0, b)
    job("mT", 0, 0)
    for j in range(TB):
        for kind in ("rope", "copies"):
            job(kind, 0, 1, j, banks=[])
    for L in range(2):
        ring([5, 6, 7])
        attention(L)
        if L == 0:
            ring([0, 1, 2, 5, 6, 7])
            job("wT", L, 0)
            job("wT", L, 1)
            for h in range(B // 2):
                for i in range(HC0):
                    n = h * HC0 + i
                    job("g", h, i)
                    job("u", h, i)
                    if n + 2 < 2 * HC0:
                        job("w0", n + 2, banks=[])
                    job("wb", h, i)
                    if n == HC0:
                        for b in (0, 1):
                            job("res", b, banks=[])
                    if n == 0:
                        job("op", L, B - 1)
                    if h == 0:
                        for b in (2, 3):
                            if i == 4 * b - 6:
                                norm(L, FFN, b)
                            if i == 4 * b - 4:
                                job("xT", L, FFN, b)
                            if i == 4 * b - 2:
                                job("rt", L, b)
                    if i > 1:
                        job("dn0", h, i - 2, banks=[3, 4])
                    if h == 0 and i == HC0 - 1:
                        job("hs0", 1, banks=[])
                    job("s0", n, banks=[])
                    if h == 1:
                        if i in (0, 1):
                            job("rs", i, banks=[])
                        before_attention(i)
                job("dn0", h, HC0 - 2, banks=[3, 4])
                if h == 0:
                    job("wT", L, 2)
                    job("wT", L, 3)
                job("dn0", h, HC0 - 1, banks=[3, 4])
            job("copies", 1, 1, 1, banks=[])
            for b in (2, 3):
                job("res", b, banks=[])
            job("rezero", banks=[])
            for b in (2, 3):
                job("rs", b, banks=[])
        else:
            def features(kind, b, i):
                job(kind, b, i)
                if feature_step(kind, b, i) + 2 < B * NF1:
                    job("bx", feature_step(kind, b, i) + 2, banks=[])

            def inputs(b):
                for k in range(2):
                    for q in range(RC1 // 2):
                        job("sel", b, k, q)
                features("xa", b, 0)
                features("xa", b, 1)
                job("wk", b)
                if b > 0:
                    job("dn", L, b - 1, 0, banks=[7])
                features("xa", b, 2)
                features("xa", b, 3)
                if b == 0:
                    job("op", L, B - 1)
                if b > 0:
                    job("dn", L, b - 1, 1, banks=[7])

            ring([5, 6, 7, 4])
            features("base", 0, 0)
            job("wT", L, 0)
            features("base", 0, 1)
            job("wb1", 0, banks=[])
            inputs(0)
            for b in range(B):
                ring([6, 7])
                for i in range(IC1):
                    n = b * IC1 + i
                    if n + 1 < B * IC1:
                        job("wb1", n + 1, banks=[])
                    if n > 0:
                        job("wd", n, banks=[])
                    job("lora", b, i, banks=[4, 5])
                    for kind in ("add", "hp", "hs"):
                        for k in range(2):
                            job(kind, b, i, k, banks=[])
                    if n == 0:
                        job("wd", n, banks=[])
                    if i + 2 < IC1:
                        features("base", b, i + 2)
                    if i + 3 == IC1 and b < B - 1:
                        job("hs1", b + 1, banks=[])
                    if i > 0:
                        job("da", b, i - 1, banks=[0, 1, 2, 3])
                    if b < B - 1:
                        if i == 0:
                            norm(L, FFN, b + 1)
                        if i == 2:
                            job("xT", L, FFN, b + 1)
                        if i == 3:
                            job("rt", L, b + 1)
                ring([4, 5, 6])
                if b < B - 1:
                    features("base", b + 1, 0)
                    job("wT", L, b + 1)
                job("da", b, IC1 - 1, banks=[0, 1, 2, 3])
                if b < B - 1:
                    features("base", b + 1, 1)
                    inputs(b + 1)
                else:
                    for part in range(2):
                        job("dn", L, b, part, banks=[7])
    return jobs


INPUTS = [
    ("x", (P, B * TB, D), F32), ("cT", (P, 2, DC, B), F32), ("wmod0", (P, DC, 6 * D), F32), ("wmod1", (P, DC, 6 * D), F32),
    ("wqkv0", (P, DC, QKV[0]), F32), ("wo0", (P, DC, D), F32),
    ("wqkv1", (P, DC, QKV[1]), F32), ("wo1", (P, DC, D), F32),
    ("wr0", (P, DC, E + 1), F32), ("wr1", (P, DC, E), F32), ("bw", (P, 2, E), F32),
    ("wgu0", (P, DC, 2, H0), F32), ("wd0", (P, HC0, D), F32),
    ("wa1", (P, DC, 2, E * R1), F32), ("wbase1", (P, DC, 2, I1), F32),
    ("wb1", (P, RC1, 2, I1), F32), ("wda1", (P, IC1, E * R1), F32),
    ("wd1", (P, IC1, D), F32), ("wdb1", (P, RC1, D), F32),
    ("identf", (P, P), F32), ("rope", (P, 2, TB, 2, HD), F32),
    ("iota", (P, E), F32),
    ("identb", (P, P), BF16), ("maskT", (P, P), BF16), ("maskQ", (P, P), BF16),
    ("msel", (3 * NH, NH, P), BF16), ("wsel0", (3 * (E + 1), HC0, P), BF16),
    ("wsel1", (2 * E + 6, 2 * RC1 + 2, P), BF16),
]


def build(nc, dram, out):
    jobs = plan()
    order = {}
    nth = {}
    owner, before = {}, {}
    seen = {}
    finished = 0
    for n, (kind, key, banks) in enumerate(jobs):
        if not banks:
            continue
        finished += 1
        order[kind, key] = finished
        count_as = (kind, key)
        if kind == "pv":
            count_as = (kind, key[:2] + (key[2] // 2,))
        if kind in ("da", "dn0"):
            count_as = (kind, key[:1])
        if kind == "dn":
            count_as = (kind, key[:2])
        if count_as not in nth:
            nth[count_as] = seen.get(kind, 0)
            seen[kind] = seen.get(kind, 0) + 1
        before[n] = {owner[k] for k in banks if k in owner and owner[k] != count_as}
        for k in banks:
            owner[k] = count_as

    with ExitStack() as ctx:
        def sb(name, shape, dt):
            return ctx.enter_context(nc.sbuf_tensor(name, shape, dt))

        def sem(name):
            return ctx.enter_context(nc.semaphore(name))

        x = sb("x_resid", [P, B * TB, D], F32)
        hT = sb("hT", [P, 2, DC, S], F32)
        xn = sb("xn", [P, 2, TB, D], F32)
        gate = [None, sb("gate_bcast", [P, B, D], F32)]
        modT = sb("modT", [P, 2, 8, B], F32)
        scT = sb("silu_cT", [P, 2, DC, B], F32)
        stats = sb("stats", [P, TB, 6], F32)
        mv = sb("mean_var", [P, 8, TB, 2], F32)
        ve = sb("var_eps", [P, 8, TB], F32)
        rstd = sb("rstd", [P, 8, TB], F32)
        mhalf = sb("minus_half", [P, TB], F32)
        tmp = sb("resid_tmp", [P, TB, D], F32)
        small = {}
        for name in ("cT", "wr0", "wr1", "bw", "identf", "iota", "identb", "wsel1"):
            shape, dt = next((s, d) for n, s, d in INPUTS if n == name)
            small[name] = sb("c_" + name, list(shape), dt)
        lg = sb("logits", [P, TB, E + 1], F32)
        bids = sb("bids", [P, TB, E], F32)
        top = sb("top", [P, TB, 8], F32)
        topi = sb("top_index", [P, TB, 8], U32)
        topf = sb("top_index_f", [P, TB, 8], F32)
        diff = sb("diff", [P, TB, 3], F32)
        sig = sb("sig", [P, TB, 3], F32)
        comb = sb("comb", [P, TB, E + 1], F32)
        comb2 = sb("comb2", [P, TB, E + 1], F32)
        wres = sb("w_rest", [P, TB, E + 1], F32)
        cp0 = sb("w_parts0", [P, 2, TB, 3, E + 1], BF16)
        cp1 = sb("w_parts1", [P, 2, TB, 2 * E + 6], BF16)
        wT = sb("w_partsT", [3 * (E + 1), 2, S], BF16)

        WB = DC * 2 * H0 + HC0 * D
        wreg = sb("expert_weights", [P, WB], F32)

        def carve(region, at, shape, dt=F32):
            n = int(np.prod(shape))
            words = n * (2 if dt == BF16 else 4) // 4
            v = region[:, at:at + words]
            if dt != F32:
                v = v.bitcast(dt)
            names = "abcde"[:len(shape)]
            if len(shape) > 1:
                v = v.rearrange(f"p ({' '.join(names)}) -> p {' '.join(names)}",
                                **dict(zip(names, shape)))
            return v, at + words

        wgu0, at = carve(wreg, 0, (DC, 2, H0))
        wd0, _ = carve(wreg, at, (HC0, D))
        wbase1, at = carve(wreg, 0, (DC, 2, I1))
        wa1, at = carve(wreg, at, (DC, 2, E * R1))
        wb1, at = carve(wreg, at, (RC1, 2, I1))
        assert at <= WB

        areg = sb("attention0_weights", [P, DC * (QKV[0] + D)], F32)
        small["wqkv0"], at = carve(areg, 0, (DC, QKV[0]))
        small["wo0"], _ = carve(areg, at, (DC, D))
        wdb1, _ = carve(areg, 0, (RC1, D))

        AR = 31744
        with nc.sbuf_tensor("arena", [P, AR], F32) as arena:
            pass
        with ExitStack() as first:
            def sb1(name, shape, dt):
                return first.enter_context(nc.sbuf_tensor(name, shape, dt))

            hTs = sb1("hT_split", [P, 2, DC, 2 * S], F32R)
            wgs = sb1("wgu_split", [P, 2, 2, DC, 2, P], F32R)
            sb1("odd_values", [P, TB * NH * P], F32)
            h0s = sb1("hidden0_split", [P, 2, 2, 2 * S], F32R)
            sb1("odd_queries", [P, NH * S // 2], F32)
            wd0s = sb1("wd0_split", [P, 2, 2, D], F32R)
        with ExitStack() as second:
            def sb2(name, shape, dt):
                return second.enter_context(nc.sbuf_tensor(name, shape, dt))

            wds = sb2("wda_split", [P, 2, 2, E * R1], F32R)
            hks = sb2("hidden_split", [P, 2, 2, 2, S], F32R)
            hTs1 = sb2("hT1_split", [P, 2, DC, S], F32R)
            bxs = sb2("feature_weights_split", [P, 2, 2, DC, 2, P], F32R)
            xam = sb2("lora_in_split", [P, 2, RC1, 2, 2, S], F32R)
            wbs = sb2("wb_split", [P, 2, 2, RC1, 2, P], F32R)
            AR1 = AR - 2 * (E * R1 * 2 + 2 * 2 * S + DC * S + 2 * DC * 2 * P + 2 * RC1 * 2 * S + 2 * RC1 * 2 * P)
            arena1 = sb2("arena1", [P, AR1], F32)
        vpad, at = carve(arena, 0, (2, TB, NH, P))
        qk_at = at
        qT, at = carve(arena, at, (2, NH, S), BF16)
        kT, at = carve(arena, at, (2, NH, S), BF16)
        pr_at = at
        pr, at = carve(arena, at, (2, 3 * S))
        qs, at = carve(arena, at, (2, 2 * NH, NPART, HD), BF16)
        qkr, at = carve(arena, at, (2, 2 * NH, HD))
        rot, at = carve(arena, at, (2 * NH, HD))
        rot2, at = carve(arena, at, (2, 2 * NH, HD))
        aT, at = carve(arena, at, (2, DC, S))
        rs, at = carve(arena, at, (S,))
        small["wqkv1"], at = carve(arena, at, (DC, QKV[1]))
        for name in ("msel", "wsel0", "rope", "maskT", "maskQ"):
            (rows, *shape), dt = next((s, d) for n, s, d in INPUTS if n == name)
            v, at = carve(arena, at, shape, dt)
            small[name] = v[0:rows]
        mx, at = carve(arena, at, (2, TB, NH))
        mrest, at = carve(arena, at, (TB, NH))
        mparts, at = carve(arena, at, (2, TB, 3, NH), BF16)
        mT, at = carve(arena, at, (2, S), BF16)
        mT = mT[0:3 * NH]
        gate4, at = carve(arena, at, (2, 2, D))
        gate4 = gate4[0:B]
        small["wo1"], at = carve(arena, at, (DC, D))
        gate[0], at = carve(arena, at, (B, D))
        assert at <= AR, at
        wmod, at = carve(wreg, 0, (2, DC, 6 * D))
        modr = [carve(wreg, at + w, (6 * D,))[0] for w in (0, 6 * D)]
        kt_at = qk_at + NH * S
        hid0, _ = carve(arena, kt_at + 2 * 2 * D, (2, 2 * S))
        s0, _ = carve(arena, pr_at, (2, 2 * S))
        wda1, at = carve(arena1, 0, (IC1, E * R1))
        wd1, at = carve(arena1, at, (IC1, D))
        base, at = carve(arena1, at, (2, 2, S))
        selb, at = carve(arena1, at, (2, RC1, S), BF16)
        wkb, at = carve(arena1, at, (2, S))
        sl1, at = carve(arena1, at, (2, S))
        xt, _ = carve(arena1, at, (2, 2, S))
        tk1, _ = carve(arena1, at, (RC1, S))
        uw, at = carve(arena1, at, (2, S))
        hk, at = carve(arena1, at, (2, S))
        hw, at = carve(arena1, at, (IC1, S))
        gu1, _ = carve(arena1, at, (2, 2, S))
        tk, at = carve(arena1, at, (RC1, S))
        assert at <= AR1, (at, AR1)

        pt = ctx.enter_context(nc.psum_tensor("psum", [P, 8, 512], F32))
        ptb = pt[:, :, :].bitcast(BF16)

        pe_jobs = sem("pe_jobs")
        done = {k: sem("done_" + k) for k in seen}
        pieces = [f"wmod{L}_{i}" for L in range(2) for i in range(3)] + [f"x_{b}" for b in range(B)]
        loaded = {n: sem("ld_" + n) for n in [n for n, _, _ in INPUTS] + pieces
                  if n not in ("x", "wmod0", "wmod1")}
        silu_ready = sem("silu_ready")
        gates_ready = sem("gates_ready")
        stats_ready, rstd_ready, xn_ready = sem("stats_ready"), sem("rstd_ready"), sem("xn_ready")
        vpad_ready, mhalf_ready = sem("vpad_ready"), sem("mhalf_ready")
        roped = sem("roped")
        parts_ready = sem("parts_ready")
        stack_ready = sem("stack_ready")
        max_ready = sem("max_parts_ready")
        diff_ready, sig_ready = sem("diff_ready"), sem("sig_ready")
        z_ready, conf_ready = sem("z_ready"), sem("conf_ready")
        wparts_ready = sem("wparts_ready")
        hthi_ready, htlo_ready = sem("hthi_ready"), sem("htlo_ready")
        w0hi_ready, w0lo_ready = sem("w0hi_ready"), sem("w0lo_ready")
        d0hi_ready, d0lo_ready = sem("d0hi_ready"), sem("d0lo_ready")
        h0hi_ready, h0lo_ready = sem("h0hi_ready"), sem("h0lo_ready")
        silu1 = sem("silu1_ready")
        uw_ready = sem("uw_ready")
        h_ready = sem("h_ready")
        hw_ready = sem("hw_ready")
        tsum_ready = sem("tsum_ready")
        hthi1_ready, htlo1_ready = sem("hthi1_ready"), sem("htlo1_ready")
        bxhi_ready, bxlo_ready = sem("bxhi_ready"), sem("bxlo_ready")
        xt_ready, xhi_ready, xlo1_ready = sem("xt_ready"), sem("xhi_ready"), sem("xlo1_ready")
        wbhi_ready, wblo_ready = sem("wbhi_ready"), sem("wblo_ready")
        wdhi_ready, wdlo_ready = sem("wdhi_ready"), sem("wdlo_ready")
        hhi_ready, hlo_ready = sem("hhi_ready"), sem("hlo_ready")
        out_ready, stored = sem("out_ready"), sem("stored")
        dve_step, act_step, pool_step = sem("dve_step"), sem("act_step"), sem("pool_step")

        def after_pe(eng, kind, key):
            eng.wait_ge(pe_jobs, order[kind, key])

        def after(eng, kind, key):
            eng.wait_ge(done[kind], (nth[kind, key] + 1) * (2 if kind == "lora" else 1))

        def need(eng, *names):
            for n in names:
                eng.wait_ge(loaded[n], 16)

        def chain(eng, s):
            count = [0]

            def link(ins):
                count[0] += 1
                ins.then_inc(s, 1)
                eng.wait_ge(s, count[0])
            return link

        def step_of(L, half, b):
            return (2 * L + half) * B + b

        def tok(L, b, j):
            return (L * B + b) * TB + j

        def chunk(b, i):
            return b * IC1 + i

        feature_job = {feature_step(k, *key): (k, key) for k, key, _ in jobs if k in ("base", "xa")}

        def feature_weights(m):
            kind, (b, i) = feature_job[m]
            return (wbase1 if kind == "base" else wa1)[:, :, :, i * P:(i + 1) * P]

        def chunk_key(n):
            return n // IC1, n % IC1

        def slot(L, b):
            return (b + L) % 2

        def unit(L, b, u):
            return (L * B + b) * (NH // 2) + u

        def key0(n):
            return n // HC0, n % HC0

        block = ctx.enter_context(nc.Block())

        @block.sync
        def _(sp):
            def load(name, dst):
                sp.dma_start(dst, dram[name]).then_inc(loaded[name], 16)

            def load_small(name):
                t = small[name]
                load(name, t[tuple(slice(None) for _ in t.shape)])

            def load_wmod(L, i):
                columns = slice(i * 512, (i + 1) * 512)
                sp.dma_start(wmod[:, L, :, columns], dram[f"wmod{L}"][:, :, columns])\
                    .then_inc(loaded[f"wmod{L}_{i}"], 16)

            load_small("cT")
            for b in range(B):
                sp.dma_start(x[:, b * TB:(b + 1) * TB, :], dram["x"][:, b * TB:(b + 1) * TB, :])\
                    .then_inc(loaded[f"x_{b}"], 16)
                if b == 0:
                    load_wmod(0, 0)
                    load_small("identf")
                    load_small("wqkv0")
                if b == 1:
                    load_small("rope")
            for i in (1, 2):
                load_wmod(0, i)
            load_small("identb")
            for i in range(3):
                load_wmod(1, i)
            for name in ("maskQ", "msel", "maskT", "wo0", "wr0", "iota", "wsel0"):
                load_small(name)
            for name in ("wqkv1", "wo1", "wr1", "bw", "wsel1"):
                load_small(name)
            after_pe(sp, "mt", (1, 1))
            sp.wait_ge(gates_ready, 2)
            load("wgu0", wgu0)
            load("wd0", wd0)
            after_pe(sp, "dn0", (1, HC0 - 1))
            load("wdb1", wdb1)
            load("wbase1", wbase1)
            load("wa1", wa1)
            load("wb1", wb1)
            after(sp, "op", (1, B - 1))
            load("wda1", wda1)
            load("wd1", wd1)
            for b in range(B):
                sp.wait_ge(out_ready, b + 1)
                sp.dma_start(out.rearrange("b (j p) d -> p (b j) d", p=P)[:, b * TB:(b + 1) * TB, :],
                             x[:, b * TB:(b + 1) * TB, :]).then_inc(stored, 16)
            sp.wait_ge(stored, 16 * B)

        @block.tensor
        def _(pe):
            mm = nc.tensor.matmul
            for n, (kind, key, banks) in enumerate(jobs):
                if not banks:
                    continue
                for k, kk in sorted(before[n]):
                    after(pe, k, kk)
                pb = pt[:, banks[0], :]
                if kind == "mod":
                    L, i = key
                    pe.wait_ge(silu_ready, L + 1)
                    need(pe, f"wmod{L}_{i}")
                    for c in range(DC):
                        last = mm(pb[0:B, :], scT[:, L, c, :], wmod[:, L, c, i * 512:(i + 1) * 512],
                                  start=c == 0, stop=c == DC - 1)
                elif kind == "mt":
                    L, half = key
                    need(pe, "identf")
                    after(pe, "mod", (L, 2 * half))
                    for q, col in enumerate(range(3 * D * half, 3 * D * half + 4 * P, P)):
                        last = nc.tensor.transpose(pb[:, q * B:(q + 1) * B], modr[L][0:B, col:col + P],
                                                   small["identf"][0:B, 0:B])
                elif kind == "gb":
                    L, b = key
                    need(pe, "identf")
                    pe.wait_ge(gates_ready, L + 1)
                    last = mm(pb, small["identf"][0:B, b:b + 1].broadcast_to((B, P)),
                              gate4[:, L, :, :].rearrange("p g d -> p (g d)"), start=True, stop=True)
                elif kind == "xT":
                    L, half, b = key
                    st = step_of(*key)
                    need(pe, "identf")
                    pe.wait_ge(xn_ready, st + 1)
                    for c in range(DC):
                        for j in range(TB):
                            last = nc.tensor.transpose(pb[:, c * S + j * P:c * S + (j + 1) * P],
                                                       xn[:, st % 2, j, c * P:(c + 1) * P],
                                                       small["identf"][:, :])
                elif kind in ("qk", "v"):
                    L, b, j = key
                    st = step_of(L, ATT, b)
                    after(pe, "xT", (L, ATT, b))
                    need(pe, f"wqkv{L}")
                    lo, hi = (0, QK[L]) if kind == "qk" else (QK[L], QKV[L])
                    for c in range(DC):
                        last = mm(pb[:, 0:hi - lo], hT[:, st % 2, c, j * P:(j + 1) * P],
                                  small[f"wqkv{L}"][:, c, lo:hi], start=c == 0, stop=c == DC - 1)
                elif kind in ("stq", "stk"):
                    L, b, j, i = key
                    need(pe, "identb")
                    pe.wait_ge(stack_ready, tok(L, b, j) + 1)
                    h0 = (NH if kind == "stk" else 0) + 8 * i
                    nh = min(8, NKV[L]) if kind == "stk" else 8
                    for h in range(nh):
                        last = nc.tensor.transpose(
                            ptb[0:NPART * HD, banks[0], h * P:(h + 1) * P],
                            qs[:, tok(L, b, j) % 2, h0 + h, :, :].rearrange("p s d -> p (s d)"),
                            small["identb"][:, :])
                elif kind in ("mx0", "mx1"):
                    L, b, i = key
                    j = 0 if kind == "mx0" else 1
                    if i == 0:
                        need(pe, "maskQ")
                        after(pe, "stq", (L, b, j, 1))
                        after(pe, "stk", (L, b, j, -(-NKV[L] // 8) - 1))
                    nk = P * (j + 1)
                    nh = 512 // nk
                    mm(pb.rearrange("p (h k) -> p h k", h=nh)[:, :, j * P:nk], small["identb"][:, :],
                       small["maskQ"][:, :].unsqueeze(1).broadcast_to((P, nh, P)),
                       start=True, stop=False, skip_group_check=True)
                    for q in range(nh):
                        h = i * nh + q
                        last = mm(pb[:, q * nk:(q + 1) * nk],
                                  qT[0:NPART * HD, slot(L, b), h, j * P:(j + 1) * P],
                                  kT[0:NPART * HD, slot(L, b), h * NKV[L] // NH, 0:nk],
                                  start=False, stop=q == nh - 1, skip_group_check=True)
                elif kind == "mT":
                    L, b = key
                    pe.wait_ge(max_ready, L * B + b + 1)
                    for j in range(TB):
                        last = nc.tensor.transpose(
                            ptb[0:3 * NH, banks[0], j * P:(j + 1) * P],
                            mparts[:, slot(L, b), j, :, :].rearrange("p s h -> p (s h)"), small["identb"][:, :])
                elif kind == "T":
                    L, b, u = key
                    if u == 0:
                        need(pe, "maskT", "msel")
                        after(pe, "mT", (L, b))
                    pb2 = pt[:, banks[1], :]
                    if u % 2 == 0:
                        places = (pb, S), (pb2[:, 0:S], P)
                    else:
                        places = (pb2, S), (pb[:, S:2 * S], P)
                    for kc, (bank, nq) in enumerate(places):
                        mm(bank[:, 0:2 * nq].rearrange("p (h k) -> p h k", h=2)[:, :, 0:P], small["identb"][:, :],
                           small["maskT"][:, :].unsqueeze(1).broadcast_to((P, 2, P)),
                           start=True, stop=False, skip_group_check=True)
                        for i in range(2):
                            h = 2 * u + i
                            o = bank[:, i * nq:(i + 1) * nq]
                            mm(o, kT[0:NPART * HD, slot(L, b), h * NKV[L] // NH, kc * P:(kc + 1) * P],
                               qT[0:NPART * HD, slot(L, b), h, S - nq:S], start=False, stop=False,
                               skip_group_check=True)
                            last = mm(o, small["msel"][:, h, :], mT[:, slot(L, b), S - nq:S],
                                      start=False, stop=i == 1, skip_group_check=True)
                elif kind == "pv":
                    L, b, u = key
                    after(pe, "T", (L, b, u))
                    if u == 0:
                        after(pe, "v", (L, b, TB - 1))
                        pe.wait_ge(vpad_ready, 2)
                    pu = unit(L, b, u) % 2
                    at0, at1 = (0, 2 * S) if u % 2 == 0 else (S, 0)
                    for i in range(2):
                        h = 2 * u + i
                        mm(pb[:, 0:S], vpad[:, slot(L, b), 0, h, :], pr[:, pu, at0 + i * S:at0 + (i + 1) * S],
                           start=u % 2 == 0 and i == 0, stop=False)
                        last = mm(pb[:, P:S], vpad[:, slot(L, b), 1, h, :],
                                  pr[:, pu, at1 + i * P:at1 + (i + 1) * P],
                                  start=False, stop=u % 2 == 1 and i == 1)
                elif kind == "op":
                    L, b = key
                    need(pe, f"wo{L}")
                    after(pe, "pv", (L, b, NH // 4 - 1))
                    for j in range(TB):
                        for c in range(DC):
                            last = mm(pb[:, j * D:(j + 1) * D], aT[:, slot(L, b), c, j * P:(j + 1) * P],
                                      small[f"wo{L}"][:, c, :], start=c == 0, stop=c == DC - 1)
                elif kind == "rt":
                    L, b = key
                    ne = E + 1 - L
                    need(pe, f"wr{L}")
                    after(pe, "xT", (L, FFN, b))
                    st = step_of(L, FFN, b)
                    for j in range(TB):
                        for c in range(DC):
                            last = mm(pb[:, j * ne:(j + 1) * ne], hT[:, st % 2, c, j * P:(j + 1) * P],
                                      small[f"wr{L}"][:, c, :], start=c == 0, stop=c == DC - 1)
                elif kind == "wT":
                    L, b = key
                    pe.wait_ge(wparts_ready, L * B + b + 1)
                    for j in range(TB):
                        if L == 0:
                            nr, src = 3 * (E + 1), cp0[:, b % 2, j, :, :].rearrange("p s e -> p (s e)")
                        else:
                            nr, src = 2 * E + 6, cp1[:, b % 2, j, :]
                        last = nc.tensor.transpose(ptb[0:nr, banks[0], j * P:(j + 1) * P], src,
                                                   small["identb"][:, :])
                elif kind in ("g", "u"):
                    h, i = key
                    n = h * HC0 + i
                    pe.wait_ge(w0lo_ready, n + 1)
                    pe.wait_ge(htlo_ready, h + 1)
                    terms = [(c, w, d) for c in range(DC) for w, d in PARTS]
                    for t, (c, w, d) in enumerate(terms):
                        last = mm(pb, wgs[:, n % 2, w, c, int(kind == "u"), :], hTs[:, d, c, :],
                                  start=t == 0, stop=t == len(terms) - 1)
                elif kind == "wb":
                    h, i = key
                    if i == 0:
                        need(pe, "wsel0")
                        after(pe, "wT", (0, 2 * h + 1))
                    last = mm(pb[0:rows0(i), :], small["wsel0"][:, i, 0:rows0(i)],
                              wT[0:3 * (E + 1), :, :].rearrange("p b s -> p (b s)"), start=True, stop=True)
                elif kind == "dn0":
                    h, i = key
                    n = h * HC0 + i
                    pe.wait_ge(d0lo_ready, n + 1)
                    pe.wait_ge(h0lo_ready, n + 1)
                    for t in range(2 * TB):
                        for a, (w, d) in enumerate(PARTS):
                            last = mm(pt[:, banks[t // TB], t % TB * D:(t % TB + 1) * D],
                                      h0s[0:rows0(i), n % 2, d, t * P:(t + 1) * P], wd0s[0:rows0(i), n % 2, w, :],
                                      start=i == 0 and t % TB == 0 and a == 0,
                                      stop=i == HC0 - 1 and t % TB == TB - 1 and a == len(PARTS) - 1,
                                      skip_group_check=True)
                elif kind == "dn":
                    L, b, part = key
                    if part == 0:
                        need(pe, "wd1")
                        pe.wait_ge(hw_ready, (b + 1) * IC1)
                        data, weights, nt = hw, wd1, IC1
                    else:
                        need(pe, "wdb1")
                        pe.wait_ge(tsum_ready, b + 1)
                        data, weights, nt = tk, wdb1, RC1
                    for j in range(TB):
                        for c in range(nt):
                            last = mm(pb[:, j * D:(j + 1) * D], data[:, c, j * P:(j + 1) * P], weights[:, c, :],
                                      start=part == 0 and j == 0 and c == 0,
                                      stop=part == 1 and j == TB - 1 and c == nt - 1, skip_group_check=True)
                elif kind in ("base", "xa"):
                    b, i = key
                    m = feature_step(kind, b, i)
                    pe.wait_ge(htlo1_ready, b + 1)
                    pe.wait_ge(bxlo_ready, m + 1)
                    terms = [(c, w, d) for c in range(DC) for w, d in PARTS]
                    for g in range(2):
                        for t, (c, w, d) in enumerate(terms):
                            last = mm(pb[:, g * S:(g + 1) * S], bxs[:, m % 2, w, c, g, :], hTs1[:, d, c, :],
                                      start=t == 0, stop=t == len(terms) - 1)
                elif kind == "sel":
                    b, k, q = key
                    if k == 0 and q == 0:
                        need(pe, "wsel1")
                        after(pe, "wT", (1, b))
                    for i in range(2):
                        last = mm(pb[:, i * S:(i + 1) * S], small["wsel1"][:, k * RC1 + 2 * q + i, :],
                                  wT[0:2 * E + 6, b % 2, :], start=True, stop=True)
                elif kind == "wk":
                    b, = key
                    for k in range(2):
                        last = mm(pb[:, k * S:(k + 1) * S], small["wsel1"][:, 2 * RC1 + k, :],
                                  wT[0:2 * E + 6, b % 2, :], start=True, stop=True)
                elif kind == "lora":
                    b, i = key
                    n = chunk(b, i)
                    pe.wait_ge(wblo_ready, n + 1)
                    for c in range(RC1):
                        if i == 0:
                            after(pe, "xa", (b, c))
                            pe.wait_ge(xlo1_ready, b * RC1 + c + 1)
                        for g in range(2):
                            for t, (w, h) in enumerate(PARTS):
                                last = mm(pt[:, banks[g], :], wbs[:, n % 2, w, c, g, :],
                                          xam[:, h, c, g, :, :].rearrange("p k s -> p (k s)"),
                                          start=c == 0 and t == 0, stop=c == RC1 - 1 and t == len(PARTS) - 1)
                elif kind == "da":
                    b, i = key
                    n = chunk(b, i)
                    pe.wait_ge(hlo_ready, 2 * n + 2)
                    pe.wait_ge(wdlo_ready, n + 1)
                    for c in range(RC1):
                        for t, (w, h) in enumerate(PARTS):
                            last = mm(pt[:, banks[c], :], wds[:, n % 2, w, c * P:(c + 1) * P],
                                      hks[:, n % 2, h, :, :].rearrange("p k s -> p (k s)"),
                                      start=i == 0 and t == 0, stop=i == IC1 - 1 and t == len(PARTS) - 1)
                last.then_inc(pe_jobs, 1)

        @block.scalar
        def _(act):
            need(act, "cT")
            for L in range(2):
                nc.scalar.activation(scT[:, L, :, :], small["cT"][:, L, :, :], ACT.Silu).then_inc(silu_ready, 1)
            for kind, key, banks in jobs:
                pb = pt[:, banks[0], :] if banks else None

                def copy_out(dst, src, kind=kind, key=key):
                    nc.scalar.activation(dst, src, ACT.Copy).then_inc(done[kind], 1)

                if kind == "gb":
                    L, b = key
                    after_pe(act, kind, key)
                    if L == 1:
                        after(act, "dn0", (b // 2,))
                    for half in range(2):
                        ins = nc.scalar.activation(gate[half][:, b, :], pb[:, half * D:(half + 1) * D], ACT.Copy)
                    ins.then_inc(done[kind], 1)
                elif kind == "xT":
                    L, half, b = key
                    st = step_of(*key)
                    after(act, "mt", (L, half))
                    after_pe(act, kind, key)
                    if st >= 2:
                        L2, half2, b2 = (st - 2) // (2 * B), (st - 2) // B % 2, (st - 2) % B
                        if half2 == ATT:
                            after_pe(act, "v", (L2, b2, TB - 1))
                        elif L2 == 0:
                            after_pe(act, "rt", (0, b2))
                            act.wait_ge(htlo_ready, b2 // 2 + 1)
                        else:
                            after_pe(act, "rt", (1, b2))
                            act.wait_ge(htlo1_ready, b2 + 1)
                    for c in range(DC):
                        ins = nc.scalar.activation(hT[:, st % 2, c, :], pb[:, c * S:(c + 1) * S], ACT.Identity,
                                                   bias=modT[:, L, 4 * half + c, b:b + 1],
                                                   scale=modT[:, L, 4 * half + 2 + c, b:b + 1])
                    ins.then_inc(done[kind], 1)
                elif kind == "qk":
                    L, b, j = key
                    t = tok(*key)
                    after_pe(act, kind, key)
                    if t >= 2:
                        act.wait_ge(roped, t - 1)
                    copy_out(qkr[:, t % 2, 0:NH + NKV[L], :],
                             pb[:, 0:QK[L]].rearrange("p (h d) -> p h d", d=HD))
                elif kind == "v":
                    L, b, j = key
                    after_pe(act, kind, key)
                    if j == 0 and b >= 2:
                        after_pe(act, "pv", (L, b - 2, NH // 2 - 1))
                    if L == 0 and b == 0:
                        act.wait_ge(vpad_ready, 2)
                    if L == 1 and b == 1:
                        act.wait_ge(vpad_ready, 4)
                    v = vpad[:, slot(L, b), j, :, :]
                    dst = bass.AP(v.tensor, v.offset, [v.ap[0], [4 * P, NH // 4], [P + HD, 4], [1, HD]])
                    src = pb[:, 0:NKV[L] * HD]
                    if NKV[L] == NH:
                        src = src.rearrange("p (g j d) -> p g j d", g=NH // 4, j=4)
                    else:
                        src = src.rearrange("p (g d) -> p g d", g=NH // 4).unsqueeze(2)\
                            .broadcast_to((P, NH // 4, 4, HD))
                    copy_out(dst, src)
                elif kind == "stq":
                    L, b, j, i = key
                    after_pe(act, kind, key)
                    if b >= 2 and j == 0 and i == 0:
                        after_pe(act, "T", (L, b - 2, NH // 2 - 1))
                    copy_out(qT[0:NPART * HD, slot(L, b), 8 * i:8 * i + 8, j * P:(j + 1) * P],
                             ptb[0:NPART * HD, banks[0], :].rearrange("p (h q) -> p h q", h=8))
                elif kind == "stk":
                    L, b, j, i = key
                    n = min(8, NKV[L])
                    after_pe(act, kind, key)
                    copy_out(kT[0:NPART * HD, slot(L, b), 8 * i:8 * i + n, j * P:(j + 1) * P],
                             ptb[0:NPART * HD, banks[0], 0:n * P].rearrange("p (h q) -> p h q", h=n))
                elif kind == "mT":
                    L, b = key
                    after_pe(act, kind, key)
                    if b >= 2:
                        after_pe(act, "T", (L, b - 2, NH // 2 - 1))
                    copy_out(mT[:, slot(L, b), :], ptb[0:3 * NH, banks[0], 0:S])
                elif kind == "T":
                    L, b, u = key
                    n = unit(L, b, u)
                    after_pe(act, kind, key)
                    if n >= 2:
                        q = n - 2
                        after_pe(act, "pv", (q // (NH // 2) // B, q // (NH // 2) % B, q % (NH // 2)))
                    src = pt[:, banks[0]:banks[0] + 2, :].rearrange("p b n -> p (b n)")
                    src = src[:, 0:3 * S] if u % 2 == 0 else src[:, S:4 * S]
                    nc.scalar.activation(pr[:, n % 2, :], src, ACT.Exp, scale=SCALE).then_inc(done[kind], 1)
                elif kind == "rt":
                    L, b = key
                    if L == 1:
                        act.wait_ge(z_ready, b + 1)
                        nc.scalar.activation(bids[:, :, :], lg[:, :, 0:E], ACT.Tanh, scale=0.5).then_inc(conf_ready, 1)
                    act.wait_ge(diff_ready, L * B + b + 1)
                    nc.scalar.activation(sig[:, :, :], diff[:, :, :], ACT.Tanh, scale=0.5).then_inc(sig_ready, 1)
                elif kind == "wT":
                    L, b = key
                    nr = 3 * (E + 1) if L == 0 else 2 * E + 6
                    after_pe(act, kind, key)
                    if b >= 2:
                        if L == 0:
                            after_pe(act, "wb", (0, HC0 - 1))
                        else:
                            after_pe(act, "wk", (b - 2,))
                    copy_out(wT[0:nr, b % 2, :], ptb[0:nr, banks[0], 0:S])
                elif kind == "hs0":
                    h, = key
                    if h == 0:
                        after_pe(act, "pv", (0, B - 2, NH // 2 - 1))
                    else:
                        after_pe(act, "u", (0, HC0 - 1))
                    for b in (2 * h, 2 * h + 1):
                        after(act, "xT", (0, FFN, b))
                        nc.scalar.activation(hTs[:, 0, :, b % 2 * S:(b % 2 + 1) * S], hT[:, b % 2, :, :],
                                             ACT.Copy).then_inc(hthi_ready, 1)
                elif kind == "w0":
                    n, = key
                    i = n % HC0
                    need(act, "wgu0")
                    if n >= 2:
                        after_pe(act, "u", key0(n - 2))
                    else:
                        after_pe(act, "pv", (0, B - 2, NH // 2 - 1))
                    nc.scalar.activation(wgs[:, n % 2, 0, :, :, 0:rows0(i)], wgu0[:, :, :, i * P:i * P + rows0(i)],
                                         ACT.Copy).then_inc(w0hi_ready, 1)
                elif kind == "g":
                    h, i = key
                    n = h * HC0 + i
                    after_pe(act, kind, key)
                    if n >= 2:
                        after(act, "u", key0(n - 2))
                    nc.scalar.activation(s0[0:rows0(i), n % 2, :], pb[0:rows0(i), :], ACT.Silu)\
                        .then_inc(done[kind], 1)
                elif kind == "s0":
                    n, = key
                    i = n % HC0
                    nr = rows0(i)
                    need(act, "wd0")
                    if n >= 2:
                        after_pe(act, "dn0", key0(n - 2))
                    else:
                        after_pe(act, "pv", (0, B - 1, NH // 2 - 1))
                    nc.scalar.activation(wd0s[0:nr, n % 2, 0, :], wd0[0:nr, i, :], ACT.Copy).then_inc(d0hi_ready, 1)
                    after(act, "wb", key0(n))
                    nc.scalar.activation(h0s[0:nr, n % 2, 0, :], hid0[0:nr, n % 2, :], ACT.Copy)\
                        .then_inc(h0hi_ready, 1)
                elif kind == "base":
                    b, i = key
                    n = chunk(b, i)
                    after_pe(act, kind, key)
                    if n >= 2:
                        after(act, "lora", chunk_key(n - 2))
                    copy_out(base[:, n % 2, :, :], pb.rearrange("p (g s) -> p g s", g=2))
                elif kind == "sel":
                    b, k, q = key
                    after_pe(act, kind, key)
                    if b > 0:
                        after(act, "da", (b - 1,))
                    copy_out(selb[:, k, 2 * q:2 * q + 2, :], pb.rearrange("p (g s) -> p g s", g=2))
                elif kind == "wk":
                    b, = key
                    after_pe(act, kind, key)
                    if b > 0:
                        act.wait_ge(uw_ready, 2 * b * IC1)
                    copy_out(wkb[:, :, :], pb.rearrange("p (g s) -> p g s", g=2))
                elif kind == "xa":
                    b, c = key
                    if c == 0 and b > 0:
                        after_pe(act, "lora", (b - 1, IC1 - 1))
                    for k in (1, 0):
                        act.wait_ge(xt_ready, 2 * (b * RC1 + c) + 2 - k)
                        nc.scalar.activation(xam[:, 0, c, :, k, :], xt[:, k, :, :], ACT.Copy).then_inc(xhi_ready, 1)
                elif kind == "hs1":
                    b, = key
                    if b == 0:
                        after_pe(act, "pv", (1, B - 2, NH // 2 - 1))
                    else:
                        after_pe(act, "base", (b - 1, IC1 - 1))
                    after(act, "xT", (1, FFN, b))
                    nc.scalar.activation(hTs1[:, 0, :, :], hT[:, b % 2, :, :], ACT.Copy).then_inc(hthi1_ready, 1)
                elif kind == "bx":
                    m, = key
                    need(act, "wbase1", "wa1")
                    if m >= 2:
                        after_pe(act, *feature_job[m - 2])
                    nc.scalar.activation(bxs[:, m % 2, 0, :, :, :], feature_weights(m), ACT.Copy)\
                        .then_inc(bxhi_ready, 1)
                elif kind == "wb1":
                    n, = key
                    need(act, "wb1")
                    if n >= 2:
                        after_pe(act, "lora", chunk_key(n - 2))
                    else:
                        after_pe(act, "pv", (1, B - 1, NH // 2 - 1))
                    i = n % IC1
                    nc.scalar.activation(wbs[:, n % 2, 0, :, :, :], wb1[:, :, :, i * P:(i + 1) * P],
                                         ACT.Copy).then_inc(wbhi_ready, 1)
                elif kind == "wd":
                    n, = key
                    need(act, "wda1")
                    if n >= 2:
                        after_pe(act, "da", chunk_key(n - 2))
                    nc.scalar.activation(wds[:, n % 2, 0, :], wda1[:, n % IC1, :], ACT.Copy).then_inc(wdhi_ready, 1)
                elif kind == "add":
                    b, i, k = key
                    m = 2 * chunk(b, i) + k
                    act.wait_ge(done["lora"], m + 1)
                    if m >= 2:
                        act.wait_ge(h_ready, m - 1)
                    nc.scalar.activation(sl1[:, m % 2, :], gu1[:, m % 2, 0, :], ACT.Silu).then_inc(silu1, 1)
                elif kind == "hs":
                    b, i, k = key
                    n = chunk(b, i)
                    act.wait_ge(h_ready, 2 * n + k + 1)
                    if n >= 2:
                        after_pe(act, "da", chunk_key(n - 2))
                    nc.scalar.activation(hks[:, n % 2, 0, k, :], hk[:, k, :], ACT.Copy).then_inc(hhi_ready, 1)

        @block.vector
        def _(dve):
            link = chain(dve, dve_step)
            vec = nc.vector

            def layer_stats(st):
                b = st % B
                if st:
                    dve.wait_ge(stats_ready, st)
                for j in range(TB):
                    ins = vec.bn_stats(stats[:, j, :], x[:, b * TB + j, :])
                link(ins)
                for j in range(TB):
                    ins = vec.bn_aggr(mv[:, st % 8, j, :], stats[:, j, :])
                ins.then_inc(stats_ready, 1)

            def residual(kind, L, half, b, bank, last=True):
                after(dve, "gb", (L, b))
                ins = vec.tensor_tensor(tmp[:, :, :], pt[:, bank, :].rearrange("p (j d) -> p j d", j=TB),
                                        gate[half][:, b, :].unsqueeze(1).broadcast_to((P, TB, D)), ALU.mult)
                if last:
                    ins.then_inc(done[kind], 1)
                    dve.wait_ge(done[kind], nth[kind, (b // 2,) if kind == "dn0" else (L, b)] + 1)
                else:
                    link(ins)
                xb = x[:, b * TB:(b + 1) * TB, :]
                ins = vec.tensor_tensor(xb, xb, tmp[:, :, :], ALU.add)
                if L == 1 and half == FFN:
                    ins.then_inc(out_ready, 1)
                    return
                link(ins)
                if kind == "op":
                    layer_stats(step_of(L, half, b) + B)

            def bf16_parts(src, rest, dst):
                link(vec.tensor_copy(dst(0), src))
                link(vec.tensor_tensor(rest, src, dst(0), ALU.subtract))
                link(vec.tensor_copy(dst(1), rest))
                return vec.tensor_tensor(dst(2), rest, dst(1), ALU.subtract)

            for kind, key, banks in jobs:
                pb = pt[:, banks[0], :] if banks else None
                if kind == "st":
                    need(dve, f"x_{key[0]}")
                    layer_stats(key[0])
                elif kind == "mod":
                    L, i = key
                    after_pe(dve, kind, key)
                    vec.tensor_copy(modr[L][0:B, i * 512:(i + 1) * 512], pb[0:B, :]).then_inc(done[kind], 1)
                elif kind == "mt":
                    L, half = key
                    after_pe(dve, kind, key)
                    m = modT[:, L, 4 * half:4 * half + 4, :]
                    link(vec.tensor_copy(m, pb[:, 0:4 * B].rearrange("p (q b) -> p q b", q=4)))
                    vec.tensor_scalar(m[:, 2:4, :], m[:, 2:4, :], 1.0, None, ALU.add).then_inc(done[kind], 1)
                    if half:
                        g = modr[L][0:B, :].rearrange("p (g k d) -> p g k d", g=2, k=3)[:, :, 2, :]
                        a, s = tmp[0:B, :, :], gate4[:, L, :, :]
                        link(vec.scalar_tensor_tensor(a, g, -1.0, g, ALU.mult, ALU.max))
                        vec.tensor_scalar(s, g, 0.0, 2.0, ALU.is_ge, ALU.mult)
                        link(vec.tensor_scalar(a, a, 0.25, None, ALU.max))
                        vec.scalar_tensor_tensor(s, s, -1.0, a, ALU.add, ALU.mult).then_inc(gates_ready, 1)
                elif kind == "ln":
                    L, half, b = key
                    st = step_of(*key)
                    dve.wait_ge(rstd_ready, st + 1)
                    if st >= 2:
                        q = st - 2
                        after_pe(dve, "xT", (q // (2 * B), q // B % 2, q % B))
                    for j in range(TB):
                        ins = vec.tensor_scalar(xn[:, st % 2, j, :], x[:, b * TB + j, :],
                                                mv[:, st % 8, j, 0:1], rstd[:, st % 8, j:j + 1],
                                                ALU.subtract, ALU.mult)
                    ins.then_inc(xn_ready, 1)
                elif kind == "rope":
                    L, b, j = key
                    t = tok(L, b, j)
                    nh = NH + NKV[L]
                    need(dve, "rope")
                    after(dve, "qk", key)
                    r = qkr[:, t % 2, 0:nh, :]
                    o, o2 = rot[:, 0:nh, :], rot2[:, t % 2, 0:nh, :]
                    cs = small["rope"][:, L, j, 0, :].unsqueeze(1).broadcast_to((P, nh, HD))
                    sn = small["rope"][:, L, j, 1, :].unsqueeze(1).broadcast_to((P, nh, HD))
                    hh = HD // 2
                    if t:
                        dve.wait_ge(parts_ready, t)
                    if t >= 2:
                        dve.wait_ge(stack_ready, t - 1)
                    vec.tensor_tensor(o, r, cs, ALU.mult)
                    vec.tensor_tensor(o2[:, :, 0:hh], r[:, :, hh:HD], sn[:, :, 0:hh], ALU.mult)
                    vec.tensor_tensor(o2[:, :, hh:HD], r[:, :, 0:hh], sn[:, :, hh:HD], ALU.mult).then_inc(roped, 1)
                    dve.wait_ge(roped, t + 1)
                    link(vec.tensor_tensor(o, o, o2, ALU.add))
                    if t >= 2:
                        q = t - 2
                        after_pe(dve, "stk", (q // (B * TB), q // TB % B, q % TB,
                                              -(-NKV[q // (B * TB)] // 8) - 1))
                    st_ = qs[:, t % 2, :, :, :]
                    link(vec.tensor_copy(st_[:, 0:nh, 0, :], o))
                    link(vec.tensor_tensor(o2, o, st_[:, 0:nh, 0, :], ALU.subtract))
                    vec.tensor_copy(st_[:, 0:nh, 1, :], o2).then_inc(parts_ready, 1)
                elif kind in ("mx0", "mx1"):
                    L, b, i = key
                    j = 0 if kind == "mx0" else 1
                    nh = 512 // (P * (j + 1))
                    after_pe(dve, kind, key)
                    vec.tensor_reduce(mx[:, slot(L, b), j, i * nh:(i + 1) * nh], pb.rearrange("p (h k) -> p h k", h=nh),
                                      AX, ALU.max).then_inc(done[kind], 1)
                elif kind == "mp":
                    L, b = key
                    after(dve, "mx1", (L, b, NH // 2 - 1))
                    if L or b:
                        dve.wait_ge(max_ready, L * B + b)
                    bf16_parts(mx[:, slot(L, b), :, :], mrest[:, :, :],
                               lambda s: mparts[:, slot(L, b), :, s, :]).then_inc(max_ready, 1)
                elif kind == "pv":
                    L, b, u = key
                    if u % 2 == 0:
                        continue
                    g = u // 2
                    after_pe(dve, kind, key)
                    if L or b or g:
                        dve.wait_ge(done[kind], nth[kind, (L, b, g)])
                    if b >= 2 and g == 0:
                        after_pe(dve, "op", (L, b - 2))
                    link(vec.reciprocal(rs[0:P // 2, :], pb[P // 2:P, 0:S]))
                    lo = P // 2 * (g % 2)
                    vec.tensor_tensor(aT[lo:lo + P // 2, slot(L, b), g // 2, :], pb[0:P // 2, 0:S],
                                      rs[0:P // 2, :], ALU.mult).then_inc(done[kind], 1)
                elif kind == "op":
                    after_pe(dve, kind, key)
                    residual(kind, key[0], ATT, key[1], banks[0])
                elif kind == "rt":
                    L, b = key
                    after_pe(dve, kind, key)
                    ne = E + 1 - L
                    if L or b:
                        dve.wait_ge(wparts_ready, L * B + b)
                    src = pb[:, 0:TB * ne].rearrange("p (j e) -> p j e", j=TB)
                    if L == 0:
                        vec.tensor_copy(lg[:, :, :], src).then_inc(done[kind], 1)
                        after(dve, kind, key)
                        vals = lg
                    else:
                        need(dve, "bw")
                        vec.tensor_tensor(lg[:, :, 0:E], src,
                                          small["bw"][:, 0:1, :].broadcast_to((P, TB, E)),
                                          ALU.add).then_inc(done[kind], 1)
                        after(dve, kind, key)
                        vec.tensor_copy(comb2[:, :, 0:E], lg[:, :, 0:E]).then_inc(z_ready, 1)
                        dve.wait_ge(conf_ready, b + 1)
                        link(vec.tensor_scalar(bids[:, :, :], bids[:, :, :], 0.5, 0.5, ALU.mult, ALU.add))
                        link(vec.tensor_tensor(bids[:, :, :], bids[:, :, :],
                                               small["bw"][:, 1:2, :].broadcast_to((P, TB, E)), ALU.mult))
                        vals = bids
                    for j in range(TB):
                        ins = vec.max(top[:, j, :], vals[:, j, 0:E])
                    link(ins)
                    for j in range(TB):
                        vec.max_index(topi[:, j, :], top[:, j, :], vals[:, j, 0:E])
                    if L == 0:
                        vec.tensor_copy(diff[:, :, 2:3], lg[:, :, E:E + 1])
                    else:
                        vec.tensor_copy(diff[:, :, 2:3], top[:, :, 0:1])
                    vec.tensor_tensor(diff[:, :, 1:2], top[:, :, 1:2], top[:, :, 0:1], ALU.subtract)
                    vec.tensor_tensor(diff[:, :, 0:1], top[:, :, 0:1], top[:, :, 1:2],
                                      ALU.subtract).then_inc(diff_ready, 1)
                    dve.wait_ge(diff_ready, L * B + b + 1)
                    link(vec.tensor_copy(topf[:, :, :], topi[:, :, :]))
                    need(dve, "iota")
                    dve.wait_ge(sig_ready, L * B + b + 1)
                    link(vec.tensor_scalar(sig[:, :, :], sig[:, :, :], 0.5, 0.5, ALU.mult, ALU.add))
                    if b >= 2:
                        after_pe(dve, "wT", (L, b - 2))
                    if L == 0:
                        for j in range(TB):
                            vec.tensor_scalar(comb[:, j, 0:E], small["iota"][:, :], topf[:, j, 0:1],
                                              sig[:, j, 0:1], ALU.is_equal, ALU.mult)
                            ins = vec.tensor_scalar(comb2[:, j, 0:E], small["iota"][:, :], topf[:, j, 1:2],
                                                    sig[:, j, 1:2], ALU.is_equal, ALU.mult)
                        link(ins)
                        vec.tensor_tensor(comb[:, :, 0:E], comb[:, :, 0:E], comb2[:, :, 0:E], ALU.add)
                        link(vec.tensor_copy(comb[:, :, E:E + 1], sig[:, :, 2:3]))
                        bf16_parts(comb[:, :, :], wres[:, :, :],
                                   lambda s: cp0[:, b % 2, :, s, :]).then_inc(wparts_ready, 1)
                    else:
                        for j in range(TB):
                            for k in range(2):
                                vec.tensor_scalar(cp1[:, b % 2, j, k * E:(k + 1) * E], small["iota"][:, :],
                                                  topf[:, j, k:k + 1], None, ALU.is_equal)
                        bf16_parts(sig[:, :, 0:2], wres[:, :, 0:2],
                                   lambda s: cp1[:, b % 2, :, 2 * E + 2 * s:2 * E + 2 * s + 2])\
                            .then_inc(wparts_ready, 1)
                elif kind == "hs0":
                    h, = key
                    for b in (2 * h, 2 * h + 1):
                        dve.wait_ge(hthi_ready, b + 1)
                        half = slice(b % 2 * S, (b % 2 + 1) * S)
                        ins = vec.tensor_tensor(hTs[:, 1, :, half], hT[:, b % 2, :, :],
                                                hTs[:, 0, :, half].bitcast(F32), ALU.subtract)
                    ins.then_inc(htlo_ready, 1)
                elif kind == "u":
                    h, i = key
                    n = h * HC0 + i
                    nr = rows0(i)
                    after(dve, "g", key)
                    after_pe(dve, kind, key)
                    if n >= 2:
                        dve.wait_ge(h0lo_ready, n - 1)
                    vec.tensor_tensor(hid0[0:nr, n % 2, :], s0[0:nr, n % 2, :], pb[0:nr, :],
                                      ALU.mult).then_inc(done[kind], 1)
                elif kind == "wb":
                    h, i = key
                    nr = rows0(i)
                    after_pe(dve, kind, key)
                    after(dve, "u", key)
                    hid = hid0[0:nr, (h * HC0 + i) % 2, :]
                    vec.tensor_tensor(hid, hid, pb[0:nr, :], ALU.mult).then_inc(done[kind], 1)
                elif kind == "s0":
                    n, = key
                    i = n % HC0
                    nr = rows0(i)
                    dve.wait_ge(h0hi_ready, n + 1)
                    after(dve, "wb", key0(n))
                    vec.tensor_tensor(h0s[0:nr, n % 2, 1, :], hid0[0:nr, n % 2, :],
                                      h0s[0:nr, n % 2, 0, :].bitcast(F32), ALU.subtract).then_inc(h0lo_ready, 1)
                elif kind == "dn" and key[2] == 1:
                    after_pe(dve, kind, key)
                    residual(kind, key[0], FFN, key[1], banks[0])
                elif kind == "rs":
                    layer_stats(step_of(0, FFN, key[0]) + B)
                elif kind == "res":
                    b, = key
                    after_pe(dve, "dn0", (b // 2, HC0 - 1))
                    residual("dn0", 0, FFN, b, 3 + b % 2, last=b % 2 == 1)
                elif kind == "xa":
                    b, c = key
                    n = b * RC1 + c
                    after_pe(dve, kind, key)
                    if c == 0:
                        after(dve, "sel", (b, 1, RC1 // 2 - 1))
                        if b > 0:
                            dve.wait_ge(tsum_ready, b)
                    if n:
                        after(dve, kind, ((n - 1) // RC1, (n - 1) % RC1))
                    for k in (1, 0):
                        if n and k == 1:
                            dve.wait_ge(xlo1_ready, n)
                        ins = vec.tensor_tensor(xt[:, k, :, :], pb.rearrange("p (g s) -> p g s", g=2),
                                                selb[:, k, c:c + 1, :].broadcast_to((P, 2, S)), ALU.mult)
                        ins.then_inc(xt_ready, 1)
                    dve.wait_ge(xt_ready, 2 * n + 2)
                    dve.wait_ge(xhi_ready, 2 * n + 2)
                    vec.tensor_tensor(xam[:, 1, c, :, 0, :], xt[:, 0, :, :],
                                      xam[:, 0, c, :, 0, :].bitcast(F32), ALU.subtract).then_inc(done[kind], 1)
                elif kind == "hs1":
                    b, = key
                    dve.wait_ge(hthi1_ready, b + 1)
                    vec.tensor_tensor(hTs1[:, 1, :, :], hT[:, b % 2, :, :], hTs1[:, 0, :, :].bitcast(F32),
                                      ALU.subtract).then_inc(htlo1_ready, 1)
                elif kind == "wb1":
                    n, = key
                    i = n % IC1
                    dve.wait_ge(wbhi_ready, n + 1)
                    vec.tensor_tensor(wbs[:, n % 2, 1, :, :, :], wb1[:, :, :, i * P:(i + 1) * P],
                                      wbs[:, n % 2, 0, :, :, :].bitcast(F32), ALU.subtract).then_inc(wblo_ready, 1)
                elif kind == "wd":
                    n, = key
                    dve.wait_ge(wdhi_ready, n + 1)
                    vec.tensor_tensor(wds[:, n % 2, 1, :], wda1[:, n % IC1, :],
                                      wds[:, n % 2, 0, :].bitcast(F32), ALU.subtract).then_inc(wdlo_ready, 1)
                elif kind == "add":
                    b, i, k = key
                    n = chunk(b, i)
                    m = 2 * n + k
                    after_pe(dve, "lora", (b, i))
                    after(dve, "base", (b, i))
                    if m >= 2:
                        dve.wait_ge(h_ready, m - 1)
                    if b > 0 and i == 0:
                        after_pe(dve, "dn", (1, b - 1, 1))
                    vec.tensor_tensor(gu1[:, m % 2, :, :], pt[:, 4:6, k * S:(k + 1) * S], base[:, n % 2, :, :],
                                      ALU.add).then_inc(done["lora"], 1)
                elif kind == "hp":
                    b, i, k = key
                    m = 2 * chunk(b, i) + k
                    dve.wait_ge(silu1, m + 1)
                    dve.wait_ge(uw_ready, m + 1)
                    if m >= 2:
                        dve.wait_ge(hw_ready, m // 2)
                        dve.wait_ge(hlo_ready, m - 1)
                    vec.tensor_tensor(hk[:, k, :], sl1[:, m % 2, :], uw[:, k, :], ALU.mult).then_inc(h_ready, 1)
                elif kind == "hs":
                    b, i, k = key
                    n = chunk(b, i)
                    dve.wait_ge(hhi_ready, 2 * n + k + 1)
                    vec.tensor_tensor(hks[:, n % 2, 1, k, :], hk[:, k, :], hks[:, n % 2, 0, k, :].bitcast(F32),
                                      ALU.subtract).then_inc(hlo_ready, 1)
                elif kind == "da" and key[1] == IC1 - 1:
                    b = key[0]
                    after_pe(dve, kind, key)
                    dve.wait_ge(hlo_ready, 2 * (b + 1) * IC1)
                    dve.wait_ge(hw_ready, (b + 1) * IC1)
                    half = RC1 // 2
                    for k, sums in enumerate((tk, tk1)):
                        for q in range(2):
                            part = slice(half * q, half * (q + 1))
                            ins = vec.tensor_tensor(sums[:, part, :], pt[:, part, k * S:(k + 1) * S],
                                                    selb[:, k, part, :], ALU.mult)
                    ins.then_inc(done[kind], 1)
                    dve.wait_ge(done[kind], b + 1)
                    vec.tensor_tensor(tk[:, :, :], tk[:, :, :], tk1[:, :, :], ALU.add).then_inc(tsum_ready, 1)

        @block.gpsimd
        def _(pool):
            link = chain(pool, pool_step)
            gp = nc.gpsimd
            gp.memset(mhalf[:, :], -0.5).then_inc(mhalf_ready, 1)
            pool.wait_ge(mhalf_ready, 1)

            def inverse_std(st):
                pool.wait_ge(stats_ready, st + 1)
                link(gp.tensor_scalar(ve[:, st % 8, :], mv[:, st % 8, :, 1], EPS, None, ALU.add))
                gp.tensor_tensor(rstd[:, st % 8, :], ve[:, st % 8, :], mhalf[:, :], ALU.pow).then_inc(rstd_ready, 1)

            inverse_std(0)
            def pad(slots, count):
                gp.memset(vpad[:, slots, :, :, :], 0.0).then_inc(vpad_ready, 1)
                pool.wait_ge(vpad_ready, count)
                for q in range(slots.start, slots.stop):
                    for r in range(TB):
                        v = vpad[:, q, r, :, :]
                        ones = bass.AP(v.tensor, v.offset + P // 2, [v.ap[0], [4 * P, NH // 4], [P + HD, 4], [1, HD]])
                        ins = gp.memset(ones, 1.0)
                ins.then_inc(vpad_ready, 1)

            pad(slice(0, 2), 1)
            for kind, key, banks in jobs:
                if kind == "copies":
                    L, b, j = key
                    t = tok(L, b, j)
                    nh = NH + NKV[L]
                    pool.wait_ge(parts_ready, t + 1)
                    s = qs[:, t % 2, :, :, :]
                    q4 = s[:, 0:NH, :, :].rearrange("p h (a c) d -> p h a c d", c=2)
                    gp.tensor_copy(q4[:, :, 1:3, 0, :], q4[:, :, 0:1, 0, :].broadcast_to((P, NH, 2, HD)))
                    gp.tensor_copy(s[:, 0:NH, 3, :], s[:, 0:NH, 1, :])
                    k4 = s[:, NH:nh, :, :].rearrange("p h (a c) d -> p h a c d", c=2)
                    gp.tensor_copy(k4[:, :, 1:3, 1, :], k4[:, :, 0:1, 0, :].broadcast_to((P, nh - NH, 2, HD)))
                    gp.tensor_copy(s[:, NH:nh, 2, :], s[:, NH:nh, 1, :])
                    gp.tensor_tensor(s[:, 0:NH, 5, :], rot2[:, t % 2, 0:NH, :], s[:, 0:NH, 1, :], ALU.subtract)
                    gp.tensor_tensor(s[:, NH:nh, 4, :], rot2[:, t % 2, NH:nh, :], s[:, NH:nh, 1, :],
                                     ALU.subtract).then_inc(stack_ready, 1)
                elif kind == "rezero":
                    after_pe(pool, "dn0", (1, HC0 - 1))
                    pad(slice(0, 1), 3)
                elif kind == "st" and key[0]:
                    inverse_std(key[0])
                elif kind == "op":
                    inverse_std(step_of(*key[:1], ATT, key[1]) + B)
                elif kind == "rs":
                    inverse_std(step_of(0, FFN, key[0]) + B)
                elif kind == "w0":
                    n, = key
                    i = n % HC0
                    nr = rows0(i)
                    pool.wait_ge(w0hi_ready, n + 1)
                    gp.tensor_tensor(wgs[:, n % 2, 1, :, :, 0:nr], wgu0[:, :, :, i * P:i * P + nr],
                                     wgs[:, n % 2, 0, :, :, 0:nr].bitcast(F32), ALU.subtract)\
                      .then_inc(w0lo_ready, 1)
                elif kind == "s0":
                    n, = key
                    i = n % HC0
                    nr = rows0(i)
                    pool.wait_ge(d0hi_ready, n + 1)
                    gp.tensor_tensor(wd0s[0:nr, n % 2, 1, :], wd0[0:nr, i, :],
                                     wd0s[0:nr, n % 2, 0, :].bitcast(F32), ALU.subtract).then_inc(d0lo_ready, 1)
                elif kind == "add":
                    b, i, k = key
                    m = 2 * chunk(b, i) + k
                    pool.wait_ge(done["lora"], m + 1)
                    after(pool, "wk", (b,))
                    if m >= 2:
                        pool.wait_ge(h_ready, m - 1)
                    gp.tensor_tensor(uw[:, k, :], gu1[:, m % 2, 1, :], wkb[:, k, :], ALU.mult).then_inc(uw_ready, 1)
                elif kind == "bx":
                    m, = key
                    pool.wait_ge(bxhi_ready, m + 1)
                    gp.tensor_tensor(bxs[:, m % 2, 1, :, :, :], feature_weights(m),
                                     bxs[:, m % 2, 0, :, :, :].bitcast(F32), ALU.subtract).then_inc(bxlo_ready, 1)
                elif kind == "xa":
                    b, c = key
                    n = b * RC1 + c
                    pool.wait_ge(xhi_ready, 2 * n + 1)
                    gp.tensor_tensor(xam[:, 1, c, :, 1, :], xt[:, 1, :, :],
                                     xam[:, 0, c, :, 1, :].bitcast(F32), ALU.subtract).then_inc(xlo1_ready, 1)
                elif kind == "hp" and key[2] == 1:
                    b, i, _ = key
                    pool.wait_ge(h_ready, 2 * chunk(b, i) + 2)
                    if i == 0 and b > 0:
                        after_pe(pool, "dn", (1, b - 1, 1))
                    gp.tensor_tensor(hw[:, i, :], hk[:, 0, :], hk[:, 1, :], ALU.add).then_inc(hw_ready, 1)


def constants():
    bf = np.dtype("bfloat16")
    c = {"identf": np.eye(P, dtype=np.float32), "identb": np.eye(P).astype(bf)}
    c["iota"] = np.broadcast_to(np.arange(E, dtype=np.float32), (P, E)).copy()
    pos = np.arange(S, dtype=np.float32)
    one, theta = np.float32(1.0), np.float32(10000.0)
    pairs = np.arange(HD // 2, dtype=np.float32)
    f0 = one / theta ** (np.float32(2.0) * pairs / np.float32(HD))
    f1 = one / theta ** (np.arange(0, HD, 2, dtype=np.float32) / np.float32(HD))
    rope = np.zeros((2, S, 2, HD), np.float32)
    for L, f in enumerate((f0, f1)):
        a = pos[:, None] * f[None, :]
        co, si = (np.cos(a), np.sin(a)) if L == 0 else (np.sin(a), np.cos(a))
        rope[L, :, 0] = np.concatenate([co, co], 1)
        rope[L, :, 1] = np.concatenate([-si, si], 1)
    c["rope"] = rope.reshape(2, TB, P, 2, HD).transpose(2, 0, 1, 3, 4)
    i = np.arange(P)
    tri = np.where(i[None, :] > i[:, None], NEG, 0.0)
    c["maskQ"] = tri.astype(bf)
    c["maskT"] = tri.T.astype(bf)
    m = np.zeros((3, NH, NH, P), np.float32)
    for h in range(NH):
        m[:, h, h] = -1.0
    c["msel"] = m.reshape(3 * NH, NH, P).astype(bf)
    row = np.arange(HC0 * P)
    e = np.minimum(row // I0, E)
    w = (e[None, :] == np.arange(E + 1)[:, None]).astype(np.float32)
    c["wsel0"] = np.tile(w, (3, 1)).reshape(3 * (E + 1), HC0, P).astype(bf)
    w = np.zeros((2 * E + 6, 2 * RC1 + 2, P), np.float32)
    for k in range(2):
        for q in range(RC1):
            for r in range(P):
                w[k * E + (q * P + r) // R1, k * RC1 + q, r] = LORA
        w[2 * E + k::2, 2 * RC1 + k] = 1.0
    c["wsel1"] = w.astype(bf)
    return c


def layouts(a):
    def kmajor(w):
        return w.reshape(w.shape[0] // P, P, *w.shape[1:]).transpose(1, 0, *range(2, w.ndim + 1))

    def halves(w):
        return w.reshape(-1, HD // 2, 2, D).transpose(0, 2, 1, 3).reshape(-1, D)

    o = {}
    o["x"] = a["L0_attn_x"].reshape(B * TB, P, D).transpose(1, 0, 2)
    o["cT"] = np.stack([kmajor(a[f"L{L}_c"].T) for L in range(2)], 1)
    for L in range(2):
        o[f"wmod{L}"] = kmajor(a[f"L{L}_wmod"])
    kv = a["L0_attn_kv_w"]
    half = kv.shape[0] // 2
    o["wqkv0"] = kmajor(np.concatenate([halves(a["L0_attn_q_w"]), halves(kv[:half]), kv[half:]], 0).T)
    o["wo0"] = kmajor(a["L0_attn_c_w"].T)
    o["wqkv1"] = kmajor(np.concatenate([a["L1_attn_Wq"], a["L1_attn_Wk"], a["L1_attn_Wv"]], 0).T)
    o["wo1"] = kmajor(a["L1_attn_Wo"].T)
    o["wr0"] = kmajor(np.concatenate([a["L0_ffn_router_weight"], a["L0_ffn_shared_gate_w"]], 0).T)
    o["wr1"] = kmajor(a["L1_ffn_conf_W"].T)
    o["bw"] = np.broadcast_to(np.stack([a["L1_ffn_conf_b"], a["L1_ffn_expert_wealth"]]), (P, 2, E))
    gu = a["L0_ffn_gate_up_proj"]
    g = np.concatenate([gu[:, :I0].reshape(-1, D), a["L0_ffn_sh_gate_w"]], 0)
    u = np.concatenate([gu[:, I0:].reshape(-1, D), a["L0_ffn_sh_up_w"]], 0)
    o["wgu0"] = kmajor(np.stack([g.T, u.T], 1))
    d = np.concatenate([a["L0_ffn_down_proj"].transpose(0, 2, 1).reshape(-1, D), a["L0_ffn_sh_down_w"].T], 0)
    d = np.concatenate([d, np.zeros((HC0 * P - H0, D), d.dtype)], 0)
    o["wd0"] = kmajor(d)
    o["wa1"] = kmajor(np.stack([a[f"L1_ffn_{n}_A"].transpose(1, 0, 2).reshape(D, -1) for n in ("gate", "up")], 1))
    o["wbase1"] = kmajor(np.stack([a["L1_ffn_base_gate"], a["L1_ffn_base_up"]], 1))
    o["wb1"] = kmajor(np.stack([a[f"L1_ffn_{n}_B"].reshape(-1, I1) for n in ("gate", "up")], 1))
    o["wda1"] = kmajor(a["L1_ffn_down_A"].transpose(1, 0, 2).reshape(I1, -1))
    o["wd1"] = kmajor(a["L1_ffn_base_down"])
    o["wdb1"] = kmajor(a["L1_ffn_down_B"].reshape(-1, D))
    return o


def kernel(**inputs):
    import concourse.bacc as bacc
    from concourse.bass_utils import run_bass_kernel_spmd

    nc = bacc.Bacc("TRN2", target_bir_lowering=False, num_devices=1)
    host = layouts({k: np.asarray(v) for k, v in inputs.items()})
    host.update(constants())
    arrays, dram = {}, {}
    for name, shape, dt in INPUTS:
        arr = np.ascontiguousarray(host[name])
        assert tuple(arr.shape) == tuple(shape), (name, arr.shape, shape)
        arrays["in_" + name] = arr
        dram[name] = nc.dram_tensor("in_" + name, list(shape), dt, kind="ExternalInput").ap()
    out = nc.dram_tensor("out_x", [B, S, D], F32, kind="ExternalOutput").ap()
    build(nc, dram, out)
    r = run_bass_kernel_spmd(nc, [arrays], core_ids=[0])
    return r.results[0]["out_x"]
```
